# Optimizing a Trainium2 kernel written in Bass

```python
import numpy as np
import jax
import jax.numpy as jnp

def _softmax(x, axis=-1):
    return jax.nn.softmax(x, axis=axis)

def _gelu(x):
    return jax.nn.gelu(x, approximate=True)

def _silu(x):
    return jax.nn.silu(x)

def _sigmoid(x):
    return jax.nn.sigmoid(x)

def _layernorm(x, axis=-1, eps=1e-05):
    m = jnp.mean(x, axis=axis, keepdims=True)
    v = jnp.var(x, axis=axis, keepdims=True)
    return (x - m) / jnp.sqrt(v + eps)

def _scatter_add(tgt, idx, src, axis=0):
    return tgt.at[idx].add(src)

def _segment_sum(src, seg, n):
    return jax.ops.segment_sum(src, seg, n)
kernel_name = 'mk_vit_tower_d2_tok_img768_r4_539c55'

def setup_inputs(seed: int=0):
    np.random.seed(seed)
    _w = jnp.asarray

    def _rec_inputs():
        import jax
        import jax.numpy as jnp
        _rk = jax.random.key(seed)
        x = -0.000348323 + 0.999952 * jax.random.normal(jax.random.fold_in(_rk, 1), (16, 3, 96, 96), jnp.float32)
        return x
    x = _rec_inputs()

    def _L0_tok_setup():
        import jax, jax.numpy as jnp
        import numpy as np
        PATCH = 16
        DIM = 192
        LN_EPS = 1e-05

        def _spt_forward(x, ln_gamma, ln_beta, w, b):
            B, C, H, W = x.shape
            p = PATCH
            x_right = jnp.pad(x, ((0, 0), (0, 0), (0, 0), (1, 0)))[:, :, :, :-1]
            x_left = jnp.pad(x, ((0, 0), (0, 0), (0, 0), (0, 1)))[:, :, :, 1:]
            x_down = jnp.pad(x, ((0, 0), (0, 0), (1, 0), (0, 0)))[:, :, :-1, :]
            x_up = jnp.pad(x, ((0, 0), (0, 0), (0, 1), (0, 0)))[:, :, 1:, :]
            xc = jnp.concatenate((x, x_right, x_left, x_down, x_up), axis=1)
            C5 = 5 * C
            h, wgrid = (H // p, W // p)
            tokens = xc.reshape(B, C5, h, p, wgrid, p)
            tokens = tokens.transpose(0, 2, 4, 3, 5, 1)
            tokens = tokens.reshape(B, h * wgrid, p * p * C5)
            mean = jnp.mean(tokens, axis=-1, keepdims=True)
            var = jnp.var(tokens, axis=-1, keepdims=True)
            normed = (tokens - mean) * jax.lax.rsqrt(var + LN_EPS) * ln_gamma + ln_beta
            return jnp.einsum('bnd,de->bne', normed, w) + b
        key = jax.random.key(seed)
        k1, k2 = jax.random.split(key)
        B, C, H, W = (32, 3, 96, 96)
        patch_dim = PATCH * PATCH * 5 * C
        x = jax.random.normal(k1, (B, C, H, W), dtype=jnp.float32)
        ln_gamma = jnp.ones((patch_dim,), dtype=jnp.float32)
        ln_beta = jnp.zeros((patch_dim,), dtype=jnp.float32)
        w = jax.random.normal(k2, (patch_dim, DIM), dtype=jnp.float32) * patch_dim ** (-0.5)
        b = jnp.zeros((DIM,), dtype=jnp.float32)
        return {'x': x, 'ln_gamma': ln_gamma, 'ln_beta': ln_beta, 'w': w, 'b': b}
    _L0_tok_all = _L0_tok_setup()
    _L0_tok_in = {k: v for k, v in _L0_tok_all.items() if k in ('ln_gamma', 'ln_beta', 'w', 'b')}
    del _L0_tok_all

    def _L0_attn_setup():
        import jax, jax.numpy as jnp
        import numpy as np
        EMBED_DIM = 192
        NUM_HEADS = 12
        HEAD_DIM = EMBED_DIM // NUM_HEADS
        MAX_REL = 14
        TABLE_ROWS = 2 * MAX_REL + 2

        def rel_pos_indices(N, max_rel):
            L = N - 1
            s = int(L ** 0.5)
            r = np.arange(L)
            dv = r[None, :] // s - r[:, None] // s
            dh = r[None, :] % s - r[:, None] % s
            fv = np.clip(dv, -max_rel, max_rel) + max_rel + 1
            fh = np.clip(dh, -max_rel, max_rel) + max_rel + 1
            fv = np.pad(fv, ((1, 0), (1, 0)), constant_values=0)
            fh = np.pad(fh, ((1, 0), (1, 0)), constant_values=0)
            return (jnp.asarray(fv, jnp.int32), jnp.asarray(fh, jnp.int32))
        key = jax.random.key(seed)
        ks = jax.random.split(key, 8)
        C = EMBED_DIM
        x = jax.random.normal(ks[0], (64, 197, C), dtype=jnp.float32)
        w_qkv = jax.random.normal(ks[1], (C, 3 * C), dtype=jnp.float32) * 0.02
        tab_vk = jax.random.normal(ks[2], (TABLE_ROWS, HEAD_DIM), dtype=jnp.float32) * 0.02
        tab_hk = jax.random.normal(ks[3], (TABLE_ROWS, HEAD_DIM), dtype=jnp.float32) * 0.02
        tab_vv = jax.random.normal(ks[4], (TABLE_ROWS, HEAD_DIM), dtype=jnp.float32) * 0.02
        tab_hv = jax.random.normal(ks[5], (TABLE_ROWS, HEAD_DIM), dtype=jnp.float32) * 0.02
        w_proj = jax.random.normal(ks[6], (C, C), dtype=jnp.float32) * 0.02
        b_proj = jnp.zeros((C,), dtype=jnp.float32)
        return {'x': x, 'w_qkv': w_qkv, 'tab_vk': tab_vk, 'tab_hk': tab_hk, 'tab_vv': tab_vv, 'tab_hv': tab_hv, 'w_proj': w_proj, 'b_proj': b_proj}
    _L0_attn_all = _L0_attn_setup()
    _L0_attn_in = {k: v for k, v in _L0_attn_all.items() if k in ('w_qkv', 'tab_vk', 'tab_hk', 'tab_vv', 'tab_hv', 'w_proj', 'b_proj')}
    del _L0_attn_all

    def _L0_ffn_setup():
        import jax, jax.numpy as jnp
        import numpy as np
        B, T, D, E, K = (4, 512, 192, 8, 2)
        H = 4 * D
        key = jax.random.key(seed)
        k0, k1, k2, k3, k4 = jax.random.split(key, 5)
        s = 0.02
        return {'x': jax.random.normal(k0, (B, T, D), jnp.float32), 'router_w': jax.random.uniform(k1, (E, D), jnp.float32, -s * 0.1, s * 0.1), 'Wg': jax.random.uniform(k2, (E, H, D), jnp.float32, -s * 0.4, s * 0.4), 'Wu': jax.random.uniform(k3, (E, H, D), jnp.float32, -s * 0.4, s * 0.4), 'Wd': jax.random.normal(k4, (E, D, H), jnp.float32) * 0.01}
    _L0_ffn_all = _L0_ffn_setup()
    _L0_ffn_in = {k: v for k, v in _L0_ffn_all.items() if k in ('router_w', 'Wg', 'Wu', 'Wd')}
    del _L0_ffn_all

    def _L1_attn_setup():
        import jax, jax.numpy as jnp
        import numpy as np
        HEADS = 12
        EPS = 1e-06

        def _rfm_softmax(seq, omega, query):
            d = seq.shape[-1]
            F = omega.shape[0]
            s = seq * float(d) ** (-0.25)
            s = jnp.einsum('bhld,fd->bhlf', s, omega)
            diag = jnp.sum(s, axis=-1, keepdims=True) / 2.0
            if query:
                m = jnp.max(s, axis=-1, keepdims=True)
            else:
                m = jnp.max(s, axis=(1, 3), keepdims=True)
            return float(F) ** (-0.5) * (jnp.exp(s - diag - m) + EPS)
        key = jax.random.key(seed)
        ks = jax.random.split(key, 5)
        B, L, E, F = (8, 128, 192, 64)
        Dh = E // HEADS
        x = jax.random.normal(ks[0], (B, L, E), dtype=jnp.float32)
        w_inp = jax.random.normal(ks[1], (1, E, 3 * E), dtype=jnp.float32) * 0.02
        b_inp = jnp.zeros((3 * E,), jnp.float32)
        w_out = jax.random.normal(ks[2], (1, E, E), dtype=jnp.float32) * 0.02
        b_out = jnp.zeros((E,), jnp.float32)
        g = jax.random.normal(ks[3], (Dh, F), dtype=jnp.float32)
        q, _ = jnp.linalg.qr(g)
        omega = q.T[:F].astype(jnp.float32)
        return {'x': x, 'w_inp': w_inp, 'b_inp': b_inp, 'w_out': w_out, 'b_out': b_out, 'omega': omega}
    _L1_attn_all = _L1_attn_setup()
    _L1_attn_in = {k: v for k, v in _L1_attn_all.items() if k in ('w_inp', 'b_inp', 'w_out', 'b_out', 'omega')}
    del _L1_attn_all

    def _L1_ffn_setup():
        import jax, jax.numpy as jnp
        import numpy as np
        HID = 192
        NQ = 12
        NKV = 3
        HD = 64
        REP = NQ // NKV
        E = 16
        TOPK = 2
        FF = 384
        EPS = 1e-06
        THETA = 10000.0

        def rms_norm(x, w):
            return x / jnp.sqrt(jnp.mean(x * x, axis=-1, keepdims=True) + EPS) * w

        def rope_tables(seq_len):
            inv = 1.0 / THETA ** (jnp.arange(0, HD, 2, dtype=jnp.float32) / HD)
            f = jnp.arange(seq_len, dtype=jnp.float32)[:, None] * inv[None, :]
            return (jnp.cos(f), jnp.sin(f))

        def apply_rope(t, cos, sin):
            B, S, H, _ = t.shape
            tr = t.reshape(B, S, H, HD // 2, 2)
            c = cos[None, :, None, :]
            s = sin[None, :, None, :]
            r0 = tr[..., 0] * c - tr[..., 1] * s
            r1 = tr[..., 0] * s + tr[..., 1] * c
            return jnp.stack([r0, r1], axis=-1).reshape(B, S, H, HD)

        def attention(x, w_qkv, w_out):
            B, S, _ = x.shape
            qkv = x @ w_qkv
            q, k, v = jnp.split(qkv, [NQ * HD, (NQ + NKV) * HD], axis=-1)
            q = q.reshape(B, S, NQ, HD)
            k = k.reshape(B, S, NKV, HD)
            v = v.reshape(B, S, NKV, HD)
            cos, sin = rope_tables(S)
            q = apply_rope(q, cos, sin)
            k = apply_rope(k, cos, sin)
            k = jnp.repeat(k, REP, axis=2)
            v = jnp.repeat(v, REP, axis=2)
            q = q.transpose(0, 2, 1, 3)
            k = k.transpose(0, 2, 1, 3)
            v = v.transpose(0, 2, 1, 3)
            scores = jnp.einsum('bhqd,bhkd->bhqk', q, k) / jnp.sqrt(jnp.float32(HD))
            causal = jnp.tril(jnp.ones((S, S), dtype=bool))
            scores = jnp.where(causal[None, None], scores, jnp.finfo(scores.dtype).min)
            attn = jax.nn.softmax(scores, axis=-1)
            out = jnp.einsum('bhqk,bhkd->bhqd', attn, v)
            out = out.transpose(0, 2, 1, 3).reshape(B, S, NQ * HD)
            return out @ w_out

        def moe_ffn(x2d, w_router, w_gate_up, w_down):
            logits = x2d @ w_router
            probs = jax.nn.softmax(logits, axis=-1)
            vals, idx = jax.lax.top_k(probs, TOPK)
            vals = vals / jnp.sum(vals, axis=-1, keepdims=True)
            combine = jnp.sum(jax.nn.one_hot(idx, E, dtype=x2d.dtype) * vals[..., None], axis=1)
            out = jnp.zeros_like(x2d)
            for e in range(E):
                gu = x2d @ w_gate_up[e]
                gate, up = jnp.split(gu, 2, axis=-1)
                h = jax.nn.silu(gate) * up
                out = out + combine[:, e:e + 1] * (h @ w_down[e])
            return out
        key = jax.random.key(seed)
        ks = jax.random.split(key, 6)
        B, S = (1, 512)
        return {'x': jax.random.normal(ks[0], (B, S, HID), dtype=jnp.float32), 'norm1_w': jnp.ones((HID,), dtype=jnp.float32), 'w_qkv': jax.random.normal(ks[1], (HID, (NQ + 2 * NKV) * HD), dtype=jnp.float32) * 0.02, 'w_out': jax.random.normal(ks[2], (NQ * HD, HID), dtype=jnp.float32) * 0.02, 'norm2_w': jnp.ones((HID,), dtype=jnp.float32), 'w_router': jax.random.normal(ks[3], (HID, E), dtype=jnp.float32) * 0.02, 'w_gate_up': jax.random.normal(ks[4], (E, HID, 2 * FF), dtype=jnp.float32) * 0.02, 'w_down': jax.random.normal(ks[5], (E, FF, HID), dtype=jnp.float32) * 0.02}
    _L1_ffn_all = _L1_ffn_setup()
    _L1_ffn_in = {k: v for k, v in _L1_ffn_all.items() if k in ('norm1_w', 'w_qkv', 'w_out', 'norm2_w', 'w_router', 'w_gate_up', 'w_down')}
    del _L1_ffn_all
    return {'x': x, 'L0_tok_ln_gamma': _L0_tok_in['ln_gamma'], 'L0_tok_ln_beta': _L0_tok_in['ln_beta'], 'L0_tok_w': _L0_tok_in['w'], 'L0_tok_b': _L0_tok_in['b'], 'L0_attn_w_qkv': _L0_attn_in['w_qkv'], 'L0_attn_tab_vk': _L0_attn_in['tab_vk'], 'L0_attn_tab_hk': _L0_attn_in['tab_hk'], 'L0_attn_tab_vv': _L0_attn_in['tab_vv'], 'L0_attn_tab_hv': _L0_attn_in['tab_hv'], 'L0_attn_w_proj': _L0_attn_in['w_proj'], 'L0_attn_b_proj': _L0_attn_in['b_proj'], 'L0_ffn_router_w': _L0_ffn_in['router_w'], 'L0_ffn_Wg': _L0_ffn_in['Wg'], 'L0_ffn_Wu': _L0_ffn_in['Wu'], 'L0_ffn_Wd': _L0_ffn_in['Wd'], 'L1_attn_w_inp': _L1_attn_in['w_inp'], 'L1_attn_b_inp': _L1_attn_in['b_inp'], 'L1_attn_w_out': _L1_attn_in['w_out'], 'L1_attn_b_out': _L1_attn_in['b_out'], 'L1_attn_omega': _L1_attn_in['omega'], 'L1_ffn_norm1_w': _L1_ffn_in['norm1_w'], 'L1_ffn_w_qkv': _L1_ffn_in['w_qkv'], 'L1_ffn_w_out': _L1_ffn_in['w_out'], 'L1_ffn_norm2_w': _L1_ffn_in['norm2_w'], 'L1_ffn_w_router': _L1_ffn_in['w_router'], 'L1_ffn_w_gate_up': _L1_ffn_in['w_gate_up'], 'L1_ffn_w_down': _L1_ffn_in['w_down']}

def reference(x, L0_tok_ln_gamma, L0_tok_ln_beta, L0_tok_w, L0_tok_b, L0_attn_w_qkv, L0_attn_tab_vk, L0_attn_tab_hk, L0_attn_tab_vv, L0_attn_tab_hv, L0_attn_w_proj, L0_attn_b_proj, L0_ffn_router_w, L0_ffn_Wg, L0_ffn_Wu, L0_ffn_Wd, L1_attn_w_inp, L1_attn_b_inp, L1_attn_w_out, L1_attn_b_out, L1_attn_omega, L1_ffn_norm1_w, L1_ffn_w_qkv, L1_ffn_w_out, L1_ffn_norm2_w, L1_ffn_w_router, L1_ffn_w_gate_up, L1_ffn_w_down):
    import jax
    import jax.numpy as jnp

    def _L0_tok_ref(x, ln_gamma, ln_beta, w, b):
        import jax, jax.numpy as jnp
        import numpy as np
        PATCH = 16
        DIM = 192
        LN_EPS = 1e-05

        def _spt_forward(x, ln_gamma, ln_beta, w, b):
            B, C, H, W = x.shape
            p = PATCH
            x_right = jnp.pad(x, ((0, 0), (0, 0), (0, 0), (1, 0)))[:, :, :, :-1]
            x_left = jnp.pad(x, ((0, 0), (0, 0), (0, 0), (0, 1)))[:, :, :, 1:]
            x_down = jnp.pad(x, ((0, 0), (0, 0), (1, 0), (0, 0)))[:, :, :-1, :]
            x_up = jnp.pad(x, ((0, 0), (0, 0), (0, 1), (0, 0)))[:, :, 1:, :]
            xc = jnp.concatenate((x, x_right, x_left, x_down, x_up), axis=1)
            C5 = 5 * C
            h, wgrid = (H // p, W // p)
            tokens = xc.reshape(B, C5, h, p, wgrid, p)
            tokens = tokens.transpose(0, 2, 4, 3, 5, 1)
            tokens = tokens.reshape(B, h * wgrid, p * p * C5)
            mean = jnp.mean(tokens, axis=-1, keepdims=True)
            var = jnp.var(tokens, axis=-1, keepdims=True)
            normed = (tokens - mean) * jax.lax.rsqrt(var + LN_EPS) * ln_gamma + ln_beta
            return jnp.einsum('bnd,de->bne', normed, w) + b
        return _spt_forward(x, ln_gamma, ln_beta, w, b)

    def _L0_attn_ref(x, w_qkv, tab_vk, tab_hk, tab_vv, tab_hv, w_proj, b_proj):
        import jax, jax.numpy as jnp
        import numpy as np
        EMBED_DIM = 192
        NUM_HEADS = 12
        HEAD_DIM = EMBED_DIM // NUM_HEADS
        MAX_REL = 14
        TABLE_ROWS = 2 * MAX_REL + 2

        def rel_pos_indices(N, max_rel):
            L = N - 1
            s = int(L ** 0.5)
            r = np.arange(L)
            dv = r[None, :] // s - r[:, None] // s
            dh = r[None, :] % s - r[:, None] % s
            fv = np.clip(dv, -max_rel, max_rel) + max_rel + 1
            fh = np.clip(dh, -max_rel, max_rel) + max_rel + 1
            fv = np.pad(fv, ((1, 0), (1, 0)), constant_values=0)
            fh = np.pad(fh, ((1, 0), (1, 0)), constant_values=0)
            return (jnp.asarray(fv, jnp.int32), jnp.asarray(fh, jnp.int32))
        B, N, C = x.shape
        H, hd = (NUM_HEADS, C // NUM_HEADS)
        scale = hd ** (-0.5)
        idx_v, idx_h = rel_pos_indices(N, MAX_REL)
        emb_k = tab_vk[idx_v] + tab_hk[idx_h]
        emb_v = tab_vv[idx_v] + tab_hv[idx_h]
        qkv = (x @ w_qkv).reshape(B, N, 3, H, hd)
        q = qkv[:, :, 0].transpose(0, 2, 1, 3)
        k = qkv[:, :, 1].transpose(0, 2, 1, 3)
        v = qkv[:, :, 2].transpose(0, 2, 1, 3)
        attn = jnp.einsum('bhqd,bhkd->bhqk', q, k) * scale
        attn = attn + jnp.einsum('bhqd,qkd->bhqk', q, emb_k) * scale
        attn = jax.nn.softmax(attn, axis=-1)
        out = jnp.einsum('bhqk,bhkd->bhqd', attn, v)
        out = out + jnp.einsum('bhqk,qkd->bhqd', attn, emb_v)
        out = out.transpose(0, 2, 1, 3).reshape(B, N, C)
        return out @ w_proj + b_proj

    def _L0_ffn_ref(x, router_w, Wg, Wu, Wd):
        import jax, jax.numpy as jnp
        import numpy as np
        B, T, D, E, K = (4, 512, 192, 8, 2)
        H = 4 * D
        Bv, Tv, Dv = x.shape
        N = Bv * Tv
        xf = x.reshape(N, Dv)
        logits = (xf @ router_w.T).astype(jnp.float32)
        top_logits, top_idx = jax.lax.top_k(logits, K)
        top_w = jax.nn.softmax(top_logits, axis=-1).astype(x.dtype)
        out = jnp.zeros_like(xf)
        for e in range(E):
            w_e = jnp.sum(top_w * (top_idx == e), axis=-1)
            h = jax.nn.silu(xf @ Wg[e].T) * (xf @ Wu[e].T)
            out = out + h @ Wd[e].T * w_e[:, None]
        return out.reshape(Bv, Tv, Dv)

    def _L1_attn_ref(x, w_inp, b_inp, w_out, b_out, omega):
        import jax, jax.numpy as jnp
        import numpy as np
        HEADS = 12
        EPS = 1e-06

        def _rfm_softmax(seq, omega, query):
            d = seq.shape[-1]
            F = omega.shape[0]
            s = seq * float(d) ** (-0.25)
            s = jnp.einsum('bhld,fd->bhlf', s, omega)
            diag = jnp.sum(s, axis=-1, keepdims=True) / 2.0
            if query:
                m = jnp.max(s, axis=-1, keepdims=True)
            else:
                m = jnp.max(s, axis=(1, 3), keepdims=True)
            return float(F) ** (-0.5) * (jnp.exp(s - diag - m) + EPS)
        B, L, E = x.shape
        H = HEADS
        Dh = E // H
        c = jnp.einsum('ble,eo->blo', x, w_inp[0]) + b_inp
        q, k, v = jnp.split(c, 3, axis=2)
        split = lambda t: t.reshape(B, L, H, Dh).transpose(0, 2, 1, 3)
        q, k, v = (split(q), split(k), split(v))
        qf = _rfm_softmax(q, omega, query=True)
        kf = _rfm_softmax(k, omega, query=False)
        qf = qf.transpose(2, 0, 1, 3)
        kf = kf.transpose(2, 0, 1, 3)
        vl = v.transpose(2, 0, 1, 3)
        rhs = jnp.cumsum(kf[..., None, :] * vl[..., :, None], axis=0)
        a = jnp.einsum('lbhdf,lbhf->lbhd', rhs, qf)
        denom = jnp.einsum('lbhf,lbhf->lbh', qf, jnp.cumsum(kf, axis=0))[..., None]
        a = a / (denom + EPS)
        a = a.transpose(1, 2, 0, 3)
        a = a.transpose(0, 2, 1, 3).reshape(B, L, E)
        out = jnp.einsum('ble,eo->blo', a, w_out[0]) + b_out
        return out

    def _L1_ffn_ref(x, norm1_w, w_qkv, w_out, norm2_w, w_router, w_gate_up, w_down):
        import jax, jax.numpy as jnp
        import numpy as np
        HID = 192
        NQ = 12
        NKV = 3
        HD = 64
        REP = NQ // NKV
        E = 16
        TOPK = 2
        FF = 384
        EPS = 1e-06
        THETA = 10000.0

        def rms_norm(x, w):
            return x / jnp.sqrt(jnp.mean(x * x, axis=-1, keepdims=True) + EPS) * w

        def rope_tables(seq_len):
            inv = 1.0 / THETA ** (jnp.arange(0, HD, 2, dtype=jnp.float32) / HD)
            f = jnp.arange(seq_len, dtype=jnp.float32)[:, None] * inv[None, :]
            return (jnp.cos(f), jnp.sin(f))

        def apply_rope(t, cos, sin):
            B, S, H, _ = t.shape
            tr = t.reshape(B, S, H, HD // 2, 2)
            c = cos[None, :, None, :]
            s = sin[None, :, None, :]
            r0 = tr[..., 0] * c - tr[..., 1] * s
            r1 = tr[..., 0] * s + tr[..., 1] * c
            return jnp.stack([r0, r1], axis=-1).reshape(B, S, H, HD)

        def attention(x, w_qkv, w_out):
            B, S, _ = x.shape
            qkv = x @ w_qkv
            q, k, v = jnp.split(qkv, [NQ * HD, (NQ + NKV) * HD], axis=-1)
            q = q.reshape(B, S, NQ, HD)
            k = k.reshape(B, S, NKV, HD)
            v = v.reshape(B, S, NKV, HD)
            cos, sin = rope_tables(S)
            q = apply_rope(q, cos, sin)
            k = apply_rope(k, cos, sin)
            k = jnp.repeat(k, REP, axis=2)
            v = jnp.repeat(v, REP, axis=2)
            q = q.transpose(0, 2, 1, 3)
            k = k.transpose(0, 2, 1, 3)
            v = v.transpose(0, 2, 1, 3)
            scores = jnp.einsum('bhqd,bhkd->bhqk', q, k) / jnp.sqrt(jnp.float32(HD))
            causal = jnp.tril(jnp.ones((S, S), dtype=bool))
            scores = jnp.where(causal[None, None], scores, jnp.finfo(scores.dtype).min)
            attn = jax.nn.softmax(scores, axis=-1)
            out = jnp.einsum('bhqk,bhkd->bhqd', attn, v)
            out = out.transpose(0, 2, 1, 3).reshape(B, S, NQ * HD)
            return out @ w_out

        def moe_ffn(x2d, w_router, w_gate_up, w_down):
            logits = x2d @ w_router
            probs = jax.nn.softmax(logits, axis=-1)
            vals, idx = jax.lax.top_k(probs, TOPK)
            vals = vals / jnp.sum(vals, axis=-1, keepdims=True)
            combine = jnp.sum(jax.nn.one_hot(idx, E, dtype=x2d.dtype) * vals[..., None], axis=1)
            out = jnp.zeros_like(x2d)
            for e in range(E):
                gu = x2d @ w_gate_up[e]
                gate, up = jnp.split(gu, 2, axis=-1)
                h = jax.nn.silu(gate) * up
                out = out + combine[:, e:e + 1] * (h @ w_down[e])
            return out
        B, S, _ = x.shape
        h = x + attention(rms_norm(x, norm1_w), w_qkv, w_out)
        moe_in = rms_norm(h, norm2_w).reshape(B * S, HID)
        out = h + moe_ffn(moe_in, w_router, w_gate_up, w_down).reshape(B, S, HID)
        return out
    h = _L0_tok_ref(x, L0_tok_ln_gamma, L0_tok_ln_beta, L0_tok_w, L0_tok_b)
    h = h + _L0_attn_ref(_layernorm(h, axis=-1), L0_attn_w_qkv, L0_attn_tab_vk, L0_attn_tab_hk, L0_attn_tab_vv, L0_attn_tab_hv, L0_attn_w_proj, L0_attn_b_proj)
    h = h + _L0_ffn_ref(_layernorm(h, axis=-1), L0_ffn_router_w, L0_ffn_Wg, L0_ffn_Wu, L0_ffn_Wd)
    h = h + _L1_attn_ref(_layernorm(h, axis=-1), L1_attn_w_inp, L1_attn_b_inp, L1_attn_w_out, L1_attn_b_out, L1_attn_omega)
    h = h + _L1_ffn_ref(_layernorm(h, axis=-1), L1_ffn_norm1_w, L1_ffn_w_qkv, L1_ffn_w_out, L1_ffn_norm2_w, L1_ffn_w_router, L1_ffn_w_gate_up, L1_ffn_w_down)
    return h

_drawn_inputs = setup_inputs


def setup_inputs(seed=0):
    import zlib

    import numpy as np

    out = dict(_drawn_inputs(seed))
    spreads = {'L0_tok_ln_gamma': (1.0, 0.2),
     'L0_tok_ln_beta': (0.0, 0.1),
     'L0_tok_b': (0.0, 0.1),
     'L0_attn_b_proj': (0.0, 0.1),
     'L1_attn_b_inp': (0.0, 0.313),
     'L1_attn_b_out': (0.0, 0.1),
     'L1_ffn_norm1_w': (1.0, 0.6),
     'L1_ffn_norm2_w': (1.0, 0.6)}
    factors = {'L0_attn_w_qkv': 3.719,
     'L0_attn_tab_vk': 8.0,
     'L0_attn_tab_hk': 8.0,
     'L0_attn_tab_vv': 8.0,
     'L0_attn_tab_hv': 8.0,
     'L0_attn_w_proj': 3.634,
     'L0_ffn_router_w': 8.0,
     'L0_ffn_Wg': 8.0,
     'L0_ffn_Wu': 8.0,
     'L0_ffn_Wd': 8.0,
     'L1_attn_omega': 8.0,
     'L1_ffn_w_router': 8.0,
     'L1_ffn_w_gate_up': 8.0,
     'L1_ffn_w_down': 8.0}
    for name, (base, spread) in spreads.items():
        noise = np.random.default_rng([zlib.crc32(name.encode()), seed]).standard_normal(out[name].shape)
        drawn = base * np.exp(spread * noise) if base else spread * noise
        out[name] = jnp.asarray(drawn.astype(out[name].dtype))
    for name, factor in factors.items():
        out[name] = (out[name] * factor).astype(out[name].dtype)
    return out
```

```python
import concourse.bass as bass
from concourse import mybir
from contextlib import ExitStack

B, CH, IMG, PATCH, DIM = 16, 3, 96, 16, 192
GRID = IMG // PATCH
N = GRID * GRID
TOK = B * N
NG = 8
GT = TOK // NG
HB = DIM // 2
NH, HD = 12, 16
NJ = 3
FP, FC = 120, 8
SH = 5
E0, F0 = 8, 768
E1, F1 = 16, 384
QH, KVH, QD = 12, 3, 64
NEG = -1e30
BS = 96
NTHR = (TOK - 1) // BS
MAXB = [(2 * TOK + (BS - 1) * e + e - 2) // BS for e in (E0, E1)]
XT_OF = {1: 0, 2: 1, 3: 2, 5: 3, 6: 4}
RING = 2
EPS_LN, EPS_RMS = 1e-5, 1e-6


class Chain:

    def __init__(self, eng, sem, base=0):
        self.eng, self.sem, self.n, self.base = eng, sem, 0, base

    def __call__(self, ins):
        self.n += 1
        ins.then_inc(self.sem, 1)
        self.eng.wait_ge(self.sem, self.base + self.n)


def tower(nc, ins, out):
    fp32, bf16, i32, u32 = mybir.dt.float32, mybir.dt.bfloat16, mybir.dt.int32, mybir.dt.uint32
    ALU, ACT = mybir.AluOpType, mybir.ActivationFunctionType
    AX = mybir.AxisListType

    ctx = ExitStack()
    with ctx:
        def sb(name, shape, dt=fp32):
            return ctx.enter_context(nc.sbuf_tensor(name, shape, dt))

        sems = {}

        def sem(name):
            if name not in sems:
                sems[name] = ctx.enter_context(nc.semaphore(name))
            return sems[name]

        PS = ctx.enter_context(nc.psum_tensor("PS", [128, 8, 512], fp32))

        ident = sb("ident", [128, 128])
        identb = sb("identb", [128, 128], bf16)
        cst = sb("cst", [128, 768])
        blk4 = cst[:, 0:4]
        blk6 = cst[0:HB, 4:10]
        cnt = cst[0:FP, 16:24]
        krows = cst[:, 32:68]
        vrows = cst[0:GT, 68:84]
        causal01 = cst[0:GT, 96:168]
        rcos = cst[:, 168:240]
        rsin = cst[:, 240:312]
        iota8 = cst[0:GT, 312:320]
        iota16 = cst[0:GT, 320:336]
        ones = cst[:, 336:464]
        eps_ln = cst[:, 464:465]
        eps_rms = cst[:, 465:466]
        w1n = cst[0:HB, 466:468]
        w2n = cst[0:HB, 468:470]
        binp = cst[0:HB, 470:474]
        thr = cst[0:GT, 474:474 + NTHR]
        before = cst[0:GT, 480:480 + (E1 + 1) * E1].rearrange("p (a b) -> p a b", b=E1)
        maskb = sb("maskb", [GT, 3, 4, GT], bf16)
        headsel = sb("headsel", [128, NH, GT], bf16)
        h = sb("h", [GT, NG, DIM])
        y = sb("y", [GT, NG, DIM])
        xnT = sb("xnT", [HB, 2, TOK])
        st6 = sb("st6", [GT, NG, 6])
        mv = sb("mv", [GT, NG, 2])
        rstd = sb("rstd", [GT, NG])
        nmr = sb("nmr", [GT, NG])
        tmpg = sb("tmpg", [GT, NG])
        bias = sb("bias", [GT, 3, DIM])
        wC1 = sb("wC1", [HB, 2, 4 * HB])
        wF1 = sb("wF1", [HB, HB])
        wV1 = sb("wV1", [HB, 2, DIM])
        wO1 = sb("wO1", [HB, 2, DIM])
        wQ2 = sb("wQ2", [HB, 2, 4 * NJ * 128])
        wV2 = sb("wV2", [HB, 2, KVH * QD])
        wO2 = sb("wO2", [128, 6, DIM])
        rw0 = sb("rw0", [HB, 2, E0])
        rw1 = sb("rw1", [HB, 2, E1])
        tri = sb("tri", [GT, GT], bf16)
        oneb = sb("oneb", [GT, GT], bf16)
        zero = sb("zero", [128, 1152])
        wgu0 = sb("wgu0", [HB, RING, 2, 2 * F0])
        wd0 = sb("wd0", [128, RING, 6, DIM])
        xs = [nc.dram_tensor(f"xs{L}", ((MAXB[L] + 1) * BS, DIM), fp32, kind="Internal").ap() for L in range(2)]

        block = ctx.enter_context(nc.Block())

        stage_ctx = ExitStack()
        ctx.enter_context(stage_ctx)

        def stage_sb(stack, name, shape, dt=fp32):
            return stack.enter_context(nc.sbuf_tensor(name, shape, dt))

        wA = sb("wA", [HB, 2, NJ * 2 * 128])
        wV0 = sb("wV0", [HB, 2, DIM])
        wP0 = sb("wP0", [64, NJ, DIM])
        t_stack = ExitStack()
        xw = stage_sb(t_stack, "xw", [FP, FC, TOK])
        xsq = stage_sb(t_stack, "xsq", [FP, FC, TOK])
        w5 = stage_sb(t_stack, "w5", [FP, FC, SH, DIM])
        gb5 = stage_sb(t_stack, "gb5", [FP, 2, FC * SH])
        wc = stage_sb(t_stack, "wc", [FP, FC, DIM + 1])
        brow = stage_sb(t_stack, "brow", [1, 2, DIM])
        gsum = stage_sb(t_stack, "gsum", [GT, 2, DIM])
        t_stack.close()
        a_stack = ExitStack()
        posk = stage_sb(a_stack, "posk", [128, N, 128])
        posv = stage_sb(a_stack, "posv", [128, N, 64])
        qT = stage_sb(a_stack, "qT", [128, NJ, TOK])
        qa = stage_sb(a_stack, "qa", [128, NJ, TOK])
        ka = stage_sb(a_stack, "ka", [128, NJ, TOK])
        va = stage_sb(a_stack, "va", [GT, NG, NH, 32])
        oaT = stage_sb(a_stack, "oaT", [128, NJ, TOK])
        of = stage_sb(a_stack, "of", [64, NJ, TOK])
        a_q = stage_sb(a_stack, "a_q", [128, NJ, GT])
        a_kz = stage_sb(a_stack, "a_kz", [128, NJ, 4, GT])
        a_m = stage_sb(a_stack, "a_m", [GT, 128], bf16)
        a_mT = stage_sb(a_stack, "a_mT", [128, GT], bf16)
        a_p = stage_sb(a_stack, "a_p", [GT, NH, GT])
        a_rec = stage_sb(a_stack, "a_rec", [GT, NH])
        a_o = stage_sb(a_stack, "a_o", [GT, NH, 32])
        a_stack.close()
        l1_stack = ExitStack()
        wgu1 = stage_sb(l1_stack, "wgu1", [HB, RING, 2, 2 * F1])
        wd1 = stage_sb(l1_stack, "wd1", [128, RING, 3, DIM])
        rn = stage_sb(l1_stack, "rn", [GT, NG, DIM])
        r_stack = ExitStack()
        cT = stage_sb(r_stack, "cT", [HB, 4, TOK])
        sf = stage_sb(r_stack, "sf", [GT, NG, 2 * NH, HD])
        ssum = stage_sb(r_stack, "ssum", [GT, NG, 2 * NH])
        smax = stage_sb(r_stack, "smax", [GT, NG, 2 * NH])
        kmax = stage_sb(r_stack, "kmax", [GT, NG])
        fT = stage_sb(r_stack, "fT", [HB, 4, TOK])
        vr = stage_sb(r_stack, "vr", [GT, NG, NH, HD + 1])
        r_qz = stage_sb(r_stack, "r_qz", [HB, 2, 6, GT])
        r_k = stage_sb(r_stack, "r_k", [HB, 2, GT])
        r_p = stage_sb(r_stack, "r_p", [GT, NH, GT])
        r_den = stage_sb(r_stack, "r_den", [GT, NH])
        r_a = stage_sb(r_stack, "r_a", [GT, NH, HD])
        r_aT = stage_sb(r_stack, "r_aT", [HB, 2, GT])
        r_stack.close()
        b_stack = ExitStack()
        rq = stage_sb(b_stack, "rq", [128, 2, NJ, TOK])
        rk = stage_sb(b_stack, "rk", [128, 2, NJ, TOK])
        vb = stage_sb(b_stack, "vb", [GT, NG, KVH, QD + 1])
        rt = stage_sb(b_stack, "rt", [128, 2, 4, 288])
        b_q = stage_sb(b_stack, "b_q", [128, 2, NJ, GT])
        b_kz = stage_sb(b_stack, "b_kz", [128, 2, NJ, 4, GT])
        b_m = stage_sb(b_stack, "b_m", [GT, 128], bf16)
        b_mT = stage_sb(b_stack, "b_mT", [128, GT], bf16)
        b_p = stage_sb(b_stack, "b_p", [GT, QH, GT])
        b_rec = stage_sb(b_stack, "b_rec", [GT, QH])
        b_o = stage_sb(b_stack, "b_o", [GT, QH, QD])
        b_oT = stage_sb(b_stack, "b_oT", [128, 6, GT])
        b_stack.close()
        m_stack = ExitStack()
        lg = stage_sb(m_stack, "lg", [GT, NG, E1])
        top8 = stage_sb(m_stack, "top8", [GT, NG, 8])
        idx8 = stage_sb(m_stack, "idx8", [GT, NG, 8], u32)
        idxf = stage_sb(m_stack, "idxf", [GT, NG, 2])
        sel = stage_sb(m_stack, "sel", [GT, 2, NG, E1])
        selb = stage_sb(m_stack, "selb", [GT, NG, E1], bf16)
        share = stage_sb(m_stack, "share", [GT, 2, NG])
        tot = stage_sb(m_stack, "tot", [GT, E1])
        over = stage_sb(m_stack, "over", [GT, E1, NTHR])
        nblk = stage_sb(m_stack, "nblk", [GT, E1])
        prod = stage_sb(m_stack, "prod", [GT, E1 + 1, E1])
        first = stage_sb(m_stack, "first", [GT, E1 + 1])
        firsti = stage_sb(m_stack, "firsti", [GT, E1 + 1], i32)
        slote = stage_sb(m_stack, "slote", [GT, NG, E1])
        slotf = stage_sb(m_stack, "slotf", [GT, 2, NG])
        slot = stage_sb(m_stack, "slot", [GT, 2, NG], u32)
        yg = stage_sb(m_stack, "yg", [GT, 2, NG, DIM])
        bx = stage_sb(m_stack, "bx", [BS, DIM])
        bxT = stage_sb(m_stack, "bxT", [HB, 2, BS])
        sg = stage_sb(m_stack, "sg", [128, 2, 3 * BS])
        hT = stage_sb(m_stack, "hT", [128, 6, BS])
        yo = stage_sb(m_stack, "yo", [BS, DIM])
        m_stack.close()
        l1_stack.close()
        WGU, WD = (wgu0, wgu1), (wd0, wd1)
        EX, HC = (E0, E1), (F0 // 128, F1 // 128)
        RW = (rw0, rw1)

        @block.sync
        def _(sp):
            sp.dma_start(cst[:, :], ins["cst"]).then_inc(sem("cst_in"), 16)
            for c in range(FC):
                sp.dma_start(w5[:, c, :, :], ins["w5"][:, c]).then_inc(sem(f"tok_in{c}"), 16)
                sp.dma_start(xw[:, c, :], ins["xw"][:, c]).then_inc(sem(f"tok_in{c}"), 16)
            sp.wait_ge(sem("t_h"), NG)
            sp.wait_ge(sem("t_acc"), 1)
            sp.dma_start(posk[:, :, :], ins["posk"]).then_inc(sem("posk_in"), 16)
            sp.dma_start(posv[:, :, :], ins["posv"]).then_inc(sem("posv_in"), 16)
            def experts_io(L):
                p = f"m{L}_"
                sp.wait_ge(sem(p + "first"), 1)
                blocks = sp.value_load(firsti[0:1, EX[L]:EX[L] + 1], min_val=1, max_val=MAXB[L])
                sp.sem_inc(sem(p + "y_out"), 16)
                sp.wait_ge(sem(p + "sent"), 16 * 2 * NG)
                sp.dma_start(bx[:, :], xs[L][0:BS, :]).then_inc(sem(p + "x_in"), 16)
                with sp.Fori(0, blocks) as b:
                    sp.wait_ge(sem(p + "xT_ps"), b + 1)
                    sp.dma_start(bx[:, :], xs[L][bass.ds(b * BS + BS, BS), :]).then_inc(sem(p + "x_in"), 16)
                    sp.wait_ge(sem(p + "y"), b + 1)
                    sp.dma_start(xs[L][bass.ds(b * BS, BS), :], yo[:, :]).then_inc(sem(p + "y_out"), 16)
                sp.wait_ge(sem(p + "y_out"), blocks * 16 + 16)
                sp.sem_inc(sem(p + "all_out"), 1)

            experts_io(0)
            experts_io(1)
            sp.wait_ge(sem("h_last"), 1)
            sp.dma_start(out, h[:, :, :]).then_inc(sem("out_done"), 16)
            sp.wait_ge(sem("out_done"), 16)

        @block.gpsimd
        def _(pool):
            pool.dma_start(identb[:, :], ins["identb"]).then_inc(sem("bf_in"), 16)
            pool.dma_start(maskb[:, :, :, :], ins["maskb"]).then_inc(sem("bf_in"), 16)
            pool.dma_start(headsel[:, :, :], ins["headsel"]).then_inc(sem("bf_in"), 16)
            pool.dma_start(tri[:, :], ins["tri"]).then_inc(sem("bf_in"), 16)
            pool.dma_start(oneb[:, :], ins["oneb"]).then_inc(sem("bf_in"), 16)
            nc.gpsimd.memset(zero[:, :], 0.0).then_inc(sem("zero"), 1)
            pool.wait_ge(sem("zero"), 1)
            for L in range(2):
                for i in range(0, (MAXB[L] + 1) * BS * DIM, 128 * 1152):
                    n = min(128 * 1152, (MAXB[L] + 1) * BS * DIM - i) // 128
                    flat = xs[L].rearrange("a b -> (a b)")[i:i + 128 * n].rearrange("(p n) -> p n", p=128)
                    pool.dma_start(flat, zero[:, 0:n]).then_inc(sem("xs_zero"), 16)
            for r in range(RING):
                pool.dma_start(wgu0[:, r, :, :], ins["wgu0"][r]).then_inc(sem(f"m0_w{r}"), 16)
                pool.dma_start(wd0[:, r, :, :], ins["wd0"][r]).then_inc(sem(f"m0_w{r}"), 16)
            NZ = sum(-(-(MAXB[L] + 1) * BS * DIM // (128 * 1152)) for L in range(2))
            pool.wait_ge(sem("xs_zero"), 16 * NZ)

            def experts_dma(L):
                p = f"m{L}_"
                pool.wait_ge(sem(p + "slot"), 1)
                for k in range(2):
                    for g in range(NG):
                        nc.gpsimd.indirect_dma_start(
                            out=xs[L], out_offset=bass.IndirectOffsetOnAxis(ap=slot[:, k, g:g + 1], axis=0),
                            in_=(y, rn)[L][:, g, :], in_offset=None).then_inc(sem(p + "sent"), 16)
                with pool.Fori(1, EX[L] // RING) as q:
                    for r in range(RING):
                        done = pool.value_load(firsti[0:1, bass.ds(q * RING + (r - RING + 1), 1)], min_val=1, max_val=MAXB[L])
                        pool.wait_ge(sem(p + "y_ps"), done)
                        pool.dma_start(WGU[L][:, r, :, :], ins[f"wgu{L}"][q * RING + r]).then_inc(sem(p + f"w{r}"), 16)
                        pool.dma_start(WD[L][:, r, :, :], ins[f"wd{L}"][q * RING + r]).then_inc(sem(p + f"w{r}"), 16)
                pool.wait_ge(sem(p + "all_out"), 1)
                for g in range(NG):
                    for k in range(2):
                        nc.gpsimd.indirect_dma_start(
                            out=yg[:, k, g, :], out_offset=None, in_=xs[L],
                            in_offset=bass.IndirectOffsetOnAxis(ap=slot[:, k, g:g + 1], axis=0))\
                            .then_inc(sem(f"back{g}"), 16)

            experts_dma(0)
            for n in range(4 * NJ):
                qk, j, q = n // (2 * NJ), n % (2 * NJ) // 2, n % 2
                dst = (rq, rk)[qk]
                pool.wait_ge(sem("b_rope"), n + 1)
                nc.gpsimd.tensor_tensor(dst[:, 0, j, q * 288:(q + 1) * 288], rt[:, n % 2, 0, :], rt[:, n % 2, 1, :],
                                        ALU.subtract).then_inc(sem("b_r"), 1)
                nc.gpsimd.tensor_tensor(dst[:, 1, j, q * 288:(q + 1) * 288], rt[:, n % 2, 2, :], rt[:, n % 2, 3, :],
                                        ALU.add).then_inc(sem("b_r"), 1)
            for r in range(RING):
                pool.dma_start(wgu1[:, r, :, :], ins["wgu1"][r]).then_inc(sem(f"m1_w{r}"), 16)
                pool.dma_start(wd1[:, r, :, :], ins["wd1"][r]).then_inc(sem(f"m1_w{r}"), 16)
            experts_dma(1)

        @block.scalar
        def _(act):
            act.dma_start(gb5[:, :, :], ins["gb5"]).then_inc(sem("gb_in"), 16)
            act.dma_start(brow[0:1, 1, :], ins["tok_b"]).then_inc(sem("gb_in"), 16)
            act.dma_start(ident[:, :], ins["ident"]).then_inc(sem("cst_in"), 16)
            act.dma_start(bias[:, :, :], ins["bias"]).then_inc(sem("cst_in"), 16)
            act.dma_start(rw0[:, :, :], ins["rw0"]).then_inc(sem("rw_in"), 16)
            act.dma_start(rw1[:, :, :], ins["rw1"]).then_inc(sem("rw_in"), 16)
            for name, t in (("wC1", wC1), ("wF1", wF1), ("wV1", wV1), ("wO1", wO1), ("wQ2", wQ2), ("wV2", wV2),
                            ("wO2", wO2)):
                act.dma_start(t[tuple([slice(None)] * len(t.shape))], ins[name]).then_inc(sem("l1_in"), 16)
            act.dma_start(wA[:, :, :], ins["wA"]).then_inc(sem("wA_in"), 16)
            act.dma_start(wV0[:, :, :], ins["wV0"]).then_inc(sem("wA_in"), 16)
            act.dma_start(wP0[:, :, :], ins["wP0"]).then_inc(sem("wA_in"), 16)
            for c in range(FC):
                act.wait_ge(sem(f"tok_in{c}"), 32)
                nc.scalar.activation(xsq[:, c, :], xw[:, c, :], ACT.Square).then_inc(sem("t_sq"), 1)
            act.wait_ge(sem("cst_in"), 48)
            act.wait_ge(sem("t_var"), 1)
            nc.scalar.activation(rstd[:, :], tmpg[:, :], ACT.Sqrt, bias=eps_ln[0:GT], scale=1.0)\
                .then_inc(sem("t_std"), 1)
            def std(k, eps=eps_ln):
                act.wait_ge(sem("ln_mv"), k)
                nc.scalar.activation(rstd[:, :], mv[:, :, 1], ACT.Sqrt, bias=eps[0:GT], scale=1.0)\
                    .then_inc(sem("ln_std"), 1)

            def evict_xnT(k, weight=None):
                for b in range(4):
                    act.wait_ge(sem("ln_T"), 4 * XT_OF[k] + b + 1)
                    hf, q = b // 2, b % 2
                    scale = 1.0 if weight is None else weight[:, hf:hf + 1]
                    nc.scalar.activation(xnT[:, hf, q * 288:(q + 1) * 288], PS[0:HB, b, 0:288], ACT.Copy,
                                         scale=scale).then_inc(sem("xnT"), 1)
            std(1)
            evict_xnT(1)
            for j in range(NJ):
                for q in range(2):
                    act.wait_ge(sem("a_qk"), 2 * j + q + 1)
                    nc.scalar.activation(qT[:, j, q * 288:(q + 1) * 288], PS[:, 4 + (2 * j + q) % 2, 0:288],
                                         ACT.Copy, scale=HD ** -0.5).then_inc(sem("a_qT"), 1)
            for g in range(NG):
                act.wait_ge(sem("a_v"), g + 1)
                nc.scalar.activation(va[:, g, :, 0:HD],
                                     PS[0:GT, g % 2, 0:DIM].rearrange("p (h d) -> p h d", h=NH),
                                     ACT.Copy).then_inc(sem("a_va"), 1)
            for i in range(4):
                act.wait_ge(sem("a_pos"), i + 1)
                nc.scalar.activation(
                    qa[:, :, :].rearrange("p j (b n) -> p n j b", n=N)[:, 9 * i:9 * i + 9, :, :],
                    PS[:, 2 + i, 0:432].rearrange("p (n j b) -> p n j b", j=NJ, b=B), ACT.Copy)\
                    .then_inc(sem("a_qa"), 1)
            with act.Fori(0, NG) as g:
                act.wait_ge(sem("att_mt_ps"), g + 1)
                nc.scalar.activation(a_mT[:, :], PS[:, 6, 0:36].bitcast(bf16), ACT.Copy).then_inc(sem("att_mt"), 1)
                act.wait_ge(sem("att_s2"), g + 1)
                nc.scalar.activation(a_p[:, :, :].rearrange("p (a b) k -> p a (b k)", a=3),
                                     PS[0:GT, 3:6, 0:288], ACT.Exp).then_inc(sem("att_exp"), 1)
                act.wait_ge(sem("a_oT"), g + 1)
                nc.scalar.activation(oaT[:, :, bass.ts(g, GT)],
                                     PS[:, 6, 128:344].rearrange("p (j t) -> p j t", j=NJ), ACT.Copy)\
                    .then_inc(sem("a_oaT"), 1)
            for i in range(4):
                act.wait_ge(sem("a_pos2"), i + 1)
                nc.scalar.activation(
                    of[:, :, :].rearrange("p j (b n) -> p n j b", n=N)[:, 9 * i:9 * i + 9, :, :],
                    PS[0:64, i, 0:432].rearrange("p (n j b) -> p n j b", j=NJ, b=B), ACT.Copy)\
                    .then_inc(sem("a_of"), 1)

            def experts_act(L):
                p, NS = f"m{L}_", HC[L] // 3
                act.wait_ge(sem(p + "diff"), 1)
                nc.scalar.activation(share[:, 1, :], share[:, 0, :], ACT.Exp).then_inc(sem(p + "exp"), 1)
                act.wait_ge(sem(p + "first"), 1)
                blocks = act.value_load(firsti[0:1, EX[L]:EX[L] + 1], min_val=1, max_val=MAXB[L])

                def block_T():
                    src = PS[0:HB, 4, 0:2 * BS].rearrange("p (k t) -> p k t", k=2)
                    if L == 0:
                        nc.scalar.activation(bxT[:, :, :], src, ACT.Copy).then_inc(sem(p + "xT"), 2)
                    else:
                        for k in range(2):
                            nc.scalar.activation(bxT[:, k, :], src[:, k, :], ACT.Copy, scale=w2n[:, k:k + 1])\
                                .then_inc(sem(p + "xT"), 1)
                act.wait_ge(sem(p + "xT_ps"), 1)
                block_T()
                with act.Fori(0, blocks) as b:
                    for s_ in range(NS):
                        act.wait_ge(sem(p + "gu"), b * NS + (s_ + 1))
                        nc.scalar.activation(sg[:, s_, :], PS[:, 2 * s_, 0:3 * BS], ACT.Silu).then_inc(sem(p + "sg"), 1)
                    act.wait_ge(sem(p + "xT_ps"), b + 2)
                    block_T()
            std(2)
            evict_xnT(2)
            experts_act(0)
            std(3)
            evict_xnT(3)
            for m in range(4):
                for q in range(2):
                    n = 2 * m + q
                    act.wait_ge(sem("r_c"), n + 1)
                    nc.scalar.activation(cT[:, m, q * 288:(q + 1) * 288], PS[0:HB, 4 + n % 2, 0:288], ACT.Identity,
                                         bias=binp[:, m:m + 1], scale=1.0).then_inc(sem("r_cT"), 1)
            for g in range(NG):
                act.wait_ge(sem("r_s"), g + 1)
                nc.scalar.activation(sf[:, g, :, :].rearrange("p h d -> p (h d)"), PS[0:GT, g % 2, 0:2 * DIM],
                                     ACT.Copy, scale=float(HD) ** -0.25).then_inc(sem("r_sf"), 1)
            for i in range(2):
                act.wait_ge(sem("r_arg"), i + 1)
                nc.scalar.activation(sf[:, 4 * i:4 * i + 4, :, :], sf[:, 4 * i:4 * i + 4, :, :], ACT.Exp)\
                    .then_inc(sem("r_exp"), 1)
            for b in range(8):
                act.wait_ge(sem("r_fT_ps"), b + 1)
                nc.scalar.activation(fT[:, b // 2, b % 2 * 288:(b % 2 + 1) * 288], PS[0:HB, 4 + b % 2, 0:288],
                                     ACT.Copy).then_inc(sem("r_fT"), 1)
            with act.Fori(0, NG) as g:
                act.wait_ge(sem("r_aT_ps"), g + 1)
                nc.scalar.activation(r_aT[:, :, :], PS[0:HB, 3, 0:2 * GT].rearrange("p (k t) -> p k t", k=2),
                                     ACT.Copy).then_inc(sem("r_aT"), 1)
            std(4)
            std(5, eps_rms)
            evict_xnT(5, w1n)
            for g in range(NG):
                act.wait_ge(sem("b_v"), g + 1)
                nc.scalar.activation(vb[:, g, :, 0:QD], PS[0:GT, g % 2, 0:KVH * QD]
                                     .rearrange("p (h d) -> p h d", h=KVH), ACT.Copy).then_inc(sem("b_vb"), 1)
            with act.Fori(0, NG) as g:
                act.wait_ge(sem("att_mt_ps"), g + (NG + 1))
                nc.scalar.activation(b_mT[:, :], PS[:, 6, 400:436].bitcast(bf16), ACT.Copy).then_inc(sem("att_mt"), 1)
                act.wait_ge(sem("att_s2"), g + (NG + 1))
                nc.scalar.activation(b_p[:, :, :].rearrange("p (a b) k -> p a (b k)", a=3),
                                     PS[0:GT, 3:6, 0:288], ACT.Exp, scale=float(QD) ** -0.5)\
                    .then_inc(sem("att_exp"), 1)
                act.wait_ge(sem("b_oT_ps"), g + 1)
                nc.scalar.activation(b_oT[:, :, :], PS[:, 0, 0:6 * GT].rearrange("p (c t) -> p c t", c=6), ACT.Copy)\
                    .then_inc(sem("b_oT"), 1)
            std(6, eps_rms)
            evict_xnT(6, w2n)
            experts_act(1)

        @block.vector
        def _(dve):
            tc = Chain(dve, sem("t_chain"))
            dve.wait_ge(sem("gb_in"), 32)
            for c in range(FC):
                dve.wait_ge(sem(f"tok_in{c}"), 32)
                tc(nc.vector.tensor_scalar(wc[:, c, 0:DIM], w5[:, c, 0, :], gb5[:, 0, c * SH:c * SH + 1], None,
                                           ALU.mult))
                for s in range(1, SH):
                    ins_ = nc.vector.scalar_tensor_tensor(wc[:, c, 0:DIM], w5[:, c, s, :],
                                                          gb5[:, 0, c * SH + s:c * SH + s + 1],
                                                          wc[:, c, 0:DIM], ALU.mult, ALU.add)
                    if s < SH - 1:
                        tc(ins_)
                if c == 0:
                    dve.wait_ge(sem("cst_in"), 48)
                ins_.then_inc(sem("t_wc"), 1)
                nc.vector.tensor_copy(wc[:, c, DIM:DIM + 1], cnt[:, c:c + 1]).then_inc(sem("t_wc"), 1)
            dve.wait_ge(sem("t_beta"), 1)
            nc.vector.tensor_tensor(brow[0:1, 0, :], PS[0:1, 6, 0:DIM], brow[0:1, 1, :], ALU.add)\
                .then_inc(sem("t_brow"), 1)
            dve.wait_ge(sem("t_acc"), 1)
            s1 = PS[0:GT, 0:4, 0:388].rearrange("p b (q c) -> p b q c", q=2)[:, :, :, DIM]
            s2 = PS[0:GT, 0:4, 0:388].rearrange("p b (q c) -> p b q c", q=2)[:, :, :, DIM + 1]
            m4 = mv[:, :, 0].rearrange("p (b q) -> p b q", q=2)
            e4 = mv[:, :, 1].rearrange("p (b q) -> p b q", q=2)
            K = PATCH * PATCH * SH * CH
            nc.vector.tensor_scalar(m4, s1, -1.0 / K, None, ALU.mult).then_inc(sem("t_chain"), 1)
            tc.n += 1
            tc(nc.vector.tensor_scalar(e4, s2, 1.0 / K, None, ALU.mult))
            tc(nc.vector.tensor_tensor(nmr[:, :], mv[:, :, 0], mv[:, :, 0], ALU.mult))
            nc.vector.tensor_tensor(tmpg[:, :], mv[:, :, 1], nmr[:, :], ALU.subtract).then_inc(sem("t_var"), 1)
            dve.wait_ge(sem("t_std"), 1)
            tc(nc.vector.reciprocal(rstd[:, :], rstd[:, :]))
            dve.wait_ge(sem("t_gsum"), 1)
            nc.vector.tensor_copy(gsum[:, :, :], PS[0:GT, 4, 0:2 * DIM].rearrange("p (a d) -> p a d", a=2))\
                .then_inc(sem("t_chain"), 1)
            tc.n += 1
            dve.wait_ge(sem("t_chain"), tc.n)
            for g in range(NG):
                acc = PS[0:GT, g // 2, (g % 2) * 194:(g % 2) * 194 + DIM]
                tc(nc.vector.scalar_tensor_tensor(h[:, g, :], gsum[:, 0, :], mv[:, g, 0:1], acc, ALU.mult, ALU.add))
                nc.vector.scalar_tensor_tensor(h[:, g, :], h[:, g, :], rstd[:, g:g + 1], gsum[:, 1, :],
                                               ALU.mult, ALU.add).then_inc(sem("t_h"), 1)
            dve.wait_ge(sem("t_h"), NG)


            lc = Chain(dve, sem("ln_chain"))

            def ln_stats(k, src=h, rms=False):
                for g in range(NG):
                    nc.vector.bn_stats(st6[:, g, :], src[:, g, :]).then_inc(sem("ln_chain"), 1)
                lc.n += NG
                dve.wait_ge(sem("ln_chain"), lc.n)
                for g in range(NG):
                    nc.vector.bn_aggr(mv[:, g, :], st6[:, g, :]).then_inc(sem("ln_agg"), 1)
                dve.wait_ge(sem("ln_agg"), k * NG)
                if rms:
                    lc(nc.vector.tensor_tensor(nmr[:, :], mv[:, :, 0], mv[:, :, 0], ALU.mult))
                    lc(nc.vector.tensor_tensor(mv[:, :, 1], mv[:, :, 1], nmr[:, :], ALU.add))
                nc.vector.tensor_copy(tmpg[:, :], mv[:, :, 0]).then_inc(sem("ln_mv"), 1)
                dve.wait_ge(sem("ln_std"), k)
                lc(nc.vector.reciprocal(rstd[:, :], rstd[:, :]))

            def ln_apply(k, dst, name):
                for g in range(NG):
                    nc.vector.tensor_scalar(dst[:, g, :], h[:, g, :], mv[:, g, 0:1], rstd[:, g:g + 1],
                                            ALU.subtract, ALU.mult).then_inc(sem(name), 1)

            def rms_apply(src, dst, name):
                for g in range(NG):
                    nc.vector.tensor_scalar(dst[:, g, :], src[:, g, :], rstd[:, g:g + 1], None,
                                            ALU.mult).then_inc(sem(name), 1)
            ln_stats(1)
            ln_apply(1, y, "a_y")
            for j in range(NJ):
                for q in range(2):
                    dve.wait_ge(sem("a_qk"), 2 * NJ + 2 * j + q + 1)
                    nc.vector.tensor_tensor(
                        ka[:, j, q * 288:(q + 1) * 288].rearrange("p (b n) -> p b n", n=N),
                        PS[:, 4 + (2 * j + q) % 2, 0:288].rearrange("p (b n) -> p b n", n=N),
                        krows.unsqueeze(1).to_broadcast([128, 8, N]), ALU.add).then_inc(sem("a_ka"), 1)
            nc.vector.memset(a_m[:, :], 0.0).then_inc(sem("a_va1"), 1)
            for g in range(NG):
                nc.vector.tensor_copy(va[:, g, :, HD:32], vrows.unsqueeze(1).to_broadcast([GT, NH, 16]))\
                    .then_inc(sem("a_va1"), 1)
            dve.wait_ge(sem("a_va1"), NG + 1)
            dve.wait_ge(sem("a_ka"), 2 * NJ)
            dve.wait_ge(sem("a_qa"), 4)
            with dve.Fori(0, NG) as g:
                nc.vector.tensor_copy(a_q[:, :, :], qa[:, :, bass.ts(g, GT)]).then_inc(sem("a_in"), 1)
                for j in range(NJ):
                    nc.vector.tensor_tensor(
                        a_kz[:, j, :, :], ka[:, j, bass.ts(g, GT)].unsqueeze(1).to_broadcast([128, 4, GT]),
                        blk4.unsqueeze(2).to_broadcast([128, 4, GT]), ALU.mult).then_inc(sem("a_in"), 1)
                dve.wait_ge(sem("att_s1"), g + 1)
                nc.vector.tensor_reduce(a_m[:, 0:NH].rearrange("p (a b) -> p a b", a=3),
                                        PS[0:GT, 0:3, 0:288].rearrange("p a (b k) -> p a b k", k=GT),
                                        AX.X, ALU.max, negate=True).then_inc(sem("att_max"), 1)
                dve.wait_ge(sem("att_av"), g + 1)
                o3 = PS[0:GT, 7, 0:384].rearrange("p (h d) -> p h d", h=NH)
                nc.vector.reciprocal(a_rec[:, :], o3[:, :, 30]).then_inc(sem("a_rec"), 1)
                dve.wait_ge(sem("a_rec"), g + 1)
                nc.vector.tensor_tensor(a_o[:, :, :], o3, a_rec[:, :].unsqueeze(2).to_broadcast([GT, NH, 32]),
                                        ALU.mult).then_inc(sem("att_o"), 1)
            for g in range(NG):
                dve.wait_ge(sem("a_proj"), g + 1)
                nc.vector.tensor_tensor(y[:, g, :], PS[0:GT, 4 + g % 2, 0:DIM], bias[:, 0, :], ALU.add)\
                    .then_inc(sem("a_res"), 1)
                dve.wait_ge(sem("a_res"), 2 * g + 1)
                nc.vector.tensor_tensor(h[:, g, :], h[:, g, :], y[:, g, :], ALU.add).then_inc(sem("a_res"), 1)
            dve.wait_ge(sem("a_res"), 2 * NG)

            def route(L):
                p, E = f"m{L}_", EX[L]
                c = Chain(dve, sem(p + "chain"))
                dve.wait_ge(sem(p + "logits"), 1)
                c(nc.vector.tensor_copy(lg[:, :, 0:E], PS[0:GT, 6, 0:NG * E].rearrange("p (g e) -> p g e", g=NG)))
                for g in range(NG):
                    nc.vector.max(top8[:, g, :], lg[:, g, 0:E]).then_inc(sem(p + "chain"), 1)
                c.n += NG
                dve.wait_ge(sem(p + "chain"), c.n)
                nc.vector.tensor_tensor(share[:, 0, :], top8[:, :, 1], top8[:, :, 0], ALU.subtract)\
                    .then_inc(sem(p + "diff"), 1)
                for g in range(NG):
                    nc.vector.max_index(idx8[:, g, :], top8[:, g, :], lg[:, g, 0:E]).then_inc(sem(p + "chain"), 1)
                c.n += NG
                dve.wait_ge(sem(p + "chain"), c.n)
                c(nc.vector.tensor_copy(idxf[:, :, :], idx8[:, :, 0:2]))
                for k in range(2):
                    nc.vector.tensor_tensor(sel[:, k, :, 0:E], iota16[:, 0:E].unsqueeze(1).to_broadcast([GT, NG, E]),
                                            idxf[:, :, k:k + 1].to_broadcast([GT, NG, E]), ALU.is_equal)\
                        .then_inc(sem(p + "chain"), 1)
                c.n += 2
                dve.wait_ge(sem(p + "chain"), c.n)
                nc.vector.tensor_tensor(selb[:, :, 0:E], sel[:, 0, :, 0:E], sel[:, 1, :, 0:E], ALU.add)\
                    .then_inc(sem(p + "sel"), 1)
                dve.wait_ge(sem(p + "exp"), 1)
                c(nc.vector.tensor_scalar(share[:, 0, :], share[:, 1, :], 1.0, None, ALU.add))
                c(nc.vector.reciprocal(share[:, 0, :], share[:, 0, :]))
                c(nc.vector.tensor_tensor(share[:, 1, :], share[:, 1, :], share[:, 0, :], ALU.mult))
                dve.wait_ge(sem(p + "pos"), 1)
                c(nc.vector.tensor_copy(tot[:, 0:E], PS[0:GT, 5, 0:E]))
                c(nc.vector.tensor_tensor(over[:, 0:E, :], tot[:, 0:E].unsqueeze(2).to_broadcast([GT, E, NTHR]),
                                          thr.unsqueeze(1).to_broadcast([GT, E, NTHR]), ALU.is_gt))
                c(nc.vector.tensor_reduce(nblk[:, 0:E], over[:, 0:E, :], AX.X, ALU.add))
                c(nc.vector.tensor_scalar(nblk[:, 0:E], nblk[:, 0:E], 1.0, None, ALU.add))
                c(nc.vector.tensor_tensor(prod[:, 0:E + 1, 0:E], before[:, 0:E + 1, 0:E],
                                          nblk[:, 0:E].unsqueeze(1).to_broadcast([GT, E + 1, E]), ALU.mult))
                c(nc.vector.tensor_reduce(first[:, 0:E + 1], prod[:, 0:E + 1, 0:E], AX.X, ALU.add))
                nc.vector.tensor_copy(firsti[:, 0:E + 1], first[:, 0:E + 1]).then_inc(sem(p + "first"), 1)
                c(nc.vector.scalar_tensor_tensor(
                    slote[:, :, 0:E], first[:, 0:E].unsqueeze(1).to_broadcast([GT, NG, E]), float(BS),
                    PS[0:GT, 7, 0:NG * E].rearrange("p (g e) -> p g e", g=NG), ALU.mult, ALU.add))
                for k in range(2):
                    c(nc.vector.tensor_tensor(sel[:, k, :, 0:E], sel[:, k, :, 0:E], slote[:, :, 0:E], ALU.mult))
                    c(nc.vector.tensor_reduce(slotf[:, k, :], sel[:, k, :, 0:E], AX.X, ALU.add))
                nc.vector.tensor_copy(slot[:, :, :], slotf[:, :, :]).then_inc(sem(p + "slot"), 1)

            def experts_dve(L):
                p, NS = f"m{L}_", HC[L] // 3
                dve.wait_ge(sem(p + "first"), 1)
                blocks = dve.value_load(firsti[0:1, EX[L]:EX[L] + 1], min_val=1, max_val=MAXB[L])
                with dve.Fori(0, blocks) as b:
                    for s_ in range(NS):
                        dve.wait_ge(sem(p + "sg"), b * NS + (s_ + 1))
                        nc.vector.tensor_tensor(hT[:, 3 * s_:3 * s_ + 3, :],
                                                sg[:, s_, :].rearrange("p (c t) -> p c t", c=3),
                                                PS[:, 2 * s_ + 1, 0:3 * BS].rearrange("p (c t) -> p c t", c=3),
                                                ALU.mult).then_inc(sem(p + "h"), 1)
                    dve.wait_ge(sem(p + "y_ps"), b + 1)
                    dve.wait_ge(sem(p + "y_out"), b * 16 + 16)
                    nc.vector.tensor_copy(yo[:, :], PS[0:BS, 5, 0:DIM]).then_inc(sem(p + "y"), 1)
                for g in range(NG):
                    dve.wait_ge(sem(f"back{g}"), 32 * (L + 1))
                    for k in range(2):
                        nc.vector.scalar_tensor_tensor(h[:, g, :], yg[:, k, g, :], share[:, k, g:g + 1], h[:, g, :],
                                                       ALU.mult, ALU.add).then_inc(sem(p + "res"), 1)
                        dve.wait_ge(sem(p + "res"), 2 * g + k + 1)

            ln_stats(2)
            ln_apply(2, y, "m0_yn")
            route(0)
            experts_dve(0)
            ln_stats(3)
            ln_apply(3, y, "r_y")
            nc.vector.memset(vr[:, :, :, HD:HD + 1], 1.0).then_inc(sem("r_v1"), 1)
            for g in range(NG):
                dve.wait_ge(sem("r_v"), g + 1)
                nc.vector.tensor_tensor(vr[:, g, :, 0:HD],
                                        PS[0:GT, 2 + g % 2, 0:DIM].rearrange("p (h d) -> p h d", h=NH),
                                        bias[:, 2, :].rearrange("p (h d) -> p h d", h=NH), ALU.add)\
                    .then_inc(sem("r_vr"), 1)
            c = Chain(dve, sem("r_chain"))
            for i in range(2):
                gs = slice(4 * i, 4 * i + 4)
                dve.wait_ge(sem("r_sf"), 4 * i + 4)
                nc.vector.tensor_reduce(ssum[:, gs, :], sf[:, gs, :, :], AX.X, ALU.add).then_inc(sem("r_chain"), 1)
                nc.vector.tensor_reduce(smax[:, gs, 0:NH], sf[:, gs, 0:NH, :], AX.X, ALU.max)\
                    .then_inc(sem("r_chain"), 1)
                nc.vector.tensor_reduce(kmax[:, gs], sf[:, gs, NH:2 * NH, :], AX.XY, ALU.max)\
                    .then_inc(sem("r_chain"), 1)
                c.n += 3
                dve.wait_ge(sem("r_chain"), c.n)
                nc.vector.scalar_tensor_tensor(smax[:, gs, 0:NH], ssum[:, gs, 0:NH], 0.5, smax[:, gs, 0:NH],
                                               ALU.mult, ALU.add).then_inc(sem("r_chain"), 1)
                nc.vector.scalar_tensor_tensor(smax[:, gs, NH:2 * NH], ssum[:, gs, NH:2 * NH], 0.5,
                                               kmax[:, gs].unsqueeze(2).to_broadcast([GT, 4, NH]),
                                               ALU.mult, ALU.add).then_inc(sem("r_chain"), 1)
                c.n += 2
                dve.wait_ge(sem("r_chain"), c.n)
                nc.vector.tensor_tensor(sf[:, gs, :, :], sf[:, gs, :, :],
                                        smax[:, gs, :].unsqueeze(3).to_broadcast([GT, 4, 2 * NH, HD]), ALU.subtract)\
                    .then_inc(sem("r_arg"), 1)
            for i in range(2):
                gs = slice(4 * i, 4 * i + 4)
                dve.wait_ge(sem("r_exp"), i + 1)
                nc.vector.tensor_scalar(sf[:, gs, :, :], sf[:, gs, :, :], 1e-6, float(HD) ** -0.5, ALU.add, ALU.mult)\
                    .then_inc(sem("r_f"), 1)
            dve.wait_ge(sem("r_fT"), 8)
            with dve.Fori(0, NG) as g:
                c = Chain(dve, sem("r_chain2"), g * 5)
                nc.vector.tensor_copy(r_k[:, :, :], fT[:, 2:4, bass.ts(g, GT)]).then_inc(sem("r_in"), 1)
                for i in range(2):
                    nc.vector.tensor_tensor(
                        r_qz[:, i, :, :], fT[:, i, bass.ts(g, GT)].unsqueeze(1).to_broadcast([HB, 6, GT]),
                        blk6.unsqueeze(2).to_broadcast([HB, 6, GT]), ALU.mult).then_inc(sem("r_in"), 1)
                dve.wait_ge(sem("r_qk"), g + 1)
                nc.vector.tensor_tensor(r_p[:, :, :].rearrange("p (a b) t -> p a b t", a=2),
                                        PS[0:GT, 0:2, 0:432].rearrange("p a (b t) -> p a b t", b=6),
                                        causal01.unsqueeze(1).unsqueeze(1).to_broadcast([GT, 2, 6, GT]), ALU.mult)\
                    .then_inc(sem("r_p"), 1)
                dve.wait_ge(sem("r_av"), g + 1)
                o3 = PS[0:GT, 2, 0:NH * (HD + 1)].rearrange("p (h d) -> p h d", h=NH)
                c(nc.vector.tensor_scalar(r_den[:, :], o3[:, :, HD], 1e-6, None, ALU.add))
                c(nc.vector.reciprocal(r_den[:, :], r_den[:, :]))
                nc.vector.tensor_tensor(r_a[:, :, :], o3[:, :, 0:HD],
                                        r_den[:, :].unsqueeze(2).to_broadcast([GT, NH, HD]), ALU.mult)\
                    .then_inc(sem("r_a"), 1)
                dve.wait_ge(sem("r_proj"), g + 1)
                c(nc.vector.tensor_tensor(h[:, bass.ds(g, 1), :], h[:, bass.ds(g, 1), :],
                                          PS[0:GT, 4:5, 0:DIM], ALU.add))
                c(nc.vector.tensor_tensor(h[:, bass.ds(g, 1), :], h[:, bass.ds(g, 1), :], bias[:, 1:2, :], ALU.add))
                c(nc.vector.tensor_copy(tmpg[:, 0:1], r_den[:, 0:1]))
            ln_stats(4)
            ln_apply(4, y, "b_y")
            dve.wait_ge(sem("b_y"), NG)
            ln_stats(5, y, True)
            rms_apply(y, rn, "b_rn")
            nc.vector.memset(vb[:, :, :, QD:QD + 1], 1.0).then_inc(sem("b_v1"), 1)
            nc.vector.memset(b_m[:, :], 0.0).then_inc(sem("b_v1"), 1)
            cs = [t[:, 0:N].unsqueeze(1).to_broadcast([128, 8, N]) for t in (rcos, rsin)]
            for n in range(4 * NJ):
                dve.wait_ge(sem("b_qk"), n + 1)
                if n >= 2:
                    dve.wait_ge(sem("b_r"), 2 * (n - 1))
                for i, (eo, t) in enumerate(((0, 0), (1, 1), (0, 1), (1, 0))):
                    last = nc.vector.tensor_tensor(
                        rt[:, n % 2, i, :].rearrange("p (b n) -> p b n", n=N),
                        PS[:, 4 + 2 * (n % 2) + eo, 0:288].rearrange("p (b n) -> p b n", n=N), cs[t], ALU.mult)
                last.then_inc(sem("b_rope"), 1)
            dve.wait_ge(sem("b_r"), 8 * NJ)
            dve.wait_ge(sem("b_v1"), 2)
            with dve.Fori(0, NG) as g:
                c = Chain(dve, sem("b_chain"), g)
                for eo in range(2):
                    nc.vector.tensor_copy(b_q[:, eo, :, :], rq[:, eo, :, bass.ts(g, GT)]).then_inc(sem("b_in"), 1)
                for eo in range(2):
                    for j in range(NJ):
                        nc.vector.tensor_tensor(
                            b_kz[:, eo, j, :, :], rk[:, eo, j, bass.ts(g, GT)].unsqueeze(1).to_broadcast([128, 4, GT]),
                            blk4.unsqueeze(2).to_broadcast([128, 4, GT]), ALU.mult).then_inc(sem("b_in"), 1)
                dve.wait_ge(sem("att_s1"), g + (NG + 1))
                nc.vector.tensor_reduce(b_m[:, 0:QH].rearrange("p (a b) -> p a b", a=3),
                                        PS[0:GT, 0:3, 0:288].rearrange("p a (b k) -> p a b k", k=GT),
                                        AX.X, ALU.max, negate=True).then_inc(sem("att_max"), 1)
                dve.wait_ge(sem("att_av"), g + (NG + 1))
                o4 = PS[0:GT, 6:8, 0:390].rearrange("p a (h d) -> p a h d", h=6)
                c(nc.vector.reciprocal(b_rec[:, :].rearrange("p (a h) -> p a h", a=2), o4[:, :, :, QD]))
                nc.vector.tensor_tensor(b_o[:, :, :].rearrange("p (a h) d -> p a h d", a=2), o4[:, :, :, 0:QD],
                                        b_rec[:, :].rearrange("p (a h) -> p a h", a=2).unsqueeze(3)
                                        .to_broadcast([GT, 2, 6, QD]), ALU.mult).then_inc(sem("att_o"), 1)
                dve.wait_ge(sem("b_proj"), g + 1)
                nc.vector.tensor_tensor(y[:, bass.ds(g, 1), :], y[:, bass.ds(g, 1), :], PS[0:GT, 1:2, 0:DIM],
                                        ALU.add).then_inc(sem("b_hin"), 1)
            dve.wait_ge(sem("b_hin"), NG)
            ln_stats(6, y, True)
            rms_apply(y, rn, "m1_yn")
            for g in range(NG):
                nc.vector.tensor_tensor(h[:, g, :], h[:, g, :], y[:, g, :], ALU.add).then_inc(sem("b_h"), 1)
            dve.wait_ge(sem("b_h"), NG)
            route(1)
            experts_dve(1)
            nc.vector.tensor_copy(tmpg[:, :], rstd[:, :]).then_inc(sem("h_last"), 1)

        @block.tensor
        def _(pe):
            mm = nc.tensor.matmul
            pe.wait_ge(sem("gb_in"), 32)
            for c in range(FC):
                pe.wait_ge(sem(f"tok_in{c}"), 32)
                for s in range(SH):
                    last = mm(PS[0:1, 6, 0:DIM], gb5[:, 1, c * SH + s:c * SH + s + 1], w5[:, c, s, :],
                              start=(c == 0 and s == 0), stop=(c == FC - 1 and s == SH - 1))
                if c == FC - 1:
                    last.then_inc(sem("t_beta"), 1)
                pe.wait_ge(sem("t_wc"), 2 * c + 2)
                pe.wait_ge(sem("t_sq"), c + 1)
                for g in range(NG):
                    o = (g % 2) * 194
                    mm(PS[0:GT, g // 2, o:o + DIM + 1], xw[:, c, bass.ts(g, GT)], wc[:, c, :],
                       start=(c == 0 and g % 2 == 0), stop=(c == FC - 1), skip_group_check=True)
                    last = mm(PS[0:GT, g // 2, o + DIM + 1:o + DIM + 2], xsq[:, c, bass.ts(g, GT)],
                              wc[:, c, DIM:DIM + 1], start=False, stop=(c == FC - 1), skip_group_check=True)
            last.then_inc(sem("t_acc"), 1)
            for c in range(FC):
                mm(PS[0:GT, 4, 0:DIM], ones[0:FP, 0:GT], wc[:, c, 0:DIM], start=(c == 0), stop=(c == FC - 1))
            pe.wait_ge(sem("t_brow"), 1)
            mm(PS[0:GT, 4, DIM:2 * DIM], ones[0:1, 0:GT], brow[0:1, 0, :], start=True, stop=True)\
                .then_inc(sem("t_gsum"), 1)

            def transpose_xn(k, name, src=y):
                for b in range(4):
                    hf, q = b // 2, b % 2
                    for i in range(4):
                        g = 4 * q + i
                        pe.wait_ge(sem(name), g + 1)
                        last = nc.tensor.transpose(PS[0:HB, b, i * GT:(i + 1) * GT],
                                                   src[:, g, hf * HB:(hf + 1) * HB], ident[0:GT, 0:GT])
                    last.then_inc(sem("ln_T"), 1)

            transpose_xn(1, "a_y")
            pe.wait_ge(sem("wA_in"), 48)
            pe.wait_ge(sem("xnT"), 4)
            for j in range(2 * NJ):
                for q in range(2):
                    n = 2 * j + q
                    if n >= 2:
                        if n - 2 < 2 * NJ:
                            pe.wait_ge(sem("a_qT"), n - 1)
                        else:
                            pe.wait_ge(sem("a_ka"), n - 1 - 2 * NJ)
                    for k in range(2):
                        last = mm(PS[:, 4 + n % 2, 0:288], wA[:, k, j * 128:(j + 1) * 128],
                                  xnT[:, k, q * 288:(q + 1) * 288], start=(k == 0), stop=(k == 1))
                    last.then_inc(sem("a_qk"), 1)
            for g in range(NG):
                if g >= 2:
                    pe.wait_ge(sem("a_va"), g - 1)
                for k in range(2):
                    last = mm(PS[0:GT, g % 2, 0:DIM], xnT[:, k, bass.ts(g, GT)], wV0[:, k, :],
                              start=(k == 0), stop=(k == 1))
                last.then_inc(sem("a_v"), 1)
            pe.wait_ge(sem("posk_in"), 16)
            pe.wait_ge(sem("bf_in"), 80)
            pe.wait_ge(sem("a_qT"), 2 * NJ)
            pe.wait_ge(sem("a_ka"), 2 * NJ)
            qn = qT[:, :, :].rearrange("p j (b n) -> p n j b", n=N)
            for n in range(N):
                i = n % 9
                last = mm(PS[:, 2 + n // 9, i * 48:(i + 1) * 48].rearrange("p (j b) -> p j b", j=NJ),
                          posk[:, n, :], qn[:, n, :, :], start=True, stop=True)
                if i == 8:
                    last.then_inc(sem("a_pos"), 1)
            pe.wait_ge(sem("a_qa"), 4)
            with pe.Fori(0, NG) as g:
                pe.wait_ge(sem("a_in"), 4 * g + 4)
                for j in range(NJ):
                    mm(PS[0:GT, j, 0:288], identb[0:GT, 0:GT], maskb[:, 0, :, :], start=True, stop=False)
                    last = mm(PS[0:GT, j, 0:288], a_q[:, j, :], a_kz[:, j, :, :], start=False, stop=True)
                last.then_inc(sem("att_s1"), 1)
                pe.wait_ge(sem("att_max"), g + 1)
                nc.tensor.transpose(PS[:, 6, 0:36].bitcast(bf16), a_m[:, :], identb[0:GT, 0:GT])\
                    .then_inc(sem("att_mt_ps"), 1)
                for j in range(NJ):
                    mm(PS[0:GT, 3 + j, 0:288], identb[0:GT, 0:GT], maskb[:, 0, :, :], start=True, stop=False,
                       skip_group_check=True)
                    for r in range(4):
                        mm(PS[0:GT, 3 + j, r * GT:(r + 1) * GT], a_kz[:, j, r, :], a_q[:, j, :],
                           start=False, stop=False, skip_group_check=True)
                pe.wait_ge(sem("att_mt"), g + 1)
                for hh in range(NH):
                    j, r = hh // 4, hh % 4
                    last = mm(PS[0:GT, 3 + j, r * GT:(r + 1) * GT], headsel[:, hh, :], a_mT[:, :],
                              start=False, stop=True, skip_group_check=True)
                last.then_inc(sem("att_s2"), 1)
                pe.wait_ge(sem("att_exp"), g + 1)
                for hh in range(NH):
                    last = mm(PS[0:GT, 7, hh * 32:(hh + 1) * 32], a_p[:, hh, :], va[:, g, hh, :],
                              start=True, stop=True)
                last.then_inc(sem("att_av"), 1)
                pe.wait_ge(sem("att_o"), g + 1)
                for j in range(NJ):
                    last = nc.tensor.transpose(PS[:, 6, 128 + j * GT:128 + (j + 1) * GT],
                                               a_o[:, 4 * j:4 * j + 4, :], ident[0:GT, 0:GT])
                last.then_inc(sem("a_oT"), 1)
                pe.wait_ge(sem("a_oaT"), g + 1)
            pe.wait_ge(sem("posv_in"), 16)
            on = oaT[:, :, :].rearrange("p j (b n) -> p n j b", n=N)
            for n in range(N):
                i = n % 9
                last = mm(PS[0:64, n // 9, i * 48:(i + 1) * 48].rearrange("p (j b) -> p j b", j=NJ),
                          posv[:, n, :], on[:, n, :, :], start=True, stop=True)
                if i == 8:
                    last.then_inc(sem("a_pos2"), 1)
            pe.wait_ge(sem("a_of"), 4)
            for g in range(NG):
                if g >= 2:
                    pe.wait_ge(sem("a_res"), 2 * g - 3)
                for j in range(NJ):
                    last = mm(PS[0:GT, 4 + g % 2, 0:DIM], of[:, j, bass.ts(g, GT)], wP0[:, j, :],
                              start=(j == 0), stop=(j == NJ - 1))
                last.then_inc(sem("a_proj"), 1)


            def route_pe(L):
                p, E = f"m{L}_", EX[L]
                pe.wait_ge(sem("rw_in"), 32)
                for g in range(NG):
                    for k in range(2):
                        last = mm(PS[0:GT, 6, g * E:(g + 1) * E], xnT[:, k, bass.ts(g, GT)], RW[L][:, k, :],
                                  start=(k == 0), stop=(k == 1))
                last.then_inc(sem(p + "logits"), 1)
                pe.wait_ge(sem(p + "sel"), 1)
                mm(PS[0:GT, 7, 0:NG * E], tri[:, :], selb[:, :, 0:E], start=True, stop=False,
                   skip_group_check=True)
                for g in range(NG - 1):
                    mm(PS[0:GT, 7, (g + 1) * E:NG * E], oneb[:, :],
                       selb[:, g:g + 1, 0:E].to_broadcast([GT, NG - 1 - g, E]), start=False, stop=(g == NG - 2),
                       skip_group_check=True)
                for g in range(NG):
                    last = mm(PS[0:GT, 5, 0:E], oneb[:, :], selb[:, g, 0:E], start=(g == 0), stop=(g == NG - 1))
                last.then_inc(sem(p + "pos"), 1)

            def experts_pe(L):
                p, NS, H = f"m{L}_", HC[L] // 3, HC[L]
                pe.wait_ge(sem(p + "first"), 1)

                def block_T():
                    for k in range(2):
                        last = nc.tensor.transpose(PS[0:HB, 4, k * BS:(k + 1) * BS], bx[:, k * HB:(k + 1) * HB],
                                                   ident[0:BS, 0:BS])
                    last.then_inc(sem(p + "xT_ps"), 1)
                pe.wait_ge(sem(p + "x_in"), 16)
                block_T()
                with pe.Fori(0, EX[L] // RING) as q:
                    for r in range(RING):
                        lo = pe.value_load(firsti[0:1, bass.ds(q * RING + r, 1)], min_val=0, max_val=MAXB[L])
                        hi = pe.value_load(firsti[0:1, bass.ds(q * RING + (r + 1), 1)], min_val=1, max_val=MAXB[L])
                        with pe.Fori(lo, hi) as b:
                            pe.wait_ge(sem(p + f"w{r}"), q * 32 + 32)
                            pe.wait_ge(sem(p + "xT"), b * 2 + 2)
                            for s_ in range(NS):
                                for u in range(2):
                                    for c in range(3):
                                        o = (u * H + 3 * s_ + c) * 128
                                        for k in range(2):
                                            last = mm(PS[:, 2 * s_ + u, c * BS:(c + 1) * BS],
                                                      WGU[L][:, r, k, o:o + 128], bxT[:, k, :],
                                                      start=(k == 0), stop=(k == 1))
                                last.then_inc(sem(p + "gu"), 1)
                            pe.wait_ge(sem(p + "x_in"), b * 16 + 32)
                            block_T()
                            for c in range(H):
                                if c % 3 == 0:
                                    pe.wait_ge(sem(p + "h"), b * NS + (c // 3 + 1))
                                last = mm(PS[0:BS, 5, 0:DIM], hT[:, c, :], WD[L][:, r, c, :],
                                          start=(c == 0), stop=(c == H - 1))
                            last.then_inc(sem(p + "y_ps"), 1)

            transpose_xn(2, "m0_yn")
            pe.wait_ge(sem("xnT"), 8)
            route_pe(0)
            experts_pe(0)
            pe.wait_ge(sem("l1_in"), 16 * 7)

            transpose_xn(3, "r_y")
            pe.wait_ge(sem("xnT"), 12)
            for m in range(4):
                for q in range(2):
                    n = 2 * m + q
                    if n >= 2:
                        pe.wait_ge(sem("r_cT"), n - 1)
                    for k in range(2):
                        last = mm(PS[0:HB, 4 + n % 2, 0:288], wC1[:, k, m * HB:(m + 1) * HB],
                                  xnT[:, k, q * 288:(q + 1) * 288], start=(k == 0), stop=(k == 1))
                    last.then_inc(sem("r_c"), 1)
            for g in range(NG):
                if g >= 2:
                    pe.wait_ge(sem("r_vr"), g - 1)
                for k in range(2):
                    last = mm(PS[0:GT, 2 + g % 2, 0:DIM], xnT[:, k, bass.ts(g, GT)], wV1[:, k, :],
                              start=(k == 0), stop=(k == 1))
                last.then_inc(sem("r_v"), 1)
            pe.wait_ge(sem("r_cT"), 8)
            for g in range(NG):
                if g >= 2:
                    pe.wait_ge(sem("r_sf"), g - 1)
                for m in range(4):
                    last = mm(PS[0:GT, g % 2, m * HB:(m + 1) * HB], cT[:, m, bass.ts(g, GT)], wF1[:, :],
                              start=True, stop=True)
                last.then_inc(sem("r_s"), 1)
            for b in range(8):
                m, q = b // 2, b % 2
                pe.wait_ge(sem("r_f"), q + 1)
                if b >= 2:
                    pe.wait_ge(sem("r_fT"), b - 1)
                for i in range(4):
                    last = nc.tensor.transpose(PS[0:HB, 4 + b % 2, i * GT:(i + 1) * GT],
                                               sf[:, 4 * q + i, 6 * m:6 * m + 6, :], ident[0:GT, 0:GT])
                last.then_inc(sem("r_fT_ps"), 1)
            pe.wait_ge(sem("r_v1"), 1)
            with pe.Fori(0, NG) as g:
                pe.wait_ge(sem("r_in"), 3 * g + 3)
                for i in range(2):
                    last = mm(PS[0:GT, i, 0:432], r_k[:, i, :], r_qz[:, i, :, :], start=True, stop=True)
                last.then_inc(sem("r_qk"), 1)
                pe.wait_ge(sem("r_p"), g + 1)
                for hh in range(NH):
                    last = mm(PS[0:GT, 2, hh * (HD + 1):(hh + 1) * (HD + 1)], r_p[:, hh, :], vr[:, g, hh, :],
                              start=True, stop=True)
                last.then_inc(sem("r_av"), 1)
                pe.wait_ge(sem("r_a"), g + 1)
                for i in range(2):
                    last = nc.tensor.transpose(PS[0:HB, 3, i * GT:(i + 1) * GT], r_a[:, 6 * i:6 * i + 6, :],
                                               ident[0:GT, 0:GT])
                last.then_inc(sem("r_aT_ps"), 1)
                pe.wait_ge(sem("r_aT"), g + 1)
                for i in range(2):
                    last = mm(PS[0:GT, 4, 0:DIM], r_aT[:, i, :], wO1[:, i, :], start=(i == 0), stop=(i == 1))
                last.then_inc(sem("r_proj"), 1)

            transpose_xn(5, "b_rn", rn)
            pe.wait_ge(sem("xnT"), 16)
            for g in range(NG):
                if g >= 2:
                    pe.wait_ge(sem("b_vb"), g - 1)
                for k in range(2):
                    last = mm(PS[0:GT, g % 2, 0:KVH * QD], xnT[:, k, bass.ts(g, GT)], wV2[:, k, :],
                              start=(k == 0), stop=(k == 1))
                last.then_inc(sem("b_v"), 1)
            for n in range(4 * NJ):
                qk, j, q = n // (2 * NJ), n % (2 * NJ) // 2, n % 2
                if n >= 2:
                    pe.wait_ge(sem("b_rope"), n - 1)
                for eo in range(2):
                    o = ((qk * NJ + j) * 2 + eo) * 128
                    for k in range(2):
                        last = mm(PS[:, 4 + 2 * (n % 2) + eo, 0:288], wQ2[:, k, o:o + 128],
                                  xnT[:, k, q * 288:(q + 1) * 288], start=(k == 0), stop=(k == 1))
                last.then_inc(sem("b_qk"), 1)
            pe.wait_ge(sem("b_vb"), NG)
            with pe.Fori(0, NG) as g:
                pe.wait_ge(sem("b_in"), 8 * g + 8)
                for j in range(NJ):
                    mm(PS[0:GT, j, 0:288], identb[0:GT, 0:GT], maskb[:, 1, :, :], start=True, stop=False)
                    for eo in range(2):
                        last = mm(PS[0:GT, j, 0:288], b_q[:, eo, j, :], b_kz[:, eo, j, :, :],
                                  start=False, stop=(eo == 1))
                last.then_inc(sem("att_s1"), 1)
                pe.wait_ge(sem("att_max"), g + (NG + 1))
                nc.tensor.transpose(PS[:, 6, 400:436].bitcast(bf16), b_m[:, :], identb[0:GT, 0:GT])\
                    .then_inc(sem("att_mt_ps"), 1)
                for j in range(NJ):
                    mm(PS[0:GT, 3 + j, 0:288], identb[0:GT, 0:GT], maskb[:, 2, :, :], start=True, stop=False,
                       skip_group_check=True)
                    for r in range(4):
                        for eo in range(2):
                            mm(PS[0:GT, 3 + j, r * GT:(r + 1) * GT], b_kz[:, eo, j, r, :], b_q[:, eo, j, :],
                               start=False, stop=False, skip_group_check=True)
                pe.wait_ge(sem("att_mt"), g + (NG + 1))
                for hh in range(QH):
                    j, r = hh // 4, hh % 4
                    last = mm(PS[0:GT, 3 + j, r * GT:(r + 1) * GT], headsel[:, hh, :], b_mT[:, :],
                              start=False, stop=True, skip_group_check=True)
                last.then_inc(sem("att_s2"), 1)
                pe.wait_ge(sem("att_exp"), g + (NG + 1))
                for hh in range(QH):
                    last = mm(PS[0:GT, 6 + hh // 6, hh % 6 * (QD + 1):(hh % 6 + 1) * (QD + 1)], b_p[:, hh, :],
                              vb[:, g, hh // 4, :], start=True, stop=True)
                last.then_inc(sem("att_av"), 1)
                pe.wait_ge(sem("att_o"), g + (NG + 1))
                for c in range(6):
                    last = nc.tensor.transpose(PS[:, 0, c * GT:(c + 1) * GT], b_o[:, 2 * c:2 * c + 2, :],
                                               ident[0:GT, 0:GT])
                last.then_inc(sem("b_oT_ps"), 1)
                pe.wait_ge(sem("b_oT"), g + 1)
                for c in range(6):
                    last = mm(PS[0:GT, 1, 0:DIM], b_oT[:, c, :], wO2[:, c, :], start=(c == 0), stop=(c == 5))
                last.then_inc(sem("b_proj"), 1)
            transpose_xn(6, "m1_yn", rn)
            pe.wait_ge(sem("xnT"), 20)
            route_pe(1)
            experts_pe(1)


def layouts(inputs):
    import numpy as np
    f = np.float32
    a = {k: np.asarray(v) for k, v in inputs.items()}
    d = {}
    feats = [(u, v, c) for u in range(18) for v in range(18) if not (u in (0, 17) and v in (0, 17)) for c in range(CH)]
    pad = np.zeros((B, CH, IMG + 2, IMG + 2), f)
    pad[:, :, 1:-1, 1:-1] = a["x"]
    fu, fv, fc = (np.array(t) for t in zip(*feats))
    at = PATCH * np.arange(GRID)
    win = pad[:, fc[:, None, None], fu[:, None, None] + at[None, :, None], fv[:, None, None] + at[None, None, :]]
    d["xw"] = win.transpose(1, 0, 2, 3).reshape(FC, FP, TOK).transpose(1, 0, 2)
    shifts = [(1, 1), (1, 0), (1, 2), (0, 1), (2, 1)]
    w5 = np.zeros((FC * FP, SH, DIM), f)
    gb = np.zeros((2, FC * FP, SH), f)
    count = np.zeros(FC * FP, f)
    for s, (du, dv) in enumerate(shifts):
        i, j = fu - du, fv - dv
        ok = (i >= 0) & (i < PATCH) & (j >= 0) & (j < PATCH)
        row = ((i * PATCH + j) * SH * CH + s * CH + fc)[ok]
        w5[ok, s] = a["L0_tok_w"][row]
        gb[0, ok, s] = a["L0_tok_ln_gamma"][row]
        gb[1, ok, s] = a["L0_tok_ln_beta"][row]
        count[ok] += 1
    d["w5"] = w5.reshape(FC, FP, SH, DIM).transpose(1, 0, 2, 3)
    d["gb5"] = gb.reshape(2, FC, FP, SH).transpose(2, 0, 1, 3).reshape(FP, 2, FC * SH)
    d["tok_b"] = a["L0_tok_b"][None, :]
    d["ident"] = np.eye(128, dtype=f)
    d["identb"] = np.eye(128).astype(f)
    cst = np.zeros((128, 768), f)
    cst[:, 0:4] = np.arange(128)[:, None] // 32 == np.arange(4)
    cst[:HB, 4:10] = np.arange(HB)[:, None] // 16 == np.arange(6)
    cst[:FP, 16:24] = count.reshape(FC, FP).T
    L = N - 1
    side = int(L ** 0.5)
    r_ = np.arange(L)
    krow = np.zeros((16, N), f)
    krow[0:7, 1:] = r_ // side == np.arange(7)[:, None]
    krow[7:12, 1:] = r_ % side == np.arange(5)[:, None]
    krow[12:14, 0] = 1
    for r in range(4):
        cst[32 * r + 16:32 * r + 32, 32:68] = krow
    vrow = np.concatenate([krow, krow], axis=1).T.copy()
    vrow[:, 14] = 1
    cst[:GT, 68:84] = vrow
    img, pos = np.arange(GT) // N, np.arange(GT) % N
    same = img[:, None] == img[None, :]
    before = same & (pos[None, :] <= pos[:, None])
    cst[:GT, 96:168] = before.T
    freq = (1.0 / f(10000.0) ** (np.arange(0, QD, 2, dtype=f) / f(QD))).astype(f)
    ang = (pos[None, :].astype(f) * np.tile(freq, 4)[:, None]).astype(f)
    cst[:, 168:240] = np.cos(ang)
    cst[:, 240:312] = np.sin(ang)
    cst[:, 312:320] = np.arange(8)
    cst[:, 320:336] = np.arange(16)
    cst[:, 336:464] = 1
    cst[:, 464] = EPS_LN
    cst[:, 465] = EPS_RMS
    cst[:HB, 466:468] = a["L1_ffn_norm1_w"].reshape(2, HB).T
    cst[:HB, 468:470] = a["L1_ffn_norm2_w"].reshape(2, HB).T
    cst[:HB, 470:474] = a["L1_attn_b_inp"][:2 * DIM].reshape(4, HB).T
    cst[:, 474:474 + NTHR] = BS * np.arange(1, NTHR + 1)
    cst[:, 480:480 + (E1 + 1) * E1] = (np.arange(E1)[None, :] < np.arange(E1 + 1)[:, None]).reshape(-1)
    d["cst"] = cst
    d["tri"] = (np.arange(GT)[:, None] < np.arange(GT)[None, :]).astype(f)
    d["oneb"] = np.ones((GT, GT)).astype(f)
    d["rw0"] = a["L0_ffn_router_w"].T.reshape(2, HB, E0).transpose(1, 0, 2)
    d["rw1"] = a["L1_ffn_w_router"].reshape(2, HB, E1).transpose(1, 0, 2)
    wgu = np.concatenate([a["L0_ffn_Wg"], a["L0_ffn_Wu"]], 1)
    d["wgu0"] = wgu.transpose(0, 2, 1).reshape(E0, 2, HB, 2 * F0).transpose(0, 2, 1, 3)
    d["wd0"] = a["L0_ffn_Wd"].transpose(0, 2, 1).reshape(E0, 6, 128, DIM).transpose(0, 2, 1, 3)
    d["wgu1"] = a["L1_ffn_w_gate_up"].reshape(E1, 2, HB, 2 * F1).transpose(0, 2, 1, 3)
    d["wd1"] = a["L1_ffn_w_down"].reshape(E1, 3, 128, DIM).transpose(0, 2, 1, 3)
    m = np.stack([np.where(same, 0, NEG), np.where(before, 0, NEG), np.where(before.T, 0, NEG)], 1)
    d["maskb"] = np.repeat(m[:, :, None, :], 4, axis=2).astype(f)
    hs = np.zeros((128, NH, GT), f)
    hs[np.arange(NH), np.arange(NH)] = 1
    d["headsel"] = hs.astype(f)
    d["bias"] = np.broadcast_to(np.stack([a["L0_attn_b_proj"], a["L1_attn_b_out"],
                                          a["L1_attn_b_inp"][2 * DIM:]])[None], (GT, 3, DIM))
    wq = a["L0_attn_w_qkv"].reshape(2, HB, 3, NH, HD)
    wA = np.zeros((2, HB, 2, NH, 32), f)
    wA[..., :HD] = wq[:, :, 0:2]
    d["wA"] = wA.reshape(2, HB, 2 * NJ * 128).transpose(1, 0, 2)
    d["wV0"] = wq[:, :, 2].reshape(2, HB, DIM).transpose(1, 0, 2)
    d["wP0"] = a["L0_attn_w_proj"].reshape(NJ, 64, DIM).transpose(1, 0, 2)
    MAXREL = 14

    def by_position(tv, th):
        t = np.zeros((N, 16, HD), f)
        t[0, 0:7] = tv[0]
        t[0, 7:12] = th[0]
        for n in range(1, N):
            rq, cq = (n - 1) // side, (n - 1) % side
            t[n, 0:7] = tv[np.clip(np.arange(7) - rq, -MAXREL, MAXREL) + MAXREL + 1]
            t[n, 7:12] = th[np.clip(np.arange(5) - cq, -MAXREL, MAXREL) + MAXREL + 1]
        t[:, 12] = tv[0]
        t[:, 13] = th[0]
        return t
    tk = by_position(a["L0_attn_tab_vk"], a["L0_attn_tab_hk"])
    tv = by_position(a["L0_attn_tab_vv"], a["L0_attn_tab_hv"])
    pk = np.zeros((4, 32, N, 4, 32), f)
    pv = np.zeros((4, 32, N, 4, HD), f)
    for r in range(4):
        pk[r, :HD, :, r, :HD] = np.eye(HD)[:, None, :]
        pk[r, :HD, :, r, HD:] = tk.transpose(2, 0, 1)
        pv[r, :HD, :, r, :] = np.eye(HD)[:, None, :]
        pv[r, HD:, :, r, :] = tv.transpose(1, 0, 2)
    w = a["L1_attn_w_inp"][0].reshape(2, HB, 3 * DIM).transpose(1, 0, 2)
    d["wC1"], d["wV1"] = w[:, :, :2 * DIM], w[:, :, 2 * DIM:]
    wf = np.zeros((6, HD, 6, HD), f)
    for i in range(6):
        wf[i, :, i, :] = a["L1_attn_omega"].T
    d["wF1"] = wf.reshape(HB, HB)
    d["wO1"] = a["L1_attn_w_out"][0].reshape(2, HB, DIM).transpose(1, 0, 2)
    w = a["L1_ffn_w_qkv"].reshape(2, HB, QH + 2 * KVH, QD // 2, 2)
    wq, wk = w[:, :, :QH], np.repeat(w[:, :, QH:QH + KVH], QH // KVH, axis=2)
    w2 = np.stack([t.reshape(2, HB, NJ, 4, 32, 2).transpose(0, 1, 2, 5, 3, 4) for t in (wq, wk)], 2)
    d["wQ2"] = w2.reshape(2, HB, 4 * NJ * 128).transpose(1, 0, 2)
    d["wV2"] = w[:, :, QH + KVH:].reshape(2, HB, KVH * QD).transpose(1, 0, 2)
    d["wO2"] = a["L1_ffn_w_out"].reshape(6, 128, DIM).transpose(1, 0, 2)
    d["posk"] = pk.reshape(128, N, 128)
    d["posv"] = pv.reshape(128, N, 64)
    return {k: np.ascontiguousarray(v) for k, v in d.items()}


def kernel(**inputs):
    import numpy as np
    import concourse.bacc as bacc
    from concourse.bass_utils import run_bass_kernel_spmd as run

    nc = bacc.Bacc("TRN2", target_bir_lowering=False, num_devices=1)
    arrays = layouts(inputs)
    ins = {k: nc.dram_tensor(f"in_{k}", v.shape, mybir.dt.from_np(v.dtype), kind="ExternalInput").ap()
           for k, v in arrays.items()}
    out = nc.dram_tensor("out_0_dram", (B, N, DIM), mybir.dt.float32, kind="ExternalOutput").ap()
    tower(nc, ins, out.rearrange("(g b) n d -> (b n) g d", g=NG))
    r = run(nc, [{f"in_{k}": v for k, v in arrays.items()}], core_ids=[0])
    return r.results[0]["out_0_dram"]
```

```python
import concourse.bass as bass
from concourse import mybir
from contextlib import ExitStack

B, CH, IMG, PATCH, DIM = 16, 3, 96, 16, 192
GRID = IMG // PATCH
N = GRID * GRID
TOK = B * N
NG = 8
GT = TOK // NG
HB = DIM // 2
NH, HD = 12, 16
NJ = 3
FP, FC = 120, 8
SH = 5
E0, F0 = 8, 768
E1, F1 = 16, 384
QH, KVH, QD = 12, 3, 64
NEG = -1e30
BS = 96
NTHR = (TOK - 1) // BS
MAXB = [(2 * TOK + (BS - 1) * e + e - 2) // BS for e in (E0, E1)]
XT_OF = {1: 0, 2: 1, 3: 2, 5: 3, 6: 4}
GUB = (0, 1, 2, 3, 6, 7)
RING = (2, 4)
ZW = 768
EPS_LN, EPS_RMS = 1e-5, 1e-6


class Chain:

    def __init__(self, eng, sem, base=0):
        self.eng, self.sem, self.n, self.base = eng, sem, 0, base

    def __call__(self, ins):
        self.n += 1
        ins.then_inc(self.sem, 1)
        self.eng.wait_ge(self.sem, self.base + self.n)


def pipelined(eng, step):
    step(0, 0, first=True)
    with eng.Fori(0, NG // 2 - 1) as n:
        step(n * 2 + 1, 1)
        step(n * 2 + 2, 0)
    step(NG - 1, 1, last=True)


PIECES = ((0, 0, 4, 0, 0), (1, 0, 2, 0, 4), (1, 2, 2, 1, 0), (2, 0, 4, 1, 2))


def tower(nc, ins, out):
    fp32, bf16, i32, u32 = mybir.dt.float32, mybir.dt.bfloat16, mybir.dt.int32, mybir.dt.uint32
    ALU, ACT = mybir.AluOpType, mybir.ActivationFunctionType
    AX = mybir.AxisListType

    ctx = ExitStack()
    with ctx:
        def sb(name, shape, dt=fp32):
            return ctx.enter_context(nc.sbuf_tensor(name, shape, dt))

        sems = {}

        def sem(name):
            if name not in sems:
                sems[name] = ctx.enter_context(nc.semaphore(name))
            return sems[name]

        PS = ctx.enter_context(nc.psum_tensor("PS", [128, 8, 512], fp32))

        ident = sb("ident", [128, 128])
        identb = sb("identb", [128, 128], bf16)
        cst = sb("cst", [128, 768])
        blk4 = cst[:, 0:4]
        blk6 = cst[0:HB, 4:10]
        cnt = cst[0:FP, 16:24]
        krows = cst[:, 32:68]
        vrows = cst[0:GT, 68:84]
        causal01 = cst[0:GT, 96:168]
        rcos = cst[:, 168:240]
        rsin = cst[:, 240:312]
        iota8 = cst[0:GT, 312:320]
        iota16 = cst[0:GT, 320:336]
        ones = cst[:, 336:464]
        eps_ln = cst[:, 464:465]
        eps_rms = cst[:, 465:466]
        w1n = cst[0:HB, 466:468]
        w2n = cst[0:HB, 468:470]
        binp = cst[0:HB, 470:474]
        thr = cst[0:GT, 474:474 + NTHR]
        before = cst[0:GT, 480:480 + (E1 + 1) * E1].rearrange("p (a b) -> p a b", b=E1)
        maskb = sb("maskb", [GT, 2, GT], bf16)
        headsel = sb("headsel", [128, NH, GT], bf16)
        h = sb("h", [GT, NG, DIM])
        y = sb("y", [GT, NG, DIM])
        xnT = sb("xnT", [128, 2, TOK])
        st6 = sb("st6", [GT, NG, 6])
        mv = sb("mv", [GT, NG, 2])
        rstd = sb("rstd", [GT, NG])
        nmr = sb("nmr", [GT, NG])
        tmpg = sb("tmpg", [GT, NG])
        bias = sb("bias", [GT, 3, DIM])
        wC1 = sb("wC1", [128, 2, 4 * HB])
        wF1 = sb("wF1", [HB, HB])
        wV1 = sb("wV1", [128, 2, DIM])
        wO1 = sb("wO1", [HB, 2, DIM])
        wQ2 = sb("wQ2", [128, 2, 4 * NJ * 128])
        wV2 = sb("wV2", [128, 2, KVH * QD])
        wO2 = sb("wO2", [128, 6, DIM])
        bxT = sb("bxT", [128, 2, BS])
        rw0 = sb("rw0", [128, 2, E0])
        rw1 = sb("rw1", [128, 2, E1])
        tri = sb("tri", [GT, GT], bf16)
        oneb = sb("oneb", [GT, GT], bf16)
        zero = sb("zero", [128, ZW])
        wgu0 = sb("wgu0", [128, RING[0], 2, 2 * F0])
        wd0 = sb("wd0", [128, RING[0], 6, DIM])
        wgu1 = wgu0[:, :, :, :].rearrange("p r k (s n) -> p (r k s n)", s=2)\
            .rearrange("p (r k n) -> p r k n", r=RING[1], k=2)
        wd1 = wd0[:, :, :, :].rearrange("p r c d -> p (r c d)").rearrange("p (r c d) -> p r c d", r=RING[1], c=3)
        xs = [nc.dram_tensor(f"xs{L}", ((MAXB[L] + 2) * BS, DIM), fp32, kind="Internal").ap() for L in range(2)]

        block = ctx.enter_context(nc.Block())

        stage_ctx = ExitStack()
        ctx.enter_context(stage_ctx)

        def stage_sb(stack, name, shape, dt=fp32):
            return stack.enter_context(nc.sbuf_tensor(name, shape, dt))

        wA = sb("wA", [128, 2, NJ * 2 * 128])
        wV0 = sb("wV0", [128, 2, DIM])
        wP0 = sb("wP0", [64, NJ, DIM])
        posk = sb("posk", [128, N, 128])
        posv = sb("posv", [128, N, 64])
        t_stack = ExitStack()
        xw = stage_sb(t_stack, "xw", [FP, FC, TOK])
        xsq = stage_sb(t_stack, "xsq", [FP, 4, TOK])
        w5 = stage_sb(t_stack, "w5", [FP, FC, SH, DIM])
        gb5 = stage_sb(t_stack, "gb5", [FP, 2, FC * SH])
        wc = stage_sb(t_stack, "wc", [FP, FC, DIM + 1])
        brow = stage_sb(t_stack, "brow", [1, 2, DIM])
        gsum = stage_sb(t_stack, "gsum", [GT, 2, DIM])
        t_stack.close()
        a_stack = ExitStack()
        qT = stage_sb(a_stack, "qT", [128, NJ, TOK])
        qa = stage_sb(a_stack, "qa", [128, NJ, TOK])
        ka = stage_sb(a_stack, "ka", [128, NJ, TOK])
        va = stage_sb(a_stack, "va", [GT, NG, NH, 32])
        oaT = stage_sb(a_stack, "oaT", [128, NJ, TOK])
        of = stage_sb(a_stack, "of", [64, NJ, TOK])
        a_q = stage_sb(a_stack, "a_q", [128, 2, NJ, GT])
        a_kz = stage_sb(a_stack, "a_kz", [128, 2, NJ, 4, GT])
        a_m = stage_sb(a_stack, "a_m", [GT, 128], bf16)
        a_mT = stage_sb(a_stack, "a_mT", [128, GT], bf16)
        a_p = stage_sb(a_stack, "a_p", [GT, NH, GT])
        a_rec = stage_sb(a_stack, "a_rec", [GT, NH])
        a_o = stage_sb(a_stack, "a_o", [GT, NH, 32])
        a_stack.close()
        l1_stack = ExitStack()
        rn = stage_sb(l1_stack, "rn", [GT, NG, DIM])
        r_stack = ExitStack()
        cT = stage_sb(r_stack, "cT", [HB, 4, TOK])
        sf = stage_sb(r_stack, "sf", [GT, NG, 2 * NH, HD])
        ssum = stage_sb(r_stack, "ssum", [GT, NG, 2 * NH])
        smax = stage_sb(r_stack, "smax", [GT, NG, 2 * NH])
        kmax = stage_sb(r_stack, "kmax", [GT, NG])
        fT = stage_sb(r_stack, "fT", [HB, 4, TOK])
        vr = stage_sb(r_stack, "vr", [GT, NG, NH, HD + 1])
        r_qz = stage_sb(r_stack, "r_qz", [HB, 2, 2, 6, GT])
        r_k = stage_sb(r_stack, "r_k", [HB, 2, 2, GT])
        r_p = stage_sb(r_stack, "r_p", [GT, 2, NH, GT])
        r_den = stage_sb(r_stack, "r_den", [GT, NH])
        r_a = stage_sb(r_stack, "r_a", [GT, NH, HD])
        r_aT = stage_sb(r_stack, "r_aT", [HB, 2, GT])
        r_stack.close()
        b_stack = ExitStack()
        rq = stage_sb(b_stack, "rq", [128, 2, NJ, TOK])
        rk = stage_sb(b_stack, "rk", [128, 2, NJ, TOK])
        vb = stage_sb(b_stack, "vb", [GT, NG, KVH, QD + 1])
        rt = stage_sb(b_stack, "rt", [128, 2, 4, 288])
        b_q = stage_sb(b_stack, "b_q", [128, 2, 2, NJ, GT])
        b_kz = stage_sb(b_stack, "b_kz", [128, 2, 2, NJ, 4, GT])
        b_m = stage_sb(b_stack, "b_m", [GT, 128], bf16)
        b_mT = stage_sb(b_stack, "b_mT", [128, GT], bf16)
        b_p = stage_sb(b_stack, "b_p", [GT, QH, GT])
        b_rec = stage_sb(b_stack, "b_rec", [GT, QH])
        b_o = stage_sb(b_stack, "b_o", [GT, QH, QD])
        b_oT = stage_sb(b_stack, "b_oT", [128, 6, GT])
        b_stack.close()
        m_stack = ExitStack()
        lg = stage_sb(m_stack, "lg", [GT, NG, E1])
        top8 = stage_sb(m_stack, "top8", [GT, NG, 8])
        idx8 = stage_sb(m_stack, "idx8", [GT, NG, 8], u32)
        idxf = stage_sb(m_stack, "idxf", [GT, NG, 2])
        sel = stage_sb(m_stack, "sel", [GT, 2, NG, E1])
        selb = stage_sb(m_stack, "selb", [GT, NG, E1], bf16)
        share = stage_sb(m_stack, "share", [GT, 2, NG])
        tot = stage_sb(m_stack, "tot", [GT, E1])
        over = stage_sb(m_stack, "over", [GT, E1, NTHR])
        nblk = stage_sb(m_stack, "nblk", [GT, E1])
        prod = stage_sb(m_stack, "prod", [GT, E1 + 1, E1])
        first = stage_sb(m_stack, "first", [GT, E1 + 1])
        firsti = stage_sb(m_stack, "firsti", [GT, E1 + 1], i32)
        slote = stage_sb(m_stack, "slote", [GT, NG, E1])
        slotf = stage_sb(m_stack, "slotf", [GT, 2, NG])
        slot = stage_sb(m_stack, "slot", [GT, 2, NG], u32)
        yg = stage_sb(m_stack, "yg", [GT, 2, NG, DIM])
        bx = stage_sb(m_stack, "bx", [BS, DIM])
        
        sg = stage_sb(m_stack, "sg", [128, 6, BS])
        hT = stage_sb(m_stack, "hT", [128, 6, BS])
        yo = stage_sb(m_stack, "yo", [BS, DIM])
        m_stack.close()
        l1_stack.close()
        WGU, WD = (wgu0, wgu1), (wd0, wd1)
        
        EX, HC = (E0, E1), (F0 // 128, F1 // 128)
        RW = (rw0, rw1)

        @block.sync
        def _(sp):
            sp.dma_start(cst[:, :], ins["cst"]).then_inc(sem("cst_in"), 16)
            for c in range(FC):
                sp.dma_start(w5[:, c, :, :], ins["w5"][:, c]).then_inc(sem(f"tok_in{c}"), 16)
                sp.dma_start(xw[:, c, :], ins["xw"][:, c]).then_inc(sem(f"tok_in{c}"), 16)
            sp.dma_start(posk[:, :, :], ins["posk"]).then_inc(sem("posk_in"), 16)
            sp.dma_start(posv[:, :, :], ins["posv"]).then_inc(sem("posv_in"), 16)
            def experts_io(L):
                p = f"m{L}_"
                sp.wait_ge(sem(p + "first"), 1)
                blocks = sp.value_load(firsti[0:1, EX[L]:EX[L] + 1], min_val=1, max_val=MAXB[L])
                sp.sem_inc(sem(p + "y_out"), 16)
                sp.wait_ge(sem(p + "sent"), 16 * 2 * NG)
                sp.dma_start(bx[:, :], xs[L][0:BS, :]).then_inc(sem(p + "x_in"), 16)
                sp.wait_ge(sem(p + "xT_ps"), 1)
                sp.dma_start(bx[:, :], xs[L][BS:2 * BS, :]).then_inc(sem(p + "x_in"), 16)
                with sp.Fori(0, blocks) as b:
                    sp.wait_ge(sem(p + "xT_ps"), b + 2)
                    sp.dma_start(bx[:, :], xs[L][bass.ds(b * BS + 2 * BS, BS), :]).then_inc(sem(p + "x_in"), 16)
                    sp.wait_ge(sem(p + "y"), b + 1)
                    sp.dma_start(xs[L][bass.ds(b * BS, BS), :], yo[:, :]).then_inc(sem(p + "y_out"), 16)
                sp.wait_ge(sem(p + "x_in"), blocks * 16 + 32)
                sp.sem_inc(sem(p + "all_out"), 1)
                sp.wait_ge(sem(p + "y_out"), blocks * 16 + 16)
                sp.sem_inc(sem(p + "all_out"), 1)

            experts_io(0)
            experts_io(1)
            sp.wait_ge(sem("h_last"), 1)
            sp.dma_start(out, h[:, :, :]).then_inc(sem("out_done"), 16)
            sp.wait_ge(sem("out_done"), 16)

        @block.gpsimd
        def _(pool):
            pool.dma_start(identb[:, :], ins["identb"]).then_inc(sem("bf_in"), 16)
            pool.dma_start(maskb[:, :, :], ins["maskb"]).then_inc(sem("bf_in"), 16)
            pool.dma_start(headsel[:, :, :], ins["headsel"]).then_inc(sem("bf_in"), 16)
            pool.dma_start(tri[:, :], ins["tri"]).then_inc(sem("bf_in"), 16)
            pool.dma_start(oneb[:, :], ins["oneb"]).then_inc(sem("bf_in"), 16)
            nc.gpsimd.memset(zero[:, :], 0.0).then_inc(sem("zero"), 1)
            pool.wait_ge(sem("zero"), 1)
            for t in (xnT, wA, wV0, rw0, rw1, bxT, wgu0, wC1, wV1, wQ2, wV2):
                nc.gpsimd.memset(t[HB:128], 0.0).then_inc(sem("pads"), 1)
            for L in range(2):
                for i in range(0, (MAXB[L] + 2) * BS * DIM, 128 * ZW):
                    n = min(128 * ZW, (MAXB[L] + 2) * BS * DIM - i) // 128
                    flat = xs[L].rearrange("a b -> (a b)")[i:i + 128 * n].rearrange("(p n) -> p n", p=128)
                    pool.dma_start(flat, zero[:, 0:n]).then_inc(sem("xs_zero"), 16)
            for r in range(RING[0]):
                pool.dma_start(wgu0[0:HB, r, :, :], ins["wgu0"][r]).then_inc(sem(f"m0_w{r}"), 16)
                pool.dma_start(wd0[:, r, :, :], ins["wd0"][r]).then_inc(sem(f"m0_w{r}"), 16)
            NZ = sum(-(-(MAXB[L] + 2) * BS * DIM // (128 * ZW)) for L in range(2))
            pool.wait_ge(sem("xs_zero"), 16 * NZ)

            def experts_dma(L):
                p = f"m{L}_"
                pool.wait_ge(sem(p + "slot"), 1)
                for k in range(2):
                    for g in range(NG):
                        nc.gpsimd.indirect_dma_start(
                            out=xs[L], out_offset=bass.IndirectOffsetOnAxis(ap=slot[:, k, g:g + 1], axis=0),
                            in_=(y, rn)[L][:, g, :], in_offset=None).then_inc(sem(p + "sent"), 16)
                R = RING[L]
                with pool.Fori(1, EX[L] // R) as q:
                    for r in range(R):
                        done = pool.value_load(firsti[0:1, bass.ds(q * R + (r - R + 1), 1)], min_val=1, max_val=MAXB[L])
                        pool.wait_ge(sem(p + "y_ps"), done)
                        pool.dma_start(WGU[L][0:HB, r, :, :], ins[f"wgu{L}"][q * R + r]).then_inc(sem(p + f"w{r}"), 16)
                        pool.dma_start(WD[L][:, r, :, :], ins[f"wd{L}"][q * R + r]).then_inc(sem(p + f"w{r}"), 16)
                pool.wait_ge(sem(p + "all_out"), 2)
                for g in range(NG):
                    for k in range(2):
                        nc.gpsimd.indirect_dma_start(
                            out=yg[:, k, g, :], out_offset=None, in_=xs[L],
                            in_offset=bass.IndirectOffsetOnAxis(ap=slot[:, k, g:g + 1], axis=0))\
                            .then_inc(sem(f"back{g}"), 16)

            experts_dma(0)
            for r in range(RING[1]):
                pool.dma_start(wgu1[0:HB, r, :, :], ins["wgu1"][r]).then_inc(sem(f"m1_w{r}"), 16)
                pool.dma_start(wd1[:, r, :, :], ins["wd1"][r]).then_inc(sem(f"m1_w{r}"), 16)
            def in_r(g, par):
                nc.gpsimd.tensor_copy(r_k[:, par, :, :], fT[:, 2:4, bass.ts(g, GT)]).then_inc(sem("r_in"), 1)
                for i in range(2):
                    nc.gpsimd.tensor_tensor(
                        r_qz[:, par, i, :, :], fT[:, i, bass.ts(g, GT)].unsqueeze(1).to_broadcast([HB, 6, GT]),
                        blk6.unsqueeze(2).to_broadcast([HB, 6, GT]), ALU.mult).then_inc(sem("r_in"), 1)

            pool.wait_ge(sem("r_fT"), 8)
            in_r(0, 0)
            in_r(1, 1)
            with pool.Fori(1, NG // 2) as n:
                for par in range(2):
                    pool.wait_ge(sem("r_qk"), n * 2 + (par - 1))
                    in_r(n * 2 + par, par)
            for n in range(4 * NJ):
                qk, j, q = n // (2 * NJ), n % (2 * NJ) // 2, n % 2
                dst = (rq, rk)[qk]
                pool.wait_ge(sem("b_rope"), n + 1)
                nc.gpsimd.tensor_tensor(dst[:, 0, j, q * 288:(q + 1) * 288], rt[:, n % 2, 0, :], rt[:, n % 2, 1, :],
                                        ALU.subtract).then_inc(sem("b_r"), 1)
                nc.gpsimd.tensor_tensor(dst[:, 1, j, q * 288:(q + 1) * 288], rt[:, n % 2, 2, :], rt[:, n % 2, 3, :],
                                        ALU.add).then_inc(sem("b_r"), 1)
            experts_dma(1)

        @block.scalar
        def _(act):
            act.dma_start(gb5[:, :, :], ins["gb5"]).then_inc(sem("gb_in"), 16)
            act.dma_start(brow[0:1, 1, :], ins["tok_b"]).then_inc(sem("gb_in"), 16)
            act.dma_start(ident[:, :], ins["ident"]).then_inc(sem("cst_in"), 16)
            act.dma_start(bias[:, :, :], ins["bias"]).then_inc(sem("cst_in"), 16)
            act.dma_start(rw0[0:HB, :, :], ins["rw0"]).then_inc(sem("rw_in"), 16)
            act.dma_start(rw1[0:HB, :, :], ins["rw1"]).then_inc(sem("rw_in"), 16)
            for name, t in (("wC1", wC1), ("wF1", wF1), ("wV1", wV1), ("wO1", wO1), ("wQ2", wQ2), ("wV2", wV2),
                            ("wO2", wO2)):
                at = (slice(0, ins[name].shape[0]),) + (slice(None),) * (len(t.shape) - 1)
                act.dma_start(t[at], ins[name]).then_inc(sem("l1_in"), 16)
            act.dma_start(wA[0:HB, :, :], ins["wA"]).then_inc(sem("wA_in"), 16)
            act.dma_start(wV0[0:HB, :, :], ins["wV0"]).then_inc(sem("wA_in"), 16)
            act.dma_start(wP0[:, :, :], ins["wP0"]).then_inc(sem("wA_in"), 16)
            for c in range(FC):
                act.wait_ge(sem(f"tok_in{c}"), 32)
                if c >= 4:
                    act.wait_ge(sem("t_used"), c - 3)
                nc.scalar.activation(xsq[:, c % 4, :], xw[:, c, :], ACT.Square).then_inc(sem("t_sq"), 1)
            act.wait_ge(sem("cst_in"), 48)
            act.wait_ge(sem("t_var"), 1)
            nc.scalar.activation(rstd[:, :], tmpg[:, :], ACT.Sqrt, bias=eps_ln[0:GT], scale=1.0)\
                .then_inc(sem("t_std"), 1)
            def std(k, eps=eps_ln):
                act.wait_ge(sem("ln_mv"), k)
                nc.scalar.activation(rstd[:, :], mv[:, :, 1], ACT.Sqrt, bias=eps[0:GT], scale=1.0)\
                    .then_inc(sem("ln_std"), 1)

            def evict_xnT(k, weight=None):
                for b in range(4):
                    act.wait_ge(sem("ln_T"), 4 * XT_OF[k] + b + 1)
                    hf, q = b // 2, b % 2
                    scale = 1.0 if weight is None else weight[:, hf:hf + 1]
                    nc.scalar.activation(xnT[0:HB, hf, q * 288:(q + 1) * 288], PS[0:HB, b, 0:288], ACT.Copy,
                                         scale=scale).then_inc(sem("xnT"), 1)
            std(1)
            evict_xnT(1)
            for j in range(NJ):
                for q in range(2):
                    act.wait_ge(sem("a_qk"), 2 * j + q + 1)
                    nc.scalar.activation(qT[:, j, q * 288:(q + 1) * 288], PS[:, 4 + (2 * j + q) % 2, 0:288],
                                         ACT.Copy, scale=HD ** -0.5).then_inc(sem("a_qT"), 1)
            for g in range(NG):
                act.wait_ge(sem("a_v"), g + 1)
                nc.scalar.activation(va[:, g, :, 0:HD],
                                     PS[0:GT, g % 2, 0:DIM].rearrange("p (h d) -> p h d", h=NH),
                                     ACT.Copy).then_inc(sem("a_va"), 1)
            for i in range(4):
                act.wait_ge(sem("a_pos"), i + 1)
                nc.scalar.activation(
                    qa[:, :, :].rearrange("p j (b n) -> p n j b", n=N)[:, 9 * i:9 * i + 9, :, :],
                    PS[:, 2 + i, 0:432].rearrange("p (n j b) -> p n j b", j=NJ, b=B), ACT.Copy)\
                    .then_inc(sem("a_qa"), 1)

            def oT_a(g):
                act.wait_ge(sem("a_oT"), g + 1)
                nc.scalar.activation(oaT[:, :, bass.ts(g, GT)],
                                     PS[:, 2, 0:3 * GT].rearrange("p (j t) -> p j t", j=NJ), ACT.Copy)\
                    .then_inc(sem("a_oaT"), 1)

            def step_a(g, par, first=False, last=False):
                act.wait_ge(sem("att_mt_ps"), g + 1)
                nc.scalar.activation(a_mT[:, :], PS[:, 4, 432:468].bitcast(bf16), ACT.Copy).then_inc(sem("att_mt"), 1)
                act.wait_ge(sem("att_s2"), g + 1)
                nc.scalar.activation(a_p[:, :, :].rearrange("p (a b) k -> p a (b k)", a=2),
                                     PS[0:GT, 3:5, 0:432], ACT.Exp).then_inc(sem("att_exp"), 1)
                if not first:
                    oT_a(g - 1)
            pipelined(act, step_a)
            oT_a(NG - 1)
            for i in range(4):
                act.wait_ge(sem("a_pos2"), i + 1)
                nc.scalar.activation(
                    of[:, :, :].rearrange("p j (b n) -> p n j b", n=N)[:, 9 * i:9 * i + 9, :, :],
                    PS[0:64, i, 0:432].rearrange("p (n j b) -> p n j b", j=NJ, b=B), ACT.Copy)\
                    .then_inc(sem("a_of"), 1)

            def experts_act(L):
                p, H = f"m{L}_", HC[L]
                act.wait_ge(sem(p + "diff"), 1)
                nc.scalar.activation(share[:, 1, :], share[:, 0, :], ACT.Exp).then_inc(sem(p + "exp"), 1)
                act.wait_ge(sem(p + "first"), 1)
                blocks = act.value_load(firsti[0:1, EX[L]:EX[L] + 1], min_val=1, max_val=MAXB[L])

                def block_T():
                    src = PS[0:HB, 4, 0:2 * BS].rearrange("p (k t) -> p k t", k=2)
                    if L == 0:
                        nc.scalar.activation(bxT[0:HB, :, :], src, ACT.Copy).then_inc(sem(p + "xT"), 2)
                    else:
                        for k in range(2):
                            nc.scalar.activation(bxT[0:HB, k, :], src[:, k, :], ACT.Copy, scale=w2n[:, k:k + 1])\
                                .then_inc(sem(p + "xT"), 1)
                act.wait_ge(sem(p + "xT_ps"), 1)
                block_T()
                with act.Fori(0, blocks) as b:
                    for c in range(H):
                        act.wait_ge(sem(p + "gu"), b * H + (c + 1))
                        nc.scalar.activation(sg[:, c, :], PS[:, GUB[c], 0:BS], ACT.Silu).then_inc(sem(p + "sg"), 1)
                    act.wait_ge(sem(p + "xT_ps"), b + 2)
                    block_T()
            std(2)
            evict_xnT(2)
            experts_act(0)
            std(3)
            evict_xnT(3)
            for m in range(4):
                for q in range(2):
                    n = 2 * m + q
                    act.wait_ge(sem("r_c"), n + 1)
                    nc.scalar.activation(cT[:, m, q * 288:(q + 1) * 288], PS[0:HB, 4 + n % 2, 0:288], ACT.Identity,
                                         bias=binp[:, m:m + 1], scale=1.0).then_inc(sem("r_cT"), 1)
            for g in range(NG):
                act.wait_ge(sem("r_s"), g + 1)
                nc.scalar.activation(sf[:, g, :, :].rearrange("p h d -> p (h d)"), PS[0:GT, g % 2, 0:2 * DIM],
                                     ACT.Copy, scale=float(HD) ** -0.25).then_inc(sem("r_sf"), 1)
            for i in range(2):
                act.wait_ge(sem("r_arg"), i + 1)
                nc.scalar.activation(sf[:, 4 * i:4 * i + 4, :, :], sf[:, 4 * i:4 * i + 4, :, :], ACT.Exp)\
                    .then_inc(sem("r_exp"), 1)
            for b in range(8):
                act.wait_ge(sem("r_fT_ps"), b + 1)
                nc.scalar.activation(fT[:, b // 2, b % 2 * 288:(b % 2 + 1) * 288], PS[0:HB, 4 + b % 2, 0:288],
                                     ACT.Copy).then_inc(sem("r_fT"), 1)
            with act.Fori(0, NG) as g:
                act.wait_ge(sem("r_aT_ps"), g + 1)
                nc.scalar.activation(r_aT[:, :, :], PS[0:HB, 3, 0:2 * GT].rearrange("p (k t) -> p k t", k=2),
                                     ACT.Copy).then_inc(sem("r_aT"), 1)
            std(4)
            std(5, eps_rms)
            evict_xnT(5, w1n)
            for g in range(NG):
                act.wait_ge(sem("b_v"), g + 1)
                nc.scalar.activation(vb[:, g, :, 0:QD], PS[0:GT, g % 2, 0:KVH * QD]
                                     .rearrange("p (h d) -> p h d", h=KVH), ACT.Copy).then_inc(sem("b_vb"), 1)

            def oT_b(g):
                act.wait_ge(sem("b_oT_ps"), g + 1)
                nc.scalar.activation(b_oT[:, :, :], PS[:, 2, 0:6 * GT].rearrange("p (c t) -> p c t", c=6), ACT.Copy)\
                    .then_inc(sem("b_oT"), 1)

            def step_b(g, par, first=False, last=False):
                act.wait_ge(sem("att_mt_ps"), g + (NG + 1))
                nc.scalar.activation(b_mT[:, :], PS[:, 4, 432:468].bitcast(bf16), ACT.Copy).then_inc(sem("att_mt"), 1)
                act.wait_ge(sem("att_s2"), g + (NG + 1))
                nc.scalar.activation(b_p[:, :, :].rearrange("p (a b) k -> p a (b k)", a=2),
                                     PS[0:GT, 3:5, 0:432], ACT.Exp, scale=float(QD) ** -0.5)\
                    .then_inc(sem("att_exp"), 1)
                if not first:
                    oT_b(g - 1)
            pipelined(act, step_b)
            oT_b(NG - 1)
            std(6, eps_rms)
            evict_xnT(6, w2n)
            experts_act(1)

        @block.vector
        def _(dve):
            tc = Chain(dve, sem("t_chain"))
            dve.wait_ge(sem("gb_in"), 32)
            for c in range(FC):
                dve.wait_ge(sem(f"tok_in{c}"), 32)
                tc(nc.vector.tensor_scalar(wc[:, c, 0:DIM], w5[:, c, 0, :], gb5[:, 0, c * SH:c * SH + 1], None,
                                           ALU.mult))
                for s in range(1, SH):
                    ins_ = nc.vector.scalar_tensor_tensor(wc[:, c, 0:DIM], w5[:, c, s, :],
                                                          gb5[:, 0, c * SH + s:c * SH + s + 1],
                                                          wc[:, c, 0:DIM], ALU.mult, ALU.add)
                    if s < SH - 1:
                        tc(ins_)
                if c == 0:
                    dve.wait_ge(sem("cst_in"), 48)
                ins_.then_inc(sem("t_wc"), 1)
                nc.vector.tensor_copy(wc[:, c, DIM:DIM + 1], cnt[:, c:c + 1]).then_inc(sem("t_wc"), 1)
            dve.wait_ge(sem("t_beta"), 1)
            nc.vector.tensor_tensor(brow[0:1, 0, :], PS[0:1, 6, 0:DIM], brow[0:1, 1, :], ALU.add)\
                .then_inc(sem("t_brow"), 1)
            dve.wait_ge(sem("t_used"), FC)
            s1 = PS[0:GT, 0:4, 0:388].rearrange("p b (q c) -> p b q c", q=2)[:, :, :, DIM]
            s2 = PS[0:GT, 0:4, 0:388].rearrange("p b (q c) -> p b q c", q=2)[:, :, :, DIM + 1]
            m4 = mv[:, :, 0].rearrange("p (b q) -> p b q", q=2)
            e4 = mv[:, :, 1].rearrange("p (b q) -> p b q", q=2)
            K = PATCH * PATCH * SH * CH
            nc.vector.tensor_scalar(m4, s1, -1.0 / K, None, ALU.mult).then_inc(sem("t_chain"), 1)
            tc.n += 1
            tc(nc.vector.tensor_scalar(e4, s2, 1.0 / K, None, ALU.mult))
            tc(nc.vector.tensor_tensor(nmr[:, :], mv[:, :, 0], mv[:, :, 0], ALU.mult))
            nc.vector.tensor_tensor(tmpg[:, :], mv[:, :, 1], nmr[:, :], ALU.subtract).then_inc(sem("t_var"), 1)
            dve.wait_ge(sem("t_std"), 1)
            tc(nc.vector.reciprocal(rstd[:, :], rstd[:, :]))
            dve.wait_ge(sem("t_gsum"), 1)
            nc.vector.tensor_copy(gsum[:, :, :], PS[0:GT, 4, 0:2 * DIM].rearrange("p (a d) -> p a d", a=2))\
                .then_inc(sem("t_chain"), 1)
            tc.n += 1
            dve.wait_ge(sem("t_chain"), tc.n)
            for g in range(NG):
                acc = PS[0:GT, g // 2, (g % 2) * 194:(g % 2) * 194 + DIM]
                tc(nc.vector.scalar_tensor_tensor(h[:, g, :], gsum[:, 0, :], mv[:, g, 0:1], acc, ALU.mult, ALU.add))
                nc.vector.scalar_tensor_tensor(h[:, g, :], h[:, g, :], rstd[:, g:g + 1], gsum[:, 1, :],
                                               ALU.mult, ALU.add).then_inc(sem("t_h"), 1)
            dve.wait_ge(sem("t_h"), NG)


            lc = Chain(dve, sem("ln_chain"))

            def ln_stats(k, src=h, rms=False):
                for g in range(NG):
                    nc.vector.bn_stats(st6[:, g, :], src[:, g, :]).then_inc(sem("ln_chain"), 1)
                lc.n += NG
                dve.wait_ge(sem("ln_chain"), lc.n)
                for g in range(NG):
                    nc.vector.bn_aggr(mv[:, g, :], st6[:, g, :]).then_inc(sem("ln_agg"), 1)
                dve.wait_ge(sem("ln_agg"), k * NG)
                if rms:
                    lc(nc.vector.tensor_tensor(nmr[:, :], mv[:, :, 0], mv[:, :, 0], ALU.mult))
                    lc(nc.vector.tensor_tensor(mv[:, :, 1], mv[:, :, 1], nmr[:, :], ALU.add))
                nc.vector.tensor_copy(tmpg[:, :], mv[:, :, 0]).then_inc(sem("ln_mv"), 1)
                dve.wait_ge(sem("ln_std"), k)
                lc(nc.vector.reciprocal(rstd[:, :], rstd[:, :]))

            def ln_apply(k, dst, name):
                for g in range(NG):
                    nc.vector.tensor_scalar(dst[:, g, :], h[:, g, :], mv[:, g, 0:1], rstd[:, g:g + 1],
                                            ALU.subtract, ALU.mult).then_inc(sem(name), 1)

            def rms_apply(src, dst, name):
                for g in range(NG):
                    nc.vector.tensor_scalar(dst[:, g, :], src[:, g, :], rstd[:, g:g + 1], None,
                                            ALU.mult).then_inc(sem(name), 1)
            ln_stats(1)
            ln_apply(1, y, "a_y")
            for j in range(NJ):
                for q in range(2):
                    dve.wait_ge(sem("a_qk"), 2 * NJ + 2 * j + q + 1)
                    nc.vector.tensor_tensor(
                        ka[:, j, q * 288:(q + 1) * 288].rearrange("p (b n) -> p b n", n=N),
                        PS[:, 4 + (2 * j + q) % 2, 0:288].rearrange("p (b n) -> p b n", n=N),
                        krows.unsqueeze(1).to_broadcast([128, 8, N]), ALU.add).then_inc(sem("a_ka"), 1)
            nc.vector.memset(a_m[:, :], 0.0).then_inc(sem("a_va1"), 1)
            dve.wait_ge(sem("a_va1"), 1)
            dve.wait_ge(sem("bf_in"), 80)
            nc.vector.tensor_copy(a_m[:, NH:NH + GT], maskb[:, 0, :]).then_inc(sem("a_va1"), 1)
            for g in range(NG):
                nc.vector.tensor_copy(va[:, g, :, HD:32], vrows.unsqueeze(1).to_broadcast([GT, NH, 16]))\
                    .then_inc(sem("a_va1"), 1)
            dve.wait_ge(sem("a_va1"), NG + 2)
            dve.wait_ge(sem("a_ka"), 2 * NJ)
            dve.wait_ge(sem("a_qa"), 4)

            def in_a(g, par):
                nc.vector.tensor_copy(a_q[:, par, :, :], qa[:, :, bass.ts(g, GT)]).then_inc(sem("a_in"), 1)
                for j in range(NJ):
                    nc.vector.tensor_tensor(
                        a_kz[:, par, j, :, :], ka[:, j, bass.ts(g, GT)].unsqueeze(1).to_broadcast([128, 4, GT]),
                        blk4.unsqueeze(2).to_broadcast([128, 4, GT]), ALU.mult).then_inc(sem("a_in"), 1)

            def max_a(g):
                dve.wait_ge(sem("att_s1"), g + 1)
                nc.vector.tensor_reduce(a_m[:, 0:NH].rearrange("p (a b) -> p a b", a=2),
                                        PS[0:GT, 0:2, 0:432].rearrange("p a (b k) -> p a b k", k=GT),
                                        AX.X, ALU.max, negate=True).then_inc(sem("att_max"), 1)

            def out_a(g):
                dve.wait_ge(sem("att_av"), g + 1)
                o3 = PS[0:GT, 7, 0:384].rearrange("p (h d) -> p h d", h=NH)
                nc.vector.reciprocal(a_rec[:, :], o3[:, :, 30]).then_inc(sem("a_rec"), 1)
                dve.wait_ge(sem("a_rec"), g + 1)
                nc.vector.tensor_tensor(a_o[:, :, :], o3, a_rec[:, :].unsqueeze(2).to_broadcast([GT, NH, 32]),
                                        ALU.mult).then_inc(sem("att_o"), 1)

            def step_a(g, par, first=False, last=False):
                if not first:
                    out_a(g - 1)
                if not last:
                    in_a(g + 1, 1 - par)
                    max_a(g + 1)
            in_a(0, 0)
            max_a(0)
            pipelined(dve, step_a)
            out_a(NG - 1)
            for g in range(NG):
                dve.wait_ge(sem("a_proj"), g + 1)
                nc.vector.tensor_tensor(y[:, g, :], PS[0:GT, 4 + g % 2, 0:DIM], bias[:, 0, :], ALU.add)\
                    .then_inc(sem("a_res"), 1)
                dve.wait_ge(sem("a_res"), 2 * g + 1)
                nc.vector.tensor_tensor(h[:, g, :], h[:, g, :], y[:, g, :], ALU.add).then_inc(sem("a_res"), 1)
            dve.wait_ge(sem("a_res"), 2 * NG)

            def route(L):
                p, E = f"m{L}_", EX[L]
                c = Chain(dve, sem(p + "chain"))
                dve.wait_ge(sem(p + "logits"), 1)
                c(nc.vector.tensor_copy(lg[:, :, 0:E], PS[0:GT, 6, 0:NG * E].rearrange("p (g e) -> p g e", g=NG)))
                for g in range(NG):
                    nc.vector.max(top8[:, g, :], lg[:, g, 0:E]).then_inc(sem(p + "chain"), 1)
                c.n += NG
                dve.wait_ge(sem(p + "chain"), c.n)
                nc.vector.tensor_tensor(share[:, 0, :], top8[:, :, 1], top8[:, :, 0], ALU.subtract)\
                    .then_inc(sem(p + "diff"), 1)
                for g in range(NG):
                    nc.vector.max_index(idx8[:, g, :], top8[:, g, :], lg[:, g, 0:E]).then_inc(sem(p + "chain"), 1)
                c.n += NG
                dve.wait_ge(sem(p + "chain"), c.n)
                c(nc.vector.tensor_copy(idxf[:, :, :], idx8[:, :, 0:2]))
                for k in range(2):
                    nc.vector.tensor_tensor(sel[:, k, :, 0:E], iota16[:, 0:E].unsqueeze(1).to_broadcast([GT, NG, E]),
                                            idxf[:, :, k:k + 1].to_broadcast([GT, NG, E]), ALU.is_equal)\
                        .then_inc(sem(p + "chain"), 1)
                c.n += 2
                dve.wait_ge(sem(p + "chain"), c.n)
                nc.vector.tensor_tensor(selb[:, :, 0:E], sel[:, 0, :, 0:E], sel[:, 1, :, 0:E], ALU.add)\
                    .then_inc(sem(p + "sel"), 1)
                dve.wait_ge(sem(p + "exp"), 1)
                c(nc.vector.tensor_scalar(share[:, 0, :], share[:, 1, :], 1.0, None, ALU.add))
                c(nc.vector.reciprocal(share[:, 0, :], share[:, 0, :]))
                c(nc.vector.tensor_tensor(share[:, 1, :], share[:, 1, :], share[:, 0, :], ALU.mult))
                dve.wait_ge(sem(p + "pos"), 1)
                c(nc.vector.tensor_copy(tot[:, 0:E], PS[0:GT, 5, 0:E]))
                c(nc.vector.tensor_tensor(over[:, 0:E, :], tot[:, 0:E].unsqueeze(2).to_broadcast([GT, E, NTHR]),
                                          thr.unsqueeze(1).to_broadcast([GT, E, NTHR]), ALU.is_gt))
                c(nc.vector.tensor_reduce(nblk[:, 0:E], over[:, 0:E, :], AX.X, ALU.add))
                c(nc.vector.tensor_scalar(nblk[:, 0:E], nblk[:, 0:E], 1.0, None, ALU.add))
                c(nc.vector.tensor_tensor(prod[:, 0:E + 1, 0:E], before[:, 0:E + 1, 0:E],
                                          nblk[:, 0:E].unsqueeze(1).to_broadcast([GT, E + 1, E]), ALU.mult))
                c(nc.vector.tensor_reduce(first[:, 0:E + 1], prod[:, 0:E + 1, 0:E], AX.X, ALU.add))
                nc.vector.tensor_copy(firsti[:, 0:E + 1], first[:, 0:E + 1]).then_inc(sem(p + "first"), 1)
                c(nc.vector.scalar_tensor_tensor(
                    slote[:, :, 0:E], first[:, 0:E].unsqueeze(1).to_broadcast([GT, NG, E]), float(BS),
                    PS[0:GT, 7, 0:NG * E].rearrange("p (g e) -> p g e", g=NG), ALU.mult, ALU.add))
                for k in range(2):
                    c(nc.vector.tensor_tensor(sel[:, k, :, 0:E], sel[:, k, :, 0:E], slote[:, :, 0:E], ALU.mult))
                    c(nc.vector.tensor_reduce(slotf[:, k, :], sel[:, k, :, 0:E], AX.X, ALU.add))
                nc.vector.tensor_copy(slot[:, :, :], slotf[:, :, :]).then_inc(sem(p + "slot"), 1)

            def experts_dve(L):
                p, H = f"m{L}_", HC[L]
                dve.wait_ge(sem(p + "first"), 1)
                blocks = dve.value_load(firsti[0:1, EX[L]:EX[L] + 1], min_val=1, max_val=MAXB[L])
                with dve.Fori(0, blocks) as b:
                    for c in range(H):
                        dve.wait_ge(sem(p + "sg"), b * H + (c + 1))
                        nc.vector.tensor_tensor(hT[:, c, :], sg[:, c, :], PS[:, GUB[c], BS:2 * BS], ALU.mult)\
                            .then_inc(sem(p + "h"), 1)
                    dve.wait_ge(sem(p + "y_ps"), b + 1)
                    dve.wait_ge(sem(p + "y_out"), b * 16 + 16)
                    nc.vector.tensor_copy(yo[:, :], PS[0:BS, 5, 0:DIM]).then_inc(sem(p + "y"), 1)
                for g in range(NG):
                    dve.wait_ge(sem(f"back{g}"), 32 * (L + 1))
                    for k in range(2):
                        nc.vector.scalar_tensor_tensor(h[:, g, :], yg[:, k, g, :], share[:, k, g:g + 1], h[:, g, :],
                                                       ALU.mult, ALU.add).then_inc(sem(p + "res"), 1)
                        dve.wait_ge(sem(p + "res"), 2 * g + k + 1)

            ln_stats(2)
            ln_apply(2, y, "m0_yn")
            route(0)
            experts_dve(0)
            ln_stats(3)
            ln_apply(3, y, "r_y")
            nc.vector.memset(vr[:, :, :, HD:HD + 1], 1.0).then_inc(sem("r_v1"), 1)
            for g in range(NG):
                dve.wait_ge(sem("r_v"), g + 1)
                nc.vector.tensor_tensor(vr[:, g, :, 0:HD],
                                        PS[0:GT, 2 + g % 2, 0:DIM].rearrange("p (h d) -> p h d", h=NH),
                                        bias[:, 2, :].rearrange("p (h d) -> p h d", h=NH), ALU.add)\
                    .then_inc(sem("r_vr"), 1)
            c = Chain(dve, sem("r_chain"))
            for i in range(2):
                gs = slice(4 * i, 4 * i + 4)
                dve.wait_ge(sem("r_sf"), 4 * i + 4)
                nc.vector.tensor_reduce(ssum[:, gs, :], sf[:, gs, :, :], AX.X, ALU.add).then_inc(sem("r_chain"), 1)
                nc.vector.tensor_reduce(smax[:, gs, 0:NH], sf[:, gs, 0:NH, :], AX.X, ALU.max)\
                    .then_inc(sem("r_chain"), 1)
                nc.vector.tensor_reduce(kmax[:, gs], sf[:, gs, NH:2 * NH, :], AX.XY, ALU.max)\
                    .then_inc(sem("r_chain"), 1)
                c.n += 3
                dve.wait_ge(sem("r_chain"), c.n)
                nc.vector.scalar_tensor_tensor(smax[:, gs, 0:NH], ssum[:, gs, 0:NH], 0.5, smax[:, gs, 0:NH],
                                               ALU.mult, ALU.add).then_inc(sem("r_chain"), 1)
                nc.vector.scalar_tensor_tensor(smax[:, gs, NH:2 * NH], ssum[:, gs, NH:2 * NH], 0.5,
                                               kmax[:, gs].unsqueeze(2).to_broadcast([GT, 4, NH]),
                                               ALU.mult, ALU.add).then_inc(sem("r_chain"), 1)
                c.n += 2
                dve.wait_ge(sem("r_chain"), c.n)
                nc.vector.tensor_tensor(sf[:, gs, :, :], sf[:, gs, :, :],
                                        smax[:, gs, :].unsqueeze(3).to_broadcast([GT, 4, 2 * NH, HD]), ALU.subtract)\
                    .then_inc(sem("r_arg"), 1)
            for i in range(2):
                gs = slice(4 * i, 4 * i + 4)
                dve.wait_ge(sem("r_exp"), i + 1)
                nc.vector.tensor_scalar(sf[:, gs, :, :], sf[:, gs, :, :], 1e-6, float(HD) ** -0.5, ALU.add, ALU.mult)\
                    .then_inc(sem("r_f"), 1)
            nc.vector.tensor_tensor(h[:, :, :], h[:, :, :], bias[:, 1:2, :].to_broadcast([GT, NG, DIM]), ALU.add)\
                .then_inc(sem("r_h"), 1)
            dve.wait_ge(sem("r_h"), 1)

            def mask_r(g, par):
                dve.wait_ge(sem("r_qk"), g + 1)
                nc.vector.tensor_tensor(r_p[:, par, :, :].rearrange("p (a b) t -> p a b t", a=2),
                                        PS[0:GT, 0:2, 0:432].rearrange("p a (b t) -> p a b t", b=6),
                                        causal01.unsqueeze(1).unsqueeze(1).to_broadcast([GT, 2, 6, GT]), ALU.mult)\
                    .then_inc(sem("r_p"), 1)

            def out_r(g):
                dve.wait_ge(sem("r_av"), g + 1)
                c = Chain(dve, sem("r_chain2"), g * 2)
                o3 = PS[0:GT, 2, 0:NH * (HD + 1)].rearrange("p (h d) -> p h d", h=NH)
                c(nc.vector.tensor_scalar(r_den[:, :], o3[:, :, HD], 1e-6, None, ALU.add))
                c(nc.vector.reciprocal(r_den[:, :], r_den[:, :]))
                nc.vector.tensor_tensor(r_a[:, :, :], o3[:, :, 0:HD],
                                        r_den[:, :].unsqueeze(2).to_broadcast([GT, NH, HD]), ALU.mult)\
                    .then_inc(sem("r_a"), 1)

            def res_r(g):
                dve.wait_ge(sem("r_proj"), g + 1)
                nc.vector.tensor_tensor(h[:, bass.ds(g, 1), :], h[:, bass.ds(g, 1), :],
                                        PS[0:GT, 4:5, 0:DIM], ALU.add).then_inc(sem("r_h"), 1)

            def step_r(g, par, first=False, last=False):
                if not first:
                    out_r(g - 1)
                if not last:
                    mask_r(g + 1, 1 - par)
                if not first:
                    res_r(g - 1)
            mask_r(0, 0)
            pipelined(dve, step_r)
            out_r(NG - 1)
            res_r(NG - 1)
            dve.wait_ge(sem("r_h"), NG + 1)
            ln_stats(4)
            ln_apply(4, y, "b_y")
            dve.wait_ge(sem("b_y"), NG)
            ln_stats(5, y, True)
            rms_apply(y, rn, "b_rn")
            nc.vector.memset(vb[:, :, :, QD:QD + 1], 1.0).then_inc(sem("b_v1"), 1)
            nc.vector.memset(b_m[:, :], 0.0).then_inc(sem("b_v1"), 1)
            dve.wait_ge(sem("b_v1"), 2)
            nc.vector.tensor_copy(b_m[:, QH:QH + GT], maskb[:, 1, :]).then_inc(sem("b_v1"), 1)
            cs = [t[:, 0:N].unsqueeze(1).to_broadcast([128, 8, N]) for t in (rcos, rsin)]
            for n in range(4 * NJ):
                dve.wait_ge(sem("b_qk"), n + 1)
                if n >= 2:
                    dve.wait_ge(sem("b_r"), 2 * (n - 1))
                for i, (eo, t) in enumerate(((0, 0), (1, 1), (0, 1), (1, 0))):
                    last = nc.vector.tensor_tensor(
                        rt[:, n % 2, i, :].rearrange("p (b n) -> p b n", n=N),
                        PS[:, 4 + 2 * (n % 2) + eo, 0:288].rearrange("p (b n) -> p b n", n=N), cs[t], ALU.mult)
                last.then_inc(sem("b_rope"), 1)
            dve.wait_ge(sem("b_r"), 8 * NJ)
            dve.wait_ge(sem("b_v1"), 3)

            def in_b(g, par):
                for eo in range(2):
                    nc.vector.tensor_copy(b_q[:, par, eo, :, :], rq[:, eo, :, bass.ts(g, GT)])\
                        .then_inc(sem("b_in"), 1)
                for eo in range(2):
                    for j in range(NJ):
                        nc.vector.tensor_tensor(
                            b_kz[:, par, eo, j, :, :],
                            rk[:, eo, j, bass.ts(g, GT)].unsqueeze(1).to_broadcast([128, 4, GT]),
                            blk4.unsqueeze(2).to_broadcast([128, 4, GT]), ALU.mult).then_inc(sem("b_in"), 1)

            def max_b(g):
                dve.wait_ge(sem("att_s1"), g + (NG + 1))
                nc.vector.tensor_reduce(b_m[:, 0:QH].rearrange("p (a b) -> p a b", a=2),
                                        PS[0:GT, 0:2, 0:432].rearrange("p a (b k) -> p a b k", k=GT),
                                        AX.X, ALU.max, negate=True).then_inc(sem("att_max"), 1)

            def out_b(g):
                dve.wait_ge(sem("att_av"), g + (NG + 1))
                o4 = PS[0:GT, 6:8, 0:390].rearrange("p a (h d) -> p a h d", h=6)
                nc.vector.reciprocal(b_rec[:, :].rearrange("p (a h) -> p a h", a=2), o4[:, :, :, QD])\
                    .then_inc(sem("b_rec"), 1)
                dve.wait_ge(sem("b_rec"), g + 1)
                nc.vector.tensor_tensor(b_o[:, :, :].rearrange("p (a h) d -> p a h d", a=2), o4[:, :, :, 0:QD],
                                        b_rec[:, :].rearrange("p (a h) -> p a h", a=2).unsqueeze(3)
                                        .to_broadcast([GT, 2, 6, QD]), ALU.mult).then_inc(sem("att_o"), 1)

            def res_b(g):
                dve.wait_ge(sem("b_proj"), g + 1)
                nc.vector.tensor_tensor(y[:, bass.ds(g, 1), :], y[:, bass.ds(g, 1), :], PS[0:GT, 5:6, 0:DIM],
                                        ALU.add).then_inc(sem("b_hin"), 1)

            def step_b(g, par, first=False, last=False):
                if not first:
                    out_b(g - 1)
                if not last:
                    in_b(g + 1, 1 - par)
                    max_b(g + 1)
                if not first:
                    res_b(g - 1)
            in_b(0, 0)
            max_b(0)
            pipelined(dve, step_b)
            out_b(NG - 1)
            res_b(NG - 1)
            dve.wait_ge(sem("b_hin"), NG)
            ln_stats(6, y, True)
            rms_apply(y, rn, "m1_yn")
            for g in range(NG):
                nc.vector.tensor_tensor(h[:, g, :], h[:, g, :], y[:, g, :], ALU.add).then_inc(sem("b_h"), 1)
            dve.wait_ge(sem("b_h"), NG)
            route(1)
            experts_dve(1)
            nc.vector.tensor_copy(tmpg[:, :], rstd[:, :]).then_inc(sem("h_last"), 1)

        @block.tensor
        def _(pe):
            mm = nc.tensor.matmul
            pe.wait_ge(sem("gb_in"), 32)
            for c in range(FC):
                pe.wait_ge(sem(f"tok_in{c}"), 32)
                for s in range(SH):
                    last = mm(PS[0:1, 6, 0:DIM], gb5[:, 1, c * SH + s:c * SH + s + 1], w5[:, c, s, :],
                              start=(c == 0 and s == 0), stop=(c == FC - 1 and s == SH - 1))
                if c == FC - 1:
                    last.then_inc(sem("t_beta"), 1)
                pe.wait_ge(sem("t_wc"), 2 * c + 2)
                pe.wait_ge(sem("t_sq"), c + 1)
                for g in range(NG):
                    o = (g % 2) * 194
                    mm(PS[0:GT, g // 2, o:o + DIM + 1], xw[:, c, bass.ts(g, GT)], wc[:, c, :],
                       start=(c == 0 and g % 2 == 0), stop=(c == FC - 1), skip_group_check=True)
                    last = mm(PS[0:GT, g // 2, o + DIM + 1:o + DIM + 2], xsq[:, c % 4, bass.ts(g, GT)],
                              wc[:, c, DIM:DIM + 1], start=False, stop=(c == FC - 1), skip_group_check=True)
                last.then_inc(sem("t_used"), 1)
            for c in range(FC):
                mm(PS[0:GT, 4, 0:DIM], ones[0:FP, 0:GT], wc[:, c, 0:DIM], start=(c == 0), stop=(c == FC - 1))
            pe.wait_ge(sem("t_brow"), 1)
            mm(PS[0:GT, 4, DIM:2 * DIM], ones[0:1, 0:GT], brow[0:1, 0, :], start=True, stop=True)\
                .then_inc(sem("t_gsum"), 1)

            def transpose_xn(k, name, src=y):
                for b in range(4):
                    hf, q = b // 2, b % 2
                    for i in range(4):
                        g = 4 * q + i
                        pe.wait_ge(sem(name), g + 1)
                        last = nc.tensor.transpose(PS[0:HB, b, i * GT:(i + 1) * GT],
                                                   src[:, g, hf * HB:(hf + 1) * HB], ident[0:GT, 0:GT])
                    last.then_inc(sem("ln_T"), 1)

            transpose_xn(1, "a_y")
            pe.wait_ge(sem("pads"), 11)
            pe.wait_ge(sem("wA_in"), 48)
            pe.wait_ge(sem("xnT"), 4)
            for j in range(2 * NJ):
                for q in range(2):
                    n = 2 * j + q
                    if n >= 2:
                        if n - 2 < 2 * NJ:
                            pe.wait_ge(sem("a_qT"), n - 1)
                        else:
                            pe.wait_ge(sem("a_ka"), n - 1 - 2 * NJ)
                    for k in range(2):
                        last = mm(PS[:, 4 + n % 2, 0:288], wA[:, k, j * 128:(j + 1) * 128],
                                  xnT[:, k, q * 288:(q + 1) * 288], start=(k == 0), stop=(k == 1))
                    last.then_inc(sem("a_qk"), 1)
            for g in range(NG):
                if g >= 2:
                    pe.wait_ge(sem("a_va"), g - 1)
                for k in range(2):
                    last = mm(PS[0:GT, g % 2, 0:DIM], xnT[:, k, bass.ts(g, GT)], wV0[:, k, :],
                              start=(k == 0), stop=(k == 1))
                last.then_inc(sem("a_v"), 1)
            pe.wait_ge(sem("posk_in"), 16)
            pe.wait_ge(sem("bf_in"), 80)
            pe.wait_ge(sem("a_qT"), 2 * NJ)
            pe.wait_ge(sem("a_ka"), 2 * NJ)
            qn = qT[:, :, :].rearrange("p j (b n) -> p n j b", n=N)
            for n in range(N):
                i = n % 9
                last = mm(PS[:, 2 + n // 9, i * 48:(i + 1) * 48].rearrange("p (j b) -> p j b", j=NJ),
                          posk[:, n, :], qn[:, n, :, :], start=True, stop=True)
                if i == 8:
                    last.then_inc(sem("a_pos"), 1)
            pe.wait_ge(sem("a_qa"), 4)

            def s1_a(g, par):
                pe.wait_ge(sem("a_in"), 4 * g + 4)
                for a in range(2):
                    mm(PS[0:GT, a, 0:432], identb[0:GT, 0:GT], maskb[:, 0:1, :].to_broadcast([GT, 6, GT]),
                       start=True, stop=False, skip_group_check=True)
                for j, r, n, a, at in PIECES:
                    last = mm(PS[0:GT, a, at * GT:(at + n) * GT], a_q[:, par, j, :], a_kz[:, par, j, r:r + n, :],
                              start=False, stop=True, skip_group_check=True)
                last.then_inc(sem("att_s1"), 1)

            def maxT(m):
                nc.tensor.transpose(PS[:, 4, 432:468].bitcast(bf16), m[:, :], identb[0:GT, 0:GT])\
                    .then_inc(sem("att_mt_ps"), 1)

            def oT_a(g):
                pe.wait_ge(sem("att_o"), g + 1)
                for j in range(NJ):
                    last = nc.tensor.transpose(PS[:, 2, j * GT:(j + 1) * GT],
                                               a_o[:, 4 * j:4 * j + 4, :], ident[0:GT, 0:GT])
                last.then_inc(sem("a_oT"), 1)

            def step_a(g, par, first=False, last=False):
                pe.wait_ge(sem("att_max"), g + 1)
                maxT(a_m)
                for hh in range(NH):
                    if hh == NH // 2:
                        pe.wait_ge(sem("att_mt"), g + 1)
                    mm(PS[0:GT, 3 + hh // 6, hh % 6 * GT:(hh % 6 + 1) * GT], a_kz[:, par, hh // 4, hh % 4, :],
                       a_q[:, par, hh // 4, :], start=(hh % 6 == 0), stop=False, skip_group_check=True)
                for hh in range(NH):
                    ins_ = mm(PS[0:GT, 3 + hh // 6, hh % 6 * GT:(hh % 6 + 1) * GT], headsel[:, hh, :], a_mT[:, :],
                              start=False, stop=True, skip_group_check=True)
                ins_.then_inc(sem("att_s2"), 1)
                if not first:
                    oT_a(g - 1)
                if not last:
                    s1_a(g + 1, 1 - par)
                pe.wait_ge(sem("att_exp"), g + 1)
                for hh in range(NH):
                    ins_ = mm(PS[0:GT, 7, hh * 32:(hh + 1) * 32], a_p[:, hh, :],
                              va[:, bass.ds(g, 1), hh, :], start=True, stop=True)
                ins_.then_inc(sem("att_av"), 1)
            s1_a(0, 0)
            pipelined(pe, step_a)
            pe.wait_ge(sem("a_oaT"), NG - 1)
            oT_a(NG - 1)
            pe.wait_ge(sem("a_oaT"), NG)
            pe.wait_ge(sem("posv_in"), 16)
            on = oaT[:, :, :].rearrange("p j (b n) -> p n j b", n=N)
            for n in range(N):
                i = n % 9
                last = mm(PS[0:64, n // 9, i * 48:(i + 1) * 48].rearrange("p (j b) -> p j b", j=NJ),
                          posv[:, n, :], on[:, n, :, :], start=True, stop=True)
                if i == 8:
                    last.then_inc(sem("a_pos2"), 1)
            pe.wait_ge(sem("a_of"), 4)
            for g in range(NG):
                if g >= 2:
                    pe.wait_ge(sem("a_res"), 2 * g - 3)
                for j in range(NJ):
                    last = mm(PS[0:GT, 4 + g % 2, 0:DIM], of[:, j, bass.ts(g, GT)], wP0[:, j, :],
                              start=(j == 0), stop=(j == NJ - 1))
                last.then_inc(sem("a_proj"), 1)


            def route_pe(L):
                p, E = f"m{L}_", EX[L]
                pe.wait_ge(sem("rw_in"), 32)
                for g in range(NG):
                    for k in range(2):
                        last = mm(PS[0:GT, 6, g * E:(g + 1) * E], xnT[:, k, bass.ts(g, GT)], RW[L][:, k, :],
                                  start=(k == 0), stop=(k == 1))
                last.then_inc(sem(p + "logits"), 1)
                pe.wait_ge(sem(p + "sel"), 1)
                mm(PS[0:GT, 7, 0:NG * E], tri[:, :], selb[:, :, 0:E], start=True, stop=False,
                   skip_group_check=True)
                for g in range(NG - 1):
                    mm(PS[0:GT, 7, (g + 1) * E:NG * E], oneb[:, :],
                       selb[:, g:g + 1, 0:E].to_broadcast([GT, NG - 1 - g, E]), start=False, stop=(g == NG - 2),
                       skip_group_check=True)
                for g in range(NG):
                    last = mm(PS[0:GT, 5, 0:E], oneb[:, :], selb[:, g, 0:E], start=(g == 0), stop=(g == NG - 1))
                last.then_inc(sem(p + "pos"), 1)

            def experts_pe(L):
                p, H = f"m{L}_", HC[L]
                pe.wait_ge(sem(p + "first"), 1)

                def block_T():
                    for k in range(2):
                        last = nc.tensor.transpose(PS[0:HB, 4, k * BS:(k + 1) * BS], bx[:, k * HB:(k + 1) * HB],
                                                   ident[0:BS, 0:BS])
                    last.then_inc(sem(p + "xT_ps"), 1)
                pe.wait_ge(sem(p + "x_in"), 16)
                block_T()
                R = RING[L]
                with pe.Fori(0, EX[L] // R) as q:
                    hi = pe.value_load(firsti[0:1, bass.ds(q * R, 1)], min_val=0, max_val=MAXB[L])
                    for r in range(R):
                        lo = hi
                        hi = pe.value_load(firsti[0:1, bass.ds(q * R + (r + 1), 1)], min_val=1, max_val=MAXB[L])
                        with pe.Fori(lo, hi) as b:
                            pe.wait_ge(sem(p + f"w{r}"), q * 32 + 32)
                            pe.wait_ge(sem(p + "xT"), b * 2 + 2)
                            for c in range(H):
                                for u in range(2):
                                    o = (u * H + c) * 128
                                    for k in range(2):
                                        last = mm(PS[:, GUB[c], u * BS:(u + 1) * BS],
                                                  WGU[L][:, r, k, o:o + 128], bxT[:, k, :],
                                                  start=(k == 0), stop=(k == 1))
                                last.then_inc(sem(p + "gu"), 1)
                            pe.wait_ge(sem(p + "x_in"), b * 16 + 32)
                            block_T()
                            for c in range(H):
                                pe.wait_ge(sem(p + "h"), b * H + (c + 1))
                                last = mm(PS[0:BS, 5, 0:DIM], hT[:, c, :], WD[L][:, r, c, :],
                                          start=(c == 0), stop=(c == H - 1))
                            last.then_inc(sem(p + "y_ps"), 1)

            transpose_xn(2, "m0_yn")
            pe.wait_ge(sem("xnT"), 8)
            route_pe(0)
            experts_pe(0)
            pe.wait_ge(sem("l1_in"), 16 * 7)

            transpose_xn(3, "r_y")
            pe.wait_ge(sem("xnT"), 12)
            for m in range(4):
                for q in range(2):
                    n = 2 * m + q
                    if n >= 2:
                        pe.wait_ge(sem("r_cT"), n - 1)
                    for k in range(2):
                        last = mm(PS[0:HB, 4 + n % 2, 0:288], wC1[:, k, m * HB:(m + 1) * HB],
                                  xnT[:, k, q * 288:(q + 1) * 288], start=(k == 0), stop=(k == 1))
                    last.then_inc(sem("r_c"), 1)
            for g in range(NG):
                if g >= 2:
                    pe.wait_ge(sem("r_vr"), g - 1)
                for k in range(2):
                    last = mm(PS[0:GT, 2 + g % 2, 0:DIM], xnT[:, k, bass.ts(g, GT)], wV1[:, k, :],
                              start=(k == 0), stop=(k == 1))
                last.then_inc(sem("r_v"), 1)
            pe.wait_ge(sem("r_cT"), 8)
            for g in range(NG):
                if g >= 2:
                    pe.wait_ge(sem("r_sf"), g - 1)
                for m in range(4):
                    last = mm(PS[0:GT, g % 2, m * HB:(m + 1) * HB], cT[:, m, bass.ts(g, GT)], wF1[:, :],
                              start=True, stop=True)
                last.then_inc(sem("r_s"), 1)
            for b in range(8):
                m, q = b // 2, b % 2
                pe.wait_ge(sem("r_f"), q + 1)
                if b >= 2:
                    pe.wait_ge(sem("r_fT"), b - 1)
                for i in range(4):
                    last = nc.tensor.transpose(PS[0:HB, 4 + b % 2, i * GT:(i + 1) * GT],
                                               sf[:, 4 * q + i, 6 * m:6 * m + 6, :], ident[0:GT, 0:GT])
                last.then_inc(sem("r_fT_ps"), 1)
            pe.wait_ge(sem("r_v1"), 1)

            def qk_r(g, par):
                pe.wait_ge(sem("r_in"), 3 * g + 3)
                for i in range(2):
                    last = mm(PS[0:GT, i, 0:432], r_k[:, par, i, :], r_qz[:, par, i, :, :], start=True, stop=True)
                last.then_inc(sem("r_qk"), 1)

            def aT_r(g):
                pe.wait_ge(sem("r_a"), g + 1)
                for i in range(2):
                    last = nc.tensor.transpose(PS[0:HB, 3, i * GT:(i + 1) * GT], r_a[:, 6 * i:6 * i + 6, :],
                                               ident[0:GT, 0:GT])
                last.then_inc(sem("r_aT_ps"), 1)

            def proj_r(g):
                pe.wait_ge(sem("r_aT"), g + 1)
                for i in range(2):
                    last = mm(PS[0:GT, 4, 0:DIM], r_aT[:, i, :], wO1[:, i, :], start=(i == 0), stop=(i == 1))
                last.then_inc(sem("r_proj"), 1)

            def step_r(g, par, first=False, last=False):
                pe.wait_ge(sem("r_p"), g + 1)
                if not last:
                    qk_r(g + 1, 1 - par)
                if not first:
                    aT_r(g - 1)
                for hh in range(NH):
                    ins_ = mm(PS[0:GT, 2, hh * (HD + 1):(hh + 1) * (HD + 1)], r_p[:, par, hh, :],
                              vr[:, bass.ds(g, 1), hh, :], start=True, stop=True)
                ins_.then_inc(sem("r_av"), 1)
                if not first:
                    proj_r(g - 1)
            qk_r(0, 0)
            pipelined(pe, step_r)
            aT_r(NG - 1)
            proj_r(NG - 1)

            transpose_xn(5, "b_rn", rn)
            pe.wait_ge(sem("xnT"), 16)
            for g in range(NG):
                if g >= 2:
                    pe.wait_ge(sem("b_vb"), g - 1)
                for k in range(2):
                    last = mm(PS[0:GT, g % 2, 0:KVH * QD], xnT[:, k, bass.ts(g, GT)], wV2[:, k, :],
                              start=(k == 0), stop=(k == 1))
                last.then_inc(sem("b_v"), 1)
            for n in range(4 * NJ):
                qk, j, q = n // (2 * NJ), n % (2 * NJ) // 2, n % 2
                if n >= 2:
                    pe.wait_ge(sem("b_rope"), n - 1)
                for eo in range(2):
                    o = ((qk * NJ + j) * 2 + eo) * 128
                    for k in range(2):
                        last = mm(PS[:, 4 + 2 * (n % 2) + eo, 0:288], wQ2[:, k, o:o + 128],
                                  xnT[:, k, q * 288:(q + 1) * 288], start=(k == 0), stop=(k == 1))
                last.then_inc(sem("b_qk"), 1)
            pe.wait_ge(sem("b_vb"), NG)

            def s1_b(g, par):
                pe.wait_ge(sem("b_in"), 8 * g + 8)
                for a in range(2):
                    mm(PS[0:GT, a, 0:432], identb[0:GT, 0:GT], maskb[:, 1:2, :].to_broadcast([GT, 6, GT]),
                       start=True, stop=False, skip_group_check=True)
                for j, r, n, a, at in PIECES:
                    for eo in range(2):
                        last = mm(PS[0:GT, a, at * GT:(at + n) * GT], b_q[:, par, eo, j, :],
                                  b_kz[:, par, eo, j, r:r + n, :], start=False, stop=(eo == 1),
                                  skip_group_check=True)
                last.then_inc(sem("att_s1"), 1)

            def oT_b(g):
                pe.wait_ge(sem("att_o"), g + (NG + 1))
                for c in range(6):
                    last = nc.tensor.transpose(PS[:, 2, c * GT:(c + 1) * GT], b_o[:, 2 * c:2 * c + 2, :],
                                               ident[0:GT, 0:GT])
                last.then_inc(sem("b_oT_ps"), 1)

            def proj_b(g):
                pe.wait_ge(sem("b_oT"), g + 1)
                for c in range(6):
                    last = mm(PS[0:GT, 5, 0:DIM], b_oT[:, c, :], wO2[:, c, :], start=(c == 0), stop=(c == 5))
                last.then_inc(sem("b_proj"), 1)

            def step_b(g, par, first=False, last=False):
                pe.wait_ge(sem("att_max"), g + (NG + 1))
                maxT(b_m)
                for hh in range(QH):
                    if hh == QH // 2:
                        pe.wait_ge(sem("att_mt"), g + (NG + 1))
                    for eo in range(2):
                        mm(PS[0:GT, 3 + hh // 6, hh % 6 * GT:(hh % 6 + 1) * GT],
                           b_kz[:, par, eo, hh // 4, hh % 4, :], b_q[:, par, eo, hh // 4, :],
                           start=(hh % 6 == 0 and eo == 0), stop=False, skip_group_check=True)
                for hh in range(QH):
                    ins_ = mm(PS[0:GT, 3 + hh // 6, hh % 6 * GT:(hh % 6 + 1) * GT], headsel[:, hh, :], b_mT[:, :],
                              start=False, stop=True, skip_group_check=True)
                ins_.then_inc(sem("att_s2"), 1)
                if not first:
                    oT_b(g - 1)
                if not last:
                    s1_b(g + 1, 1 - par)
                pe.wait_ge(sem("att_exp"), g + (NG + 1))
                for hh in range(QH):
                    ins_ = mm(PS[0:GT, 6 + hh // 6, hh % 6 * (QD + 1):(hh % 6 + 1) * (QD + 1)], b_p[:, hh, :],
                              vb[:, bass.ds(g, 1), hh // 4, :], start=True, stop=True)
                ins_.then_inc(sem("att_av"), 1)
                if not first:
                    proj_b(g - 1)
            s1_b(0, 0)
            pipelined(pe, step_b)
            oT_b(NG - 1)
            proj_b(NG - 1)
            transpose_xn(6, "m1_yn", rn)
            pe.wait_ge(sem("xnT"), 20)
            route_pe(1)
            experts_pe(1)


def layouts(inputs):
    import numpy as np
    f = np.float32
    a = {k: np.asarray(v) for k, v in inputs.items()}
    d = {}
    feats = [(u, v, c) for u in range(18) for v in range(18) if not (u in (0, 17) and v in (0, 17)) for c in range(CH)]
    pad = np.zeros((B, CH, IMG + 2, IMG + 2), f)
    pad[:, :, 1:-1, 1:-1] = a["x"]
    fu, fv, fc = (np.array(t) for t in zip(*feats))
    at = PATCH * np.arange(GRID)
    win = pad[:, fc[:, None, None], fu[:, None, None] + at[None, :, None], fv[:, None, None] + at[None, None, :]]
    d["xw"] = win.transpose(1, 0, 2, 3).reshape(FC, FP, TOK).transpose(1, 0, 2)
    shifts = [(1, 1), (1, 0), (1, 2), (0, 1), (2, 1)]
    w5 = np.zeros((FC * FP, SH, DIM), f)
    gb = np.zeros((2, FC * FP, SH), f)
    count = np.zeros(FC * FP, f)
    for s, (du, dv) in enumerate(shifts):
        i, j = fu - du, fv - dv
        ok = (i >= 0) & (i < PATCH) & (j >= 0) & (j < PATCH)
        row = ((i * PATCH + j) * SH * CH + s * CH + fc)[ok]
        w5[ok, s] = a["L0_tok_w"][row]
        gb[0, ok, s] = a["L0_tok_ln_gamma"][row]
        gb[1, ok, s] = a["L0_tok_ln_beta"][row]
        count[ok] += 1
    d["w5"] = w5.reshape(FC, FP, SH, DIM).transpose(1, 0, 2, 3)
    d["gb5"] = gb.reshape(2, FC, FP, SH).transpose(2, 0, 1, 3).reshape(FP, 2, FC * SH)
    d["tok_b"] = a["L0_tok_b"][None, :]
    d["ident"] = np.eye(128, dtype=f)
    d["identb"] = np.eye(128).astype(f)
    cst = np.zeros((128, 768), f)
    cst[:, 0:4] = np.arange(128)[:, None] // 32 == np.arange(4)
    cst[:HB, 4:10] = np.arange(HB)[:, None] // 16 == np.arange(6)
    cst[:FP, 16:24] = count.reshape(FC, FP).T
    L = N - 1
    side = int(L ** 0.5)
    r_ = np.arange(L)
    krow = np.zeros((16, N), f)
    krow[0:7, 1:] = r_ // side == np.arange(7)[:, None]
    krow[7:12, 1:] = r_ % side == np.arange(5)[:, None]
    krow[12:14, 0] = 1
    for r in range(4):
        cst[32 * r + 16:32 * r + 32, 32:68] = krow
    vrow = np.concatenate([krow, krow], axis=1).T.copy()
    vrow[:, 14] = 1
    cst[:GT, 68:84] = vrow
    img, pos = np.arange(GT) // N, np.arange(GT) % N
    same = img[:, None] == img[None, :]
    before = same & (pos[None, :] <= pos[:, None])
    cst[:GT, 96:168] = before.T
    freq = (1.0 / f(10000.0) ** (np.arange(0, QD, 2, dtype=f) / f(QD))).astype(f)
    ang = (pos[None, :].astype(f) * np.tile(freq, 4)[:, None]).astype(f)
    cst[:, 168:240] = np.cos(ang)
    cst[:, 240:312] = np.sin(ang)
    cst[:, 312:320] = np.arange(8)
    cst[:, 320:336] = np.arange(16)
    cst[:, 336:464] = 1
    cst[:, 464] = EPS_LN
    cst[:, 465] = EPS_RMS
    cst[:HB, 466:468] = a["L1_ffn_norm1_w"].reshape(2, HB).T
    cst[:HB, 468:470] = a["L1_ffn_norm2_w"].reshape(2, HB).T
    cst[:HB, 470:474] = a["L1_attn_b_inp"][:2 * DIM].reshape(4, HB).T
    cst[:, 474:474 + NTHR] = BS * np.arange(1, NTHR + 1)
    cst[:, 480:480 + (E1 + 1) * E1] = (np.arange(E1)[None, :] < np.arange(E1 + 1)[:, None]).reshape(-1)
    d["cst"] = cst
    d["tri"] = (np.arange(GT)[:, None] < np.arange(GT)[None, :]).astype(f)
    d["oneb"] = np.ones((GT, GT)).astype(f)
    d["rw0"] = a["L0_ffn_router_w"].T.reshape(2, HB, E0).transpose(1, 0, 2)
    d["rw1"] = a["L1_ffn_w_router"].reshape(2, HB, E1).transpose(1, 0, 2)
    wgu = np.concatenate([a["L0_ffn_Wg"], a["L0_ffn_Wu"]], 1)
    d["wgu0"] = wgu.transpose(0, 2, 1).reshape(E0, 2, HB, 2 * F0).transpose(0, 2, 1, 3)
    d["wd0"] = a["L0_ffn_Wd"].transpose(0, 2, 1).reshape(E0, 6, 128, DIM).transpose(0, 2, 1, 3)
    d["wgu1"] = a["L1_ffn_w_gate_up"].reshape(E1, 2, HB, 2 * F1).transpose(0, 2, 1, 3)
    d["wd1"] = a["L1_ffn_w_down"].reshape(E1, 3, 128, DIM).transpose(0, 2, 1, 3)
    d["maskb"] = np.stack([np.where(same, 0, NEG), np.where(before, 0, NEG)], 1).astype(f)
    hs = np.zeros((128, NH, GT), f)
    hs[np.arange(NH), np.arange(NH)] = 1
    for k in range(GT):
        hs[NH + k, :, k] = 1
    d["headsel"] = hs.astype(f)
    d["bias"] = np.broadcast_to(np.stack([a["L0_attn_b_proj"], a["L1_attn_b_out"],
                                          a["L1_attn_b_inp"][2 * DIM:]])[None], (GT, 3, DIM))
    wq = a["L0_attn_w_qkv"].reshape(2, HB, 3, NH, HD)
    wA = np.zeros((2, HB, 2, NH, 32), f)
    wA[..., :HD] = wq[:, :, 0:2]
    d["wA"] = wA.reshape(2, HB, 2 * NJ * 128).transpose(1, 0, 2)
    d["wV0"] = wq[:, :, 2].reshape(2, HB, DIM).transpose(1, 0, 2)
    d["wP0"] = a["L0_attn_w_proj"].reshape(NJ, 64, DIM).transpose(1, 0, 2)
    MAXREL = 14

    def by_position(tv, th):
        t = np.zeros((N, 16, HD), f)
        t[0, 0:7] = tv[0]
        t[0, 7:12] = th[0]
        for n in range(1, N):
            rq, cq = (n - 1) // side, (n - 1) % side
            t[n, 0:7] = tv[np.clip(np.arange(7) - rq, -MAXREL, MAXREL) + MAXREL + 1]
            t[n, 7:12] = th[np.clip(np.arange(5) - cq, -MAXREL, MAXREL) + MAXREL + 1]
        t[:, 12] = tv[0]
        t[:, 13] = th[0]
        return t
    tk = by_position(a["L0_attn_tab_vk"], a["L0_attn_tab_hk"])
    tv = by_position(a["L0_attn_tab_vv"], a["L0_attn_tab_hv"])
    pk = np.zeros((4, 32, N, 4, 32), f)
    pv = np.zeros((4, 32, N, 4, HD), f)
    for r in range(4):
        pk[r, :HD, :, r, :HD] = np.eye(HD)[:, None, :]
        pk[r, :HD, :, r, HD:] = tk.transpose(2, 0, 1)
        pv[r, :HD, :, r, :] = np.eye(HD)[:, None, :]
        pv[r, HD:, :, r, :] = tv.transpose(1, 0, 2)
    w = a["L1_attn_w_inp"][0].reshape(2, HB, 3 * DIM).transpose(1, 0, 2)
    d["wC1"], d["wV1"] = w[:, :, :2 * DIM], w[:, :, 2 * DIM:]
    wf = np.zeros((6, HD, 6, HD), f)
    for i in range(6):
        wf[i, :, i, :] = a["L1_attn_omega"].T
    d["wF1"] = wf.reshape(HB, HB)
    d["wO1"] = a["L1_attn_w_out"][0].reshape(2, HB, DIM).transpose(1, 0, 2)
    w = a["L1_ffn_w_qkv"].reshape(2, HB, QH + 2 * KVH, QD // 2, 2)
    wq, wk = w[:, :, :QH], np.repeat(w[:, :, QH:QH + KVH], QH // KVH, axis=2)
    w2 = np.stack([t.reshape(2, HB, NJ, 4, 32, 2).transpose(0, 1, 2, 5, 3, 4) for t in (wq, wk)], 2)
    d["wQ2"] = w2.reshape(2, HB, 4 * NJ * 128).transpose(1, 0, 2)
    d["wV2"] = w[:, :, QH + KVH:].reshape(2, HB, KVH * QD).transpose(1, 0, 2)
    d["wO2"] = a["L1_ffn_w_out"].reshape(6, 128, DIM).transpose(1, 0, 2)
    d["posk"] = pk.reshape(128, N, 128)
    d["posv"] = pv.reshape(128, N, 64)
    return {k: np.ascontiguousarray(v) for k, v in d.items()}


def kernel(**inputs):
    import numpy as np
    import concourse.bacc as bacc
    from concourse.bass_utils import run_bass_kernel_spmd as run

    nc = bacc.Bacc("TRN2", target_bir_lowering=False, num_devices=1)
    arrays = layouts(inputs)
    ins = {k: nc.dram_tensor(f"in_{k}", v.shape, mybir.dt.from_np(v.dtype), kind="ExternalInput").ap()
           for k, v in arrays.items()}
    out = nc.dram_tensor("out_0_dram", (B, N, DIM), mybir.dt.float32, kind="ExternalOutput").ap()
    tower(nc, ins, out.rearrange("(g b) n d -> (b n) g d", g=NG))
    r = run(nc, [{f"in_{k}": v for k, v in arrays.items()}], core_ids=[0])
    return r.results[0]["out_0_dram"]
```

```python
import concourse.bass as bass
from concourse import mybir
from contextlib import ExitStack

B, CH, IMG, PATCH, DIM = 16, 3, 96, 16, 192
GRID = IMG // PATCH
N = GRID * GRID
TOK = B * N
NG = 8
GT = TOK // NG
HB = DIM // 2
NH, HD = 12, 16
NJ = 3
FP, FC = 120, 8
SH = 5
BC = 6
E0, F0 = 8, 768
E1, F1 = 16, 384
QH, KVH, QD = 12, 3, 64
QT, BT = QH // 2, QH // 2 + KVH
NEG = -1e30
BS = 112
NTHR = (TOK - 1) // BS
MAXB = [(2 * TOK + (BS - 1) * e + e - 2) // BS for e in (E0, E1)]
XT_OF = {1: 0, 2: 1, 3: 2, 5: 3, 6: 4}
GUB = (0, 1, 2, 3, 6, 7)
RING = (2, 4)
ZW = 768
EPS_LN, EPS_RMS = 1e-5, 1e-6


class Chain:

    def __init__(self, eng, sem, base=0):
        self.eng, self.sem, self.n, self.base = eng, sem, 0, base

    def __call__(self, ins):
        self.n += 1
        ins.then_inc(self.sem, 1)
        self.eng.wait_ge(self.sem, self.base + self.n)


def pipelined(eng, step):
    step(0, 0, first=True)
    with eng.Fori(0, NG // 2 - 1) as n:
        step(n * 2 + 1, 1)
        step(n * 2 + 2, 0)
    step(NG - 1, 1, last=True)


PIECES = ((0, 0, 4, 0, 0), (1, 0, 2, 0, 4), (1, 2, 2, 1, 0), (2, 0, 4, 1, 2))


def tower(nc, ins, out):
    fp32, bf16, i32, u32 = mybir.dt.float32, mybir.dt.bfloat16, mybir.dt.int32, mybir.dt.uint32
    ALU, ACT = mybir.AluOpType, mybir.ActivationFunctionType
    AX = mybir.AxisListType

    ctx = ExitStack()
    with ctx:
        def sb(name, shape, dt=fp32):
            return ctx.enter_context(nc.sbuf_tensor(name, shape, dt))

        sems = {}

        def sem(name):
            if name not in sems:
                sems[name] = ctx.enter_context(nc.semaphore(name))
            return sems[name]

        PS = ctx.enter_context(nc.psum_tensor("PS", [128, 8, 512], fp32))

        ident = sb("ident", [128, 128])
        identb = sb("identb", [128, 128], bf16)
        cst = sb("cst", [128, 768])
        blk4 = cst[:, 0:4]
        blk6 = cst[:, 4:10]
        cnt = cst[0:FP, 16:24]
        krows = cst[:, 32:68]
        vrows = cst[0:GT, 68:84]
        causal01 = cst[0:GT, 96:168]
        rcos = cst[:, 168:240]
        rsin = cst[:, 240:312]
        iota8 = cst[0:GT, 312:320]
        iota16 = cst[0:GT, 320:336]
        ones = cst[:, 336:464]
        eps_ln = cst[:, 464:465]
        eps_rms = cst[:, 465:466]
        eps_f = cst[:, 24:25]
        w1n = cst[0:HB, 466:468]
        w2n = cst[0:HB, 468:470]
        binp = cst[0:HB, 470:474]
        thr = cst[0:GT, 474:474 + NTHR]
        before = cst[0:GT, 480:480 + (E1 + 1) * E1].rearrange("p (a b) -> p a b", b=E1)
        maskb = sb("maskb", [GT, 2, GT], bf16)
        headsel = sb("headsel", [128, NH, GT], bf16)
        h = sb("h", [GT, NG, DIM])
        y = sb("y", [GT, NG, DIM])
        xnT = sb("xnT", [128, 2, TOK])
        st6 = sb("st6", [GT, NG, 6])
        mv = sb("mv", [GT, NG, 2])
        rstd = sb("rstd", [GT, NG])
        nmr = sb("nmr", [GT, NG])
        tmpg = sb("tmpg", [GT, NG])
        root = sb("root", [GT, 7])
        bias = sb("bias", [GT, 3, DIM])
        wC1 = sb("wC1", [128, 2, 4 * HB])
        wF1 = sb("wF1", [HB, HB])
        wV1 = sb("wV1", [128, 2, DIM])
        wO1 = sb("wO1", [128, 2, DIM])
        wQ2 = sb("wQ2", [128, 2, BT * 128])
        swap = sb("swap", [128, 128])
        wV2 = sb("wV2", [128, 2, KVH * QD])
        wO2 = sb("wO2", [128, 6, DIM])
        bxT = sb("bxT", [128, 2, BS])
        rw0 = sb("rw0", [128, 2, E0])
        rw1 = sb("rw1", [128, 2, E1])
        tri = sb("tri", [GT, GT], bf16)
        oneb = sb("oneb", [GT, GT], bf16)
        zero = sb("zero", [128, ZW])
        wgu0 = sb("wgu0", [128, RING[0], 2, 2 * F0])
        wd0 = sb("wd0", [128, RING[0], 6, DIM])
        wgu1 = wgu0[:, :, :, :].rearrange("p r k (s n) -> p (r k s n)", s=2)\
            .rearrange("p (r k n) -> p r k n", r=RING[1], k=2)
        wd1 = wd0[:, :, :, :].rearrange("p r c d -> p (r c d)").rearrange("p (r c d) -> p r c d", r=RING[1], c=3)
        xs = [nc.dram_tensor(f"xs{L}", ((MAXB[L] + 2) * BS, DIM), fp32, kind="Internal").ap() for L in range(2)]

        block = ctx.enter_context(nc.Block())

        stage_ctx = ExitStack()
        ctx.enter_context(stage_ctx)

        def stage_sb(stack, name, shape, dt=fp32):
            return stack.enter_context(nc.sbuf_tensor(name, shape, dt))

        wA = sb("wA", [128, 2, NJ * 2 * 128])
        wV0 = sb("wV0", [128, 2, DIM])
        wP0 = sb("wP0", [64, NJ, DIM])
        posk = sb("posk", [128, N, 128])
        posv = sb("posv", [128, N, 64])
        t_stack = ExitStack()
        xw = stage_sb(t_stack, "xw", [FP, FC, TOK])
        xsq = stage_sb(t_stack, "xsq", [FP, 4, TOK])
        w5 = stage_sb(t_stack, "w5", [FP, FC, SH, DIM])
        gb5 = stage_sb(t_stack, "gb5", [FP, 2, FC * SH])
        wc = stage_sb(t_stack, "wc", [FP, FC, DIM + 1])
        wbd = stage_sb(t_stack, "wbd", [FP, DIM])
        wcs = stage_sb(t_stack, "wcs", [FP, DIM])
        wb = stage_sb(t_stack, "wb", [FP, 2, DIM])
        wbs = stage_sb(t_stack, "wbs", [FP, SH, DIM])
        brow = stage_sb(t_stack, "brow", [1, DIM])
        gsum = stage_sb(t_stack, "gsum", [GT, 2, DIM])
        t_stack.close()
        a_stack = ExitStack()
        qT = stage_sb(a_stack, "qT", [128, NJ, TOK])
        qa = stage_sb(a_stack, "qa", [128, NJ, TOK])
        ka = stage_sb(a_stack, "ka", [128, NJ, TOK])
        va = stage_sb(a_stack, "va", [GT, NG, NH, 32])
        oaT = stage_sb(a_stack, "oaT", [128, NJ, TOK])
        of = stage_sb(a_stack, "of", [64, NJ, TOK])
        a_q = stage_sb(a_stack, "a_q", [128, 2, NJ, GT])
        a_k = stage_sb(a_stack, "a_k", [128, 2, NJ, GT])
        a_qz = stage_sb(a_stack, "a_qz", [128, 2, NJ, 4, GT])
        a_kz = stage_sb(a_stack, "a_kz", [128, 2, NJ, 4, GT])
        a_m = stage_sb(a_stack, "a_m", [GT, 128], bf16)
        a_mT = stage_sb(a_stack, "a_mT", [128, GT], bf16)
        a_p = stage_sb(a_stack, "a_p", [GT, NH, GT])
        a_rec = stage_sb(a_stack, "a_rec", [GT, NH])
        a_o = stage_sb(a_stack, "a_o", [GT, NH, 32])
        a_stack.close()
        l1_stack = ExitStack()
        rn = stage_sb(l1_stack, "rn", [GT, NG, DIM])
        r_stack = ExitStack()
        cT = stage_sb(r_stack, "cT", [HB, 4, TOK])
        sf = stage_sb(r_stack, "sf", [GT, NG, 2 * NH, HD])
        ssum = stage_sb(r_stack, "ssum", [GT, NG, 2 * NH])
        smax = stage_sb(r_stack, "smax", [GT, NG, 2 * NH])
        kmax = stage_sb(r_stack, "kmax", [GT, NG])
        fT = stage_sb(r_stack, "fT", [128, 4, TOK])
        vr = stage_sb(r_stack, "vr", [GT, NG, NH, HD + 1])
        r_qz = stage_sb(r_stack, "r_qz", [128, 2, 2, 6, GT])
        r_k = stage_sb(r_stack, "r_k", [128, 2, 2, GT])
        r_p = stage_sb(r_stack, "r_p", [GT, 2, NH, GT])
        r_den = stage_sb(r_stack, "r_den", [GT, NH])
        r_a = stage_sb(r_stack, "r_a", [GT, NH, HD])
        r_aT = stage_sb(r_stack, "r_aT", [128, 2, GT])
        r_stack.close()
        b_stack = ExitStack()
        rqk = stage_sb(b_stack, "rqk", [128, BT, TOK])
        qkx = stage_sb(b_stack, "qkx", [128, 2, 288])
        vb = stage_sb(b_stack, "vb", [GT, NG, KVH, QD + 1])
        rt = stage_sb(b_stack, "rt", [128, 2, 2, 288])
        b_q = stage_sb(b_stack, "b_q", [128, 2, QT, GT])
        b_kz = stage_sb(b_stack, "b_kz", [128, 2, KVH, 2, GT])
        b_m = stage_sb(b_stack, "b_m", [GT, 128], bf16)
        b_mT = stage_sb(b_stack, "b_mT", [128, GT], bf16)
        b_p = stage_sb(b_stack, "b_p", [GT, QH, GT])
        b_rec = stage_sb(b_stack, "b_rec", [GT, QH])
        b_o = stage_sb(b_stack, "b_o", [GT, QH, QD])
        b_oT = stage_sb(b_stack, "b_oT", [128, 6, GT])
        b_stack.close()
        m_stack = ExitStack()
        lg = stage_sb(m_stack, "lg", [GT, NG, E1])
        top8 = stage_sb(m_stack, "top8", [GT, NG, 8])
        idx8 = stage_sb(m_stack, "idx8", [GT, NG, 8], u32)
        idxf = stage_sb(m_stack, "idxf", [GT, NG, 2])
        sel = stage_sb(m_stack, "sel", [GT, 2, NG, E1])
        selb = stage_sb(m_stack, "selb", [GT, NG, E1], bf16)
        share = stage_sb(m_stack, "share", [GT, 2, NG])
        tot = stage_sb(m_stack, "tot", [GT, E1])
        over = stage_sb(m_stack, "over", [GT, E1, NTHR])
        nblk = stage_sb(m_stack, "nblk", [GT, E1])
        prod = stage_sb(m_stack, "prod", [GT, E1 + 1, E1])
        first = stage_sb(m_stack, "first", [GT, E1 + 1])
        firsti = stage_sb(m_stack, "firsti", [GT, E1 + 1], i32)
        slote = stage_sb(m_stack, "slote", [GT, NG, E1])
        slotf = stage_sb(m_stack, "slotf", [GT, 2, NG])
        slot = stage_sb(m_stack, "slot", [GT, 2, NG], u32)
        yg = stage_sb(m_stack, "yg", [GT, 2, NG, DIM])
        bx = stage_sb(m_stack, "bx", [BS, DIM])
        sg = stage_sb(m_stack, "sg", [128, 6, BS])
        hT = stage_sb(m_stack, "hT", [128, 6, BS])
        yo = stage_sb(m_stack, "yo", [BS, DIM])
        m_stack.close()
        l1_stack.close()
        WGU, WD = (wgu0, wgu1), (wd0, wd1)
        EX, HC = (E0, E1), (F0 // 128, F1 // 128)
        RW = (rw0, rw1)

        @block.sync
        def _(sp):
            sp.dma_start(cst[:, :], ins["cst"]).then_inc(sem("cst_in"), 16)
            for c in range(FC):
                sp.dma_start(w5[:, c, :, :], ins["w5"][:, c]).then_inc(sem(f"tok_in{c}"), 16)
                sp.dma_start(xw[:, c, :], ins["xw"][:, c]).then_inc(sem(f"tok_in{c}"), 16)
            sp.dma_start(posk[:, :, :], ins["posk"]).then_inc(sem("posk_in"), 16)
            sp.dma_start(posv[:, :, :], ins["posv"]).then_inc(sem("posv_in"), 16)
            sp.wait_ge(sem("zero"), 1)
            for L in range(2):
                for i in range(0, (MAXB[L] + 2) * BS * DIM, 128 * ZW):
                    n = min(128 * ZW, (MAXB[L] + 2) * BS * DIM - i) // 128
                    flat = xs[L].rearrange("a b -> (a b)")[i:i + 128 * n].rearrange("(p n) -> p n", p=128)
                    sp.dma_start(flat, zero[:, 0:n]).then_inc(sem("xs_zero"), 16)

            def experts_io(L):
                p = f"m{L}_"
                sp.wait_ge(sem(p + "first"), 1)
                blocks = sp.value_load(firsti[0:1, EX[L]:EX[L] + 1], min_val=1, max_val=MAXB[L])
                sp.sem_inc(sem(p + "y_out"), 16)
                sp.wait_ge(sem(p + "sent"), 16 * 2 * NG)
                sp.dma_start(bx[:, :], xs[L][0:BS, :]).then_inc(sem(p + "x_in"), 16)
                sp.wait_ge(sem(p + "xT_ps"), 1)
                sp.dma_start(bx[:, :], xs[L][BS:2 * BS, :]).then_inc(sem(p + "x_in"), 16)
                with sp.Fori(0, blocks) as b:
                    sp.wait_ge(sem(p + "xT_ps"), b + 2)
                    sp.dma_start(bx[:, :], xs[L][bass.ds(b * BS + 2 * BS, BS), :]).then_inc(sem(p + "x_in"), 16)
                    sp.wait_ge(sem(p + "y"), b + 1)
                    sp.dma_start(xs[L][bass.ds(b * BS, BS), :], yo[:, :]).then_inc(sem(p + "y_out"), 16)
                sp.wait_ge(sem(p + "x_in"), blocks * 16 + 32)
                sp.sem_inc(sem(p + "all_out"), 1)
                sp.wait_ge(sem(p + "y_out"), blocks * 16 + 16)
                sp.sem_inc(sem(p + "all_out"), 1)

            experts_io(0)
            experts_io(1)
            sp.wait_ge(sem("h_last"), 1)
            sp.dma_start(out, h[:, :, :]).then_inc(sem("out_done"), 16)
            sp.wait_ge(sem("out_done"), 16)

        @block.gpsimd
        def _(pool):
            pool.dma_start(identb[:, :], ins["identb"]).then_inc(sem("bf_in"), 16)
            pool.dma_start(maskb[:, :, :], ins["maskb"]).then_inc(sem("bf_in"), 16)
            pool.dma_start(headsel[:, :, :], ins["headsel"]).then_inc(sem("bf_in"), 16)
            pool.dma_start(tri[:, :], ins["tri"]).then_inc(sem("bf_in"), 16)
            pool.dma_start(oneb[:, :], ins["oneb"]).then_inc(sem("bf_in"), 16)
            pool.wait_ge(sem("gb_in"), 32)
            for c in range(BC):
                pool.wait_ge(sem(f"tok_in{c}"), 32)
                nc.gpsimd.tensor_tensor(wbs[:, :, :], w5[:, c, :, :],
                                        gb5[:, 1, c * SH:(c + 1) * SH].unsqueeze(2).to_broadcast([FP, SH, DIM]),
                                        ALU.mult).then_inc(sem("t_wb"), 1)
                pool.wait_ge(sem("t_wb"), 4 * c + 1)
                nc.gpsimd.tensor_tensor(wbs[:, 0:2, :], wbs[:, 0:2, :], wbs[:, 2:4, :], ALU.add)\
                    .then_inc(sem("t_wb"), 1)
                pool.wait_ge(sem("t_wb"), 4 * c + 2)
                part = wb[:, 0, :] if c == 0 else wb[:, 1, :]
                nc.gpsimd.tensor_tensor(part, wbs[:, 0, :], wbs[:, 1, :], ALU.add).then_inc(sem("t_wb"), 1)
                pool.wait_ge(sem("t_wb"), 4 * c + 3)
                nc.gpsimd.tensor_tensor(part, part, wbs[:, 4, :], ALU.add).then_inc(sem("t_wb"), 1)
                pool.wait_ge(sem("t_wb"), 4 * c + 4)
                if c > 0:
                    nc.gpsimd.tensor_tensor(wb[:, 0, :], wb[:, 0, :], part, ALU.add).then_inc(sem("t_wbs"), 1)
                    pool.wait_ge(sem("t_wbs"), c)
            for t in (xnT, wA, wV0):
                nc.gpsimd.memset(t[HB:128], 0.0).then_inc(sem("pads"), 1)
            pool.wait_ge(sem("t_inv"), 1)
            pool.wait_ge(sem("t_gs"), 1)
            late = y[:, NG // 2:NG, :]
            nc.gpsimd.tensor_tensor(late, gsum[:, 0:1, :].to_broadcast([GT, NG // 2, DIM]),
                                    nmr[:, NG // 2:NG].unsqueeze(2).to_broadcast([GT, NG // 2, DIM]), ALU.mult)\
                .then_inc(sem("t_shift"), 1)
            pool.wait_ge(sem("t_shift"), 1)
            nc.gpsimd.tensor_tensor(late, late, gsum[:, 1:2, :].to_broadcast([GT, NG // 2, DIM]), ALU.add)\
                .then_inc(sem("t_shift"), 1)
            nc.gpsimd.memset(zero[:, :], 0.0).then_inc(sem("zero"), 1)
            pool.wait_ge(sem("zero"), 1)
            for t in (rw0, rw1, bxT, wgu0, wC1, wV1, wO1, wQ2, wV2):
                nc.gpsimd.memset(t[HB:128], 0.0).then_inc(sem("pads"), 1)
            for r in range(RING[0]):
                pool.dma_start(wgu0[0:HB, r, :, :], ins["wgu0"][r]).then_inc(sem(f"m0_w{r}"), 16)
                pool.dma_start(wd0[:, r, :, :], ins["wd0"][r]).then_inc(sem(f"m0_w{r}"), 16)
            NZ = sum(-(-(MAXB[L] + 2) * BS * DIM // (128 * ZW)) for L in range(2))
            pool.wait_ge(sem("xs_zero"), 16 * NZ)

            def in_a(g, par):
                nc.gpsimd.tensor_copy(a_k[:, par, :, :], ka[:, :, bass.ts(g, GT)]).then_inc(sem("a_qz"), 1)
                for j in range(NJ):
                    nc.gpsimd.tensor_tensor(
                        a_qz[:, par, j, :, :], qa[:, j, bass.ts(g, GT)].unsqueeze(1).to_broadcast([128, 4, GT]),
                        blk4.unsqueeze(2).to_broadcast([128, 4, GT]), ALU.mult).then_inc(sem("a_qz"), 1)
            pool.wait_ge(sem("pads"), 12)
            pool.wait_ge(sem("a_ka"), 2 * NJ)
            pool.wait_ge(sem("a_qa"), 4)
            in_a(0, 0)
            in_a(1, 1)
            with pool.Fori(1, NG // 2) as n:
                for par in range(2):
                    pool.wait_ge(sem("att_s2"), n * 2 + (par - 1))
                    in_a(n * 2 + par, par)

            def experts_dma(L):
                p = f"m{L}_"
                pool.wait_ge(sem(p + "slot"), 1)
                for k in range(2):
                    for g in range(NG):
                        nc.gpsimd.indirect_dma_start(
                            out=xs[L], out_offset=bass.IndirectOffsetOnAxis(ap=slot[:, k, g:g + 1], axis=0),
                            in_=(y, rn)[L][:, g, :], in_offset=None).then_inc(sem(p + "sent"), 16)
                R = RING[L]
                with pool.Fori(1, EX[L] // R) as q:
                    for r in range(R):
                        done = pool.value_load(firsti[0:1, bass.ds(q * R + (r - R + 1), 1)], min_val=1, max_val=MAXB[L])
                        pool.wait_ge(sem(p + "y_ps"), done)
                        pool.dma_start(WGU[L][0:HB, r, :, :], ins[f"wgu{L}"][q * R + r]).then_inc(sem(p + f"w{r}"), 16)
                        pool.dma_start(WD[L][:, r, :, :], ins[f"wd{L}"][q * R + r]).then_inc(sem(p + f"w{r}"), 16)
                pool.wait_ge(sem(p + "all_out"), 2)
                for g in range(NG):
                    for k in range(2):
                        nc.gpsimd.indirect_dma_start(
                            out=yg[:, k, g, :], out_offset=None, in_=xs[L],
                            in_offset=bass.IndirectOffsetOnAxis(ap=slot[:, k, g:g + 1], axis=0))\
                            .then_inc(sem(f"back{g}"), 16)

            experts_dma(0)
            for r in range(RING[1]):
                pool.dma_start(wgu1[0:HB, r, :, :], ins["wgu1"][r]).then_inc(sem(f"m1_w{r}"), 16)
                pool.dma_start(wd1[:, r, :, :], ins["wd1"][r]).then_inc(sem(f"m1_w{r}"), 16)
            nc.gpsimd.memset(fT[HB:128, :, :], 0.0).then_inc(sem("pads"), 1)
            nc.gpsimd.memset(r_aT[HB:128, :, :], 0.0).then_inc(sem("pads"), 1)
            pool.wait_ge(sem("pads"), 14)

            def in_r(g, par):
                nc.gpsimd.tensor_copy(r_k[:, par, :, :], fT[:, 2:4, bass.ts(g, GT)]).then_inc(sem("r_in"), 1)
                for i in range(2):
                    nc.gpsimd.tensor_tensor(
                        r_qz[:, par, i, :, :], fT[:, i, bass.ts(g, GT)].unsqueeze(1).to_broadcast([128, 6, GT]),
                        blk6.unsqueeze(2).to_broadcast([128, 6, GT]), ALU.mult).then_inc(sem("r_in"), 1)

            pool.wait_ge(sem("r_fT"), 4)
            in_r(0, 0)
            in_r(1, 1)
            pool.wait_ge(sem("r_qk"), 1)
            in_r(2, 0)
            pool.wait_ge(sem("r_qk"), 2)
            in_r(3, 1)
            pool.wait_ge(sem("r_fT"), 8)
            with pool.Fori(2, NG // 2) as n:
                for par in range(2):
                    pool.wait_ge(sem("r_qk"), n * 2 + (par - 1))
                    in_r(n * 2 + par, par)
            for n in range(2 * BT):
                t, q = n // 2, n % 2
                pool.wait_ge(sem("b_rope"), n + 1)
                nc.gpsimd.tensor_tensor(rqk[:, t, q * 288:(q + 1) * 288], rt[:, n % 2, 0, :], rt[:, n % 2, 1, :],
                                        ALU.add).then_inc(sem("b_r"), 1)
            experts_dma(1)

        @block.scalar
        def _(act):
            act.dma_start(gb5[:, :, :], ins["gb5"]).then_inc(sem("gb_in"), 16)
            act.dma_start(brow[:, :], ins["tok_b"]).then_inc(sem("gb_in"), 16)
            act.dma_start(ident[:, :], ins["ident"]).then_inc(sem("cst_in"), 16)
            act.dma_start(bias[:, :, :], ins["bias"]).then_inc(sem("cst_in"), 16)

            def squares(c):
                act.wait_ge(sem(f"tok_in{c}"), 32)
                if c >= 4:
                    act.wait_ge(sem("t_used"), c - 3)
                nc.scalar.activation(xsq[:, c % 4, :], xw[:, c, :], ACT.Square).then_inc(sem("t_sq"), 1)
            for c in range(4):
                squares(c)
            act.dma_start(wA[0:HB, :, :], ins["wA"]).then_inc(sem("wA_in"), 16)
            act.dma_start(wV0[0:HB, :, :], ins["wV0"]).then_inc(sem("wA_in"), 16)
            act.dma_start(wP0[:, :, :], ins["wP0"]).then_inc(sem("wA_in"), 16)
            for c in range(4, FC):
                squares(c)
            act.dma_start(rw0[0:HB, :, :], ins["rw0"]).then_inc(sem("rw_in"), 16)
            act.dma_start(rw1[0:HB, :, :], ins["rw1"]).then_inc(sem("rw_in"), 16)
            for name, t in (("wC1", wC1), ("wF1", wF1), ("wV1", wV1), ("wO1", wO1), ("wQ2", wQ2), ("wV2", wV2),
                            ("wO2", wO2), ("swap", swap)):
                at = (slice(0, ins[name].shape[0]),) + (slice(None),) * (len(t.shape) - 1)
                act.dma_start(t[at], ins[name]).then_inc(sem("l1_in"), 16)
            act.wait_ge(sem("cst_in"), 48)
            nc.scalar.activation(root[:, 0:1], eps_ln[0:GT], ACT.Sqrt)
            act.wait_ge(sem("t_gsum"), 1)
            nc.scalar.activation(gsum[:, :, :], PS[0:GT, 4, 0:2 * DIM].rearrange("p (a d) -> p a d", a=2), ACT.Copy)\
                .then_inc(sem("t_gs"), 1)
            act.wait_ge(sem("t_var"), 1)
            nc.scalar.activation(rstd[:, :], tmpg[:, :], ACT.Sqrt, bias=eps_ln[0:GT], scale=1.0)\
                .then_inc(sem("t_std"), 1)
            def std(k, src, dst, eps=eps_ln):
                nc.scalar.activation(root[:, k:k + 1], eps_ln[0:GT], ACT.Sqrt)
                act.wait_ge(sem("ln_mv"), k)
                nc.scalar.activation(rstd[:, :], mv[:, :, 1], ACT.Sqrt, bias=eps[0:GT], scale=1.0)\
                    .then_inc(sem("ln_std"), 1)
                act.wait_ge(sem("ln_inv"), k)
                for g in range(1, NG, 2):
                    if eps is eps_ln:
                        nc.scalar.activation(dst[:, g, :], src[:, g, :], ACT.Identity, bias=nmr[:, g:g + 1],
                                             scale=rstd[:, g:g + 1]).then_inc(sem("ln_odd"), 1)
                    else:
                        nc.scalar.activation(dst[:, g, :], src[:, g, :], ACT.Copy, scale=rstd[:, g:g + 1])\
                            .then_inc(sem("ln_odd"), 1)

            def evict_xnT(k, weight=None):
                for b in range(0, 4, 2):
                    act.wait_ge(sem("ln_T"), 4 * XT_OF[k] + b + 1)
                    hf, q = b // 2, b % 2
                    scale = 1.0 if weight is None else weight[:, hf:hf + 1]
                    nc.scalar.activation(xnT[0:HB, hf, q * 288:(q + 1) * 288], PS[0:HB, b, 0:288], ACT.Copy,
                                         scale=scale).then_inc(sem("xnT"), 1)
            std(1, h, y)
            evict_xnT(1)
            for j in range(NJ):
                for q in range(2):
                    act.wait_ge(sem("a_qk"), 2 * j + q + 1)
                    nc.scalar.activation(qT[:, j, q * 288:(q + 1) * 288], PS[:, 4 + (2 * j + q) % 2, 0:288],
                                         ACT.Copy, scale=HD ** -0.5).then_inc(sem("a_qT"), 1)
            for i in range(4):
                act.wait_ge(sem("a_pos"), i + 1)
                nc.scalar.activation(
                    qa[:, :, :].rearrange("p j (b n) -> p n j b", n=N)[:, 9 * i:9 * i + 9, :, :],
                    PS[:, 2 + i, 0:432].rearrange("p (n j b) -> p n j b", j=NJ, b=B), ACT.Copy)\
                    .then_inc(sem("a_qa"), 1)
            for g in range(NG):
                act.wait_ge(sem("a_v"), g + 1)
                nc.scalar.activation(va[:, g, :, 0:HD],
                                     PS[0:GT, g % 2, 0:DIM].rearrange("p (h d) -> p h d", h=NH),
                                     ACT.Copy).then_inc(sem("a_va"), 1)

            def oT_a(g):
                act.wait_ge(sem("a_oT"), g + 1)
                nc.scalar.activation(oaT[:, :, bass.ts(g, GT)],
                                     PS[:, 2, 0:3 * GT].rearrange("p (j t) -> p j t", j=NJ), ACT.Copy)\
                    .then_inc(sem("a_oaT"), 1)

            def step_a(g, par, first=False, last=False):
                act.wait_ge(sem("att_mt_ps"), g + 1)
                nc.scalar.activation(a_mT[:, :], PS[:, 4, 432:468].bitcast(bf16), ACT.Copy).then_inc(sem("att_mt"), 1)
                act.wait_ge(sem("att_s2"), g + 1)
                nc.scalar.activation(a_p[:, :, :].rearrange("p (a b) k -> p a (b k)", a=2),
                                     PS[0:GT, 3:5, 0:432], ACT.Exp).then_inc(sem("att_exp"), 1)
                if not first:
                    oT_a(g - 1)
            pipelined(act, step_a)
            oT_a(NG - 1)
            for i in range(4):
                act.wait_ge(sem("a_pos2"), i + 1)
                nc.scalar.activation(
                    of[:, :, :].rearrange("p j (b n) -> p n j b", n=N)[:, 9 * i:9 * i + 9, :, :],
                    PS[0:64, i, 0:432].rearrange("p (n j b) -> p n j b", j=NJ, b=B), ACT.Copy)\
                    .then_inc(sem("a_of"), 1)

            def experts_act(L):
                p, H = f"m{L}_", HC[L]
                act.wait_ge(sem("route_diff"), L + 1)
                nc.scalar.activation(share[:, 1, :], share[:, 0, :], ACT.Exp).then_inc(sem("route_exp"), 1)
                act.wait_ge(sem(p + "first"), 1)
                blocks = act.value_load(firsti[0:1, EX[L]:EX[L] + 1], min_val=1, max_val=MAXB[L])

                def block_T():
                    src = PS[0:HB, 4, 0:2 * BS].rearrange("p (k t) -> p k t", k=2)
                    if L == 0:
                        nc.scalar.activation(bxT[0:HB, :, :], src, ACT.Copy).then_inc(sem(p + "xT"), 2)
                    else:
                        for k in range(2):
                            nc.scalar.activation(bxT[0:HB, k, :], src[:, k, :], ACT.Copy, scale=w2n[:, k:k + 1])\
                                .then_inc(sem(p + "xT"), 1)
                act.wait_ge(sem(p + "xT_ps"), 1)
                block_T()
                with act.Fori(0, blocks) as b:
                    for c in range(H):
                        act.wait_ge(sem(p + "gu"), b * H + (c + 1))
                        nc.scalar.activation(sg[:, c, :], PS[:, GUB[c], 0:BS], ACT.Silu).then_inc(sem(p + "sg"), 1)
                    act.wait_ge(sem(p + "xT_ps"), b + 2)
                    block_T()
            std(2, h, y)
            evict_xnT(2)
            experts_act(0)
            std(3, h, y)
            evict_xnT(3)
            for q in range(2):
                for m in range(4):
                    n = 4 * q + m
                    act.wait_ge(sem("r_c"), n + 1)
                    nc.scalar.activation(cT[:, m, q * 288:(q + 1) * 288], PS[0:HB, 4 + n % 2, 0:288], ACT.Identity,
                                         bias=binp[:, m:m + 1], scale=1.0).then_inc(sem("r_cT"), 1)
                if q == 1:
                    act.wait_ge(sem("r_arg"), 2)
                    nc.scalar.activation(sf[:, 0:4, :, :], sf[:, 0:4, :, :], ACT.Exp).then_inc(sem("r_exp"), 1)
                for g in range(4 * q, 4 * q + 4):
                    act.wait_ge(sem("r_s"), g + 1)
                    nc.scalar.activation(sf[:, g, :, :].rearrange("p h d -> p (h d)"), PS[0:GT, g % 2, 0:2 * DIM],
                                         ACT.Copy, scale=float(HD) ** -0.25).then_inc(sem("r_sf"), 1)
            for g in range(NG):
                act.wait_ge(sem("r_v"), g + 1)
                nc.scalar.activation(vr[:, g, :, 0:HD],
                                     PS[0:GT, 2 + g % 2, 0:DIM].rearrange("p (h d) -> p h d", h=NH), ACT.Copy)\
                    .then_inc(sem("r_vr"), 1)
            for q in range(2):
                if q == 1:
                    act.wait_ge(sem("r_arg"), 4)
                    nc.scalar.activation(sf[:, 4:8, :, :], sf[:, 4:8, :, :], ACT.Exp).then_inc(sem("r_exp"), 1)
                for m in range(4):
                    b = 4 * q + m
                    act.wait_ge(sem("r_fT_ps"), b + 1)
                    nc.scalar.activation(fT[0:HB, m, q * 288:(q + 1) * 288], PS[0:HB, 4 + b % 2, 0:288],
                                         ACT.Identity, bias=eps_f[0:HB], scale=float(HD) ** -0.5)\
                        .then_inc(sem("r_fT"), 1)
            with act.Fori(0, NG) as g:
                act.wait_ge(sem("r_aT_ps"), g + 1)
                nc.scalar.activation(r_aT[0:HB, :, :], PS[0:HB, 3, 0:2 * GT].rearrange("p (k t) -> p k t", k=2),
                                     ACT.Copy).then_inc(sem("r_aT"), 1)
            std(4, h, y)
            std(5, y, rn, eps_rms)
            evict_xnT(5, w1n)
            for n in range(2 * BT):
                act.wait_ge(sem("b_x_ps"), n + 1)
                if n >= 2:
                    act.wait_ge(sem("b_rope"), n - 1)
                nc.scalar.activation(qkx[:, n % 2, :], PS[:, 4 + n % 2, 0:288], ACT.Copy).then_inc(sem("b_x"), 1)
            for g in range(NG):
                act.wait_ge(sem("b_v"), g + 1)
                nc.scalar.activation(vb[:, g, :, 0:QD], PS[0:GT, g % 2, 0:KVH * QD]
                                     .rearrange("p (h d) -> p h d", h=KVH), ACT.Copy).then_inc(sem("b_vb"), 1)


            def oT_b(g):
                act.wait_ge(sem("b_oT_ps"), g + 1)
                nc.scalar.activation(b_oT[:, :, :], PS[:, 2, 0:6 * GT].rearrange("p (c t) -> p c t", c=6), ACT.Copy)\
                    .then_inc(sem("b_oT"), 1)

            def step_b(g, par, first=False, last=False):
                act.wait_ge(sem("att_mt_ps"), g + (NG + 1))
                nc.scalar.activation(b_mT[:, :], PS[:, 2, 432:468].bitcast(bf16), ACT.Copy).then_inc(sem("att_mt"), 1)
                act.wait_ge(sem("att_s2"), g + (NG + 1))
                nc.scalar.activation(b_p[:, :, :].rearrange("p (a b) k -> p a (b k)", a=2),
                                     PS[0:GT, 3:5, 0:432], ACT.Exp, scale=float(QD) ** -0.5)\
                    .then_inc(sem("att_exp"), 1)
                if not first:
                    oT_b(g - 1)
            pipelined(act, step_b)
            oT_b(NG - 1)
            std(6, y, rn, eps_rms)
            evict_xnT(6, w2n)
            experts_act(1)

        @block.vector
        def _(dve):
            tc = Chain(dve, sem("t_chain"))
            dve.wait_ge(sem("gb_in"), 32)
            for c in range(FC):
                dve.wait_ge(sem(f"tok_in{c}"), 32)
                tc(nc.vector.tensor_scalar(wc[:, c, 0:DIM], w5[:, c, 0, :], gb5[:, 0, c * SH:c * SH + 1], None,
                                           ALU.mult))
                for s in range(1, SH):
                    ins_ = nc.vector.scalar_tensor_tensor(wc[:, c, 0:DIM], w5[:, c, s, :],
                                                          gb5[:, 0, c * SH + s:c * SH + s + 1],
                                                          wc[:, c, 0:DIM], ALU.mult, ALU.add)
                    if s < SH - 1:
                        tc(ins_)
                if c == 0:
                    dve.wait_ge(sem("cst_in"), 48)
                ins_.then_inc(sem("t_wc"), 1)
                nc.vector.tensor_copy(wc[:, c, DIM:DIM + 1], cnt[:, c:c + 1]).then_inc(sem("t_wc"), 1)
                if c > 0:
                    dve.wait_ge(sem("t_wc"), 2 * c + 2)
                    if c > 1:
                        dve.wait_ge(sem("t_wcs"), c - 1)
                    nc.vector.tensor_tensor(wcs[:, :], wc[:, 0, 0:DIM] if c == 1 else wcs[:, :], wc[:, c, 0:DIM],
                                            ALU.add).then_inc(sem("t_wcs"), 1)
            for n in range((FC - BC) * SH):
                c, s = BC + n // SH, n % SH
                beta = gb5[:, 1, c * SH + s:c * SH + s + 1]
                if n == 0:
                    ins_ = nc.vector.tensor_scalar(wbd[:, :], w5[:, c, s, :], beta, None, ALU.mult)
                else:
                    dve.wait_ge(sem("t_wbd"), n)
                    ins_ = nc.vector.scalar_tensor_tensor(wbd[:, :], w5[:, c, s, :], beta, wbd[:, :], ALU.mult,
                                                          ALU.add)
                ins_.then_inc(sem("t_wbd"), 1)
            dve.wait_ge(sem("t_used"), FC)
            s1 = PS[0:GT, 0:4, 0:388].rearrange("p b (q c) -> p b q c", q=2)[:, :, :, DIM]
            s2 = PS[0:GT, 0:4, 0:388].rearrange("p b (q c) -> p b q c", q=2)[:, :, :, DIM + 1]
            m4 = mv[:, :, 0].rearrange("p (b q) -> p b q", q=2)
            e4 = mv[:, :, 1].rearrange("p (b q) -> p b q", q=2)
            K = PATCH * PATCH * SH * CH
            nc.vector.tensor_scalar(m4, s1, -1.0 / K, None, ALU.mult).then_inc(sem("t_chain"), 1)
            tc.n += 1
            tc(nc.vector.tensor_scalar(e4, s2, 1.0 / K, None, ALU.mult))
            tc(nc.vector.tensor_tensor(nmr[:, :], mv[:, :, 0], mv[:, :, 0], ALU.mult))
            nc.vector.tensor_tensor(tmpg[:, :], mv[:, :, 1], nmr[:, :], ALU.subtract).then_inc(sem("t_var"), 1)
            dve.wait_ge(sem("t_std"), 1)
            tc(nc.vector.reciprocal(rstd[:, :], rstd[:, :]))
            nc.vector.tensor_tensor(nmr[:, :], mv[:, :, 0], rstd[:, :], ALU.mult).then_inc(sem("t_inv"), 1)
            for g in range(NG // 2):
                if g == 0:
                    dve.wait_ge(sem("t_inv"), 1)
                    dve.wait_ge(sem("t_gs"), 1)
                nc.vector.scalar_tensor_tensor(y[:, g, :], gsum[:, 0, :], nmr[:, g:g + 1], gsum[:, 1, :],
                                               ALU.mult, ALU.add).then_inc(sem("t_h"), 1)
            for g in range(NG):
                if g < NG // 2:
                    dve.wait_ge(sem("t_h"), g + 1)
                else:
                    dve.wait_ge(sem("t_shift"), 2)
                acc = PS[0:GT, g // 2, (g % 2) * 194:(g % 2) * 194 + DIM]
                nc.vector.scalar_tensor_tensor(h[:, g, :], acc, rstd[:, g:g + 1], y[:, g, :],
                                               ALU.mult, ALU.add).then_inc(sem("t_h"), 1)
            dve.wait_ge(sem("t_h"), NG // 2 + NG)

            lc = Chain(dve, sem("ln_chain"))

            def stat(k, src, g):
                at = bass.ds(g, 1)
                nc.vector.bn_stats(st6[:, at, :], src[:, at, :]).then_inc(sem("ln_stat"), 1)

            def norm(k, src, dst, rms=False):
                dve.wait_ge(sem("ln_stat"), k * NG)
                for g in range(NG):
                    nc.vector.bn_aggr(mv[:, g, :], st6[:, g, :]).then_inc(sem("ln_agg"), 1)
                dve.wait_ge(sem("ln_agg"), k * NG)
                if rms:
                    lc(nc.vector.tensor_tensor(nmr[:, :], mv[:, :, 0], mv[:, :, 0], ALU.mult))
                    lc(nc.vector.tensor_tensor(mv[:, :, 1], mv[:, :, 1], nmr[:, :], ALU.add))
                nc.vector.tensor_copy(tmpg[:, :], mv[:, :, 0]).then_inc(sem("ln_mv"), 1)
                dve.wait_ge(sem("ln_std"), k)
                lc(nc.vector.reciprocal(rstd[:, :], rstd[:, :]))
                nc.vector.scalar_tensor_tensor(nmr[:, :], mv[:, :, 0], -1.0, rstd[:, :], ALU.mult, ALU.mult)\
                    .then_inc(sem("ln_inv"), 1)
                for g in range(0, NG, 2):
                    if rms:
                        last = nc.vector.tensor_scalar(dst[:, g, :], src[:, g, :], rstd[:, g:g + 1], None, ALU.mult)
                    else:
                        last = nc.vector.tensor_scalar(dst[:, g, :], src[:, g, :], mv[:, g, 0:1], rstd[:, g:g + 1],
                                                       ALU.subtract, ALU.mult)
                    last.then_inc(sem("ln_even"), 1)

            def evict_xnT(k, weight=None):
                for b in range(1, 4, 2):
                    dve.wait_ge(sem("ln_T"), 4 * XT_OF[k] + b + 1)
                    hf, q = b // 2, b % 2
                    scale = 1.0 if weight is None else weight[:, hf:hf + 1]
                    nc.vector.tensor_scalar(xnT[0:HB, hf, q * 288:(q + 1) * 288], PS[0:HB, b, 0:288], scale, None,
                                            ALU.mult).then_inc(sem("xnT"), 1)
            for g in range(NG):
                stat(1, h, g)
            norm(1, h, y)
            evict_xnT(1)
            for j in range(NJ):
                for q in range(2):
                    dve.wait_ge(sem("a_qk"), 2 * NJ + 2 * j + q + 1)
                    nc.vector.tensor_tensor(
                        ka[:, j, q * 288:(q + 1) * 288].rearrange("p (b n) -> p b n", n=N),
                        PS[:, 4 + (2 * j + q) % 2, 0:288].rearrange("p (b n) -> p b n", n=N),
                        krows.unsqueeze(1).to_broadcast([128, 8, N]), ALU.add).then_inc(sem("a_ka"), 1)
            nc.vector.memset(a_m[:, :], 0.0).then_inc(sem("a_va1"), 1)
            dve.wait_ge(sem("a_va1"), 1)
            dve.wait_ge(sem("bf_in"), 80)
            nc.vector.tensor_copy(a_m[:, NH:NH + GT], maskb[:, 0, :]).then_inc(sem("a_va1"), 1)
            for g in range(NG):
                nc.vector.tensor_copy(va[:, g, :, HD:32], vrows.unsqueeze(1).to_broadcast([GT, NH, 16]))\
                    .then_inc(sem("a_va1"), 1)
            dve.wait_ge(sem("a_va1"), NG + 2)
            dve.wait_ge(sem("a_ka"), 2 * NJ)
            dve.wait_ge(sem("a_qa"), 4)

            def in_a(g, par):
                at = bass.ts(g, GT)
                nc.vector.tensor_copy(a_q[:, par, :, :], qa[:, :, at]).then_inc(sem("a_in"), 1)
                for j in range(NJ):
                    nc.vector.tensor_tensor(
                        a_kz[:, par, j, :, :], ka[:, j, at].unsqueeze(1).to_broadcast([128, 4, GT]),
                        blk4.unsqueeze(2).to_broadcast([128, 4, GT]), ALU.mult).then_inc(sem("a_in"), 1)

            def max_a(g):
                dve.wait_ge(sem("att_s1"), g + 1)
                nc.vector.tensor_reduce(a_m[:, 0:NH].rearrange("p (a b) -> p a b", a=2),
                                        PS[0:GT, 0:2, 0:432].rearrange("p a (b k) -> p a b k", k=GT),
                                        AX.X, ALU.max, negate=True).then_inc(sem("att_max"), 1)

            def out_a(g):
                dve.wait_ge(sem("att_av"), g + 1)
                o3 = PS[0:GT, 7, 0:384].rearrange("p (h d) -> p h d", h=NH)
                nc.vector.reciprocal(a_rec[:, :], o3[:, :, 30]).then_inc(sem("att_rec"), 1)
                dve.wait_ge(sem("att_rec"), g + 1)
                nc.vector.tensor_tensor(a_o[:, :, :], o3, a_rec[:, :].unsqueeze(2).to_broadcast([GT, NH, 32]),
                                        ALU.mult).then_inc(sem("att_o"), 1)

            def step_a(g, par, first=False, early=True, last=False):
                if not first:
                    out_a(g - 1)
                if early:
                    in_a(g + 2, par)
                if not last:
                    max_a(g + 1)
            in_a(0, 0)
            in_a(1, 1)
            max_a(0)
            step_a(0, 0, first=True)
            with dve.Fori(0, NG // 2 - 2) as n:
                step_a(n * 2 + 1, 1)
                step_a(n * 2 + 2, 0)
            step_a(NG - 3, 1)
            step_a(NG - 2, 0, early=False)
            step_a(NG - 1, 1, early=False, last=True)
            out_a(NG - 1)
            nc.vector.tensor_tensor(h[:, :, :], h[:, :, :], bias[:, 0:1, :].to_broadcast([GT, NG, DIM]), ALU.add)\
                .then_inc(sem("a_res"), 1)
            dve.wait_ge(sem("a_res"), 1)
            for g in range(NG):
                dve.wait_ge(sem("a_proj"), g + 1)
                nc.vector.tensor_tensor(h[:, g, :], h[:, g, :], PS[0:GT, 4 + g % 2, 0:DIM], ALU.add)\
                    .then_inc(sem("a_res"), 1)
                dve.wait_ge(sem("a_res"), g + 2)
                stat(2, h, g)

            def route(L):
                p, E = f"m{L}_", EX[L]
                c = Chain(dve, sem(p + "chain"))
                dve.wait_ge(sem("route_logits"), L + 1)
                c(nc.vector.tensor_copy(lg[:, :, 0:E], PS[0:GT, 6, 0:NG * E].rearrange("p (g e) -> p g e", g=NG)))
                for g in range(NG):
                    nc.vector.max(top8[:, g, :], lg[:, g, 0:E]).then_inc(sem(p + "chain"), 1)
                c.n += NG
                dve.wait_ge(sem(p + "chain"), c.n)
                nc.vector.tensor_tensor(share[:, 0, :], top8[:, :, 1], top8[:, :, 0], ALU.subtract)\
                    .then_inc(sem("route_diff"), 1)
                for g in range(NG):
                    nc.vector.max_index(idx8[:, g, :], top8[:, g, :], lg[:, g, 0:E]).then_inc(sem(p + "chain"), 1)
                c.n += NG
                dve.wait_ge(sem(p + "chain"), c.n)
                c(nc.vector.tensor_copy(idxf[:, :, :], idx8[:, :, 0:2]))
                for k in range(2):
                    nc.vector.tensor_tensor(sel[:, k, :, 0:E], iota16[:, 0:E].unsqueeze(1).to_broadcast([GT, NG, E]),
                                            idxf[:, :, k:k + 1].to_broadcast([GT, NG, E]), ALU.is_equal)\
                        .then_inc(sem(p + "chain"), 1)
                c.n += 2
                dve.wait_ge(sem(p + "chain"), c.n)
                nc.vector.tensor_tensor(selb[:, :, 0:E], sel[:, 0, :, 0:E], sel[:, 1, :, 0:E], ALU.add)\
                    .then_inc(sem("route_sel"), 1)
                dve.wait_ge(sem("route_exp"), L + 1)
                c(nc.vector.tensor_scalar(share[:, 0, :], share[:, 1, :], 1.0, None, ALU.add))
                c(nc.vector.reciprocal(share[:, 0, :], share[:, 0, :]))
                c(nc.vector.tensor_tensor(share[:, 1, :], share[:, 1, :], share[:, 0, :], ALU.mult))
                dve.wait_ge(sem("route_pos"), L + 1)
                c(nc.vector.tensor_copy(tot[:, 0:E], PS[0:GT, 5, 0:E]))
                c(nc.vector.tensor_tensor(over[:, 0:E, :], tot[:, 0:E].unsqueeze(2).to_broadcast([GT, E, NTHR]),
                                          thr.unsqueeze(1).to_broadcast([GT, E, NTHR]), ALU.is_gt))
                c(nc.vector.tensor_reduce(nblk[:, 0:E], over[:, 0:E, :], AX.X, ALU.add))
                c(nc.vector.tensor_scalar(nblk[:, 0:E], nblk[:, 0:E], 1.0, None, ALU.add))
                c(nc.vector.tensor_tensor(prod[:, 0:E + 1, 0:E], before[:, 0:E + 1, 0:E],
                                          nblk[:, 0:E].unsqueeze(1).to_broadcast([GT, E + 1, E]), ALU.mult))
                c(nc.vector.tensor_reduce(first[:, 0:E + 1], prod[:, 0:E + 1, 0:E], AX.X, ALU.add))
                nc.vector.tensor_copy(firsti[:, 0:E + 1], first[:, 0:E + 1]).then_inc(sem(p + "first"), 1)
                c(nc.vector.scalar_tensor_tensor(
                    slote[:, :, 0:E], first[:, 0:E].unsqueeze(1).to_broadcast([GT, NG, E]), float(BS),
                    PS[0:GT, 7, 0:NG * E].rearrange("p (g e) -> p g e", g=NG), ALU.mult, ALU.add))
                for k in range(2):
                    c(nc.vector.tensor_tensor(sel[:, k, :, 0:E], sel[:, k, :, 0:E], slote[:, :, 0:E], ALU.mult))
                    c(nc.vector.tensor_reduce(slotf[:, k, :], sel[:, k, :, 0:E], AX.X, ALU.add))
                nc.vector.tensor_copy(slot[:, :, :], slotf[:, :, :]).then_inc(sem(p + "slot"), 1)

            def experts_dve(L):
                p, H = f"m{L}_", HC[L]
                dve.wait_ge(sem(p + "first"), 1)
                blocks = dve.value_load(firsti[0:1, EX[L]:EX[L] + 1], min_val=1, max_val=MAXB[L])
                with dve.Fori(0, blocks) as b:
                    for c in range(H):
                        dve.wait_ge(sem(p + "sg"), b * H + (c + 1))
                        nc.vector.tensor_tensor(hT[:, c, :], sg[:, c, :], PS[:, GUB[c], BS:2 * BS], ALU.mult)\
                            .then_inc(sem(p + "h"), 1)
                    dve.wait_ge(sem(p + "y_ps"), b + 1)
                    dve.wait_ge(sem(p + "y_out"), b * 16 + 16)
                    nc.vector.tensor_copy(yo[:, :], PS[0:BS, 5, 0:DIM]).then_inc(sem(p + "y"), 1)
                for g in range(NG):
                    dve.wait_ge(sem(f"back{g}"), 32 * (L + 1))
                    for k in range(2):
                        nc.vector.scalar_tensor_tensor(h[:, g, :], yg[:, k, g, :], share[:, k, g:g + 1], h[:, g, :],
                                                       ALU.mult, ALU.add).then_inc(sem(p + "res"), 1)
                        dve.wait_ge(sem(p + "res"), 2 * g + k + 1)
                    if L == 0:
                        stat(3, h, g)

            norm(2, h, y)
            evict_xnT(2)
            route(0)
            experts_dve(0)
            norm(3, h, y)
            evict_xnT(3)
            nc.vector.memset(vr[:, :, :, HD:HD + 1], 1.0).then_inc(sem("r_v1"), 1)
            c = Chain(dve, sem("r_chain"))
            for i in range(4):
                gs = slice(2 * i, 2 * i + 2)
                dve.wait_ge(sem("r_sf"), 2 * i + 2)
                nc.vector.tensor_reduce(ssum[:, gs, :], sf[:, gs, :, :], AX.X, ALU.add).then_inc(sem("r_chain"), 1)
                nc.vector.tensor_reduce(smax[:, gs, 0:NH], sf[:, gs, 0:NH, :], AX.X, ALU.max)\
                    .then_inc(sem("r_chain"), 1)
                nc.vector.tensor_reduce(kmax[:, gs], sf[:, gs, NH:2 * NH, :], AX.XY, ALU.max)\
                    .then_inc(sem("r_chain"), 1)
                c.n += 3
                dve.wait_ge(sem("r_chain"), c.n)
                nc.vector.scalar_tensor_tensor(smax[:, gs, 0:NH], ssum[:, gs, 0:NH], 0.5, smax[:, gs, 0:NH],
                                               ALU.mult, ALU.add).then_inc(sem("r_chain"), 1)
                nc.vector.scalar_tensor_tensor(smax[:, gs, NH:2 * NH], ssum[:, gs, NH:2 * NH], 0.5,
                                               kmax[:, gs].unsqueeze(2).to_broadcast([GT, 2, NH]),
                                               ALU.mult, ALU.add).then_inc(sem("r_chain"), 1)
                c.n += 2
                dve.wait_ge(sem("r_chain"), c.n)
                nc.vector.tensor_tensor(sf[:, gs, :, :], sf[:, gs, :, :],
                                        smax[:, gs, :].unsqueeze(3).to_broadcast([GT, 2, 2 * NH, HD]), ALU.subtract)\
                    .then_inc(sem("r_arg"), 1)
            nc.vector.tensor_tensor(h[:, :, :], h[:, :, :], bias[:, 1:2, :].to_broadcast([GT, NG, DIM]), ALU.add)\
                .then_inc(sem("r_h"), 1)
            dve.wait_ge(sem("r_h"), 1)
            dve.wait_ge(sem("r_vr"), NG)
            values = vr[:, :, :, 0:HD]
            nc.vector.tensor_tensor(values, values, bias[:, 2, :].rearrange("p (h d) -> p h d", h=NH).unsqueeze(1)
                                    .to_broadcast([GT, NG, NH, HD]), ALU.add).then_inc(sem("r_v1"), 1)

            def mask_r(g, par):
                dve.wait_ge(sem("r_qk"), g + 1)
                nc.vector.tensor_tensor(r_p[:, par, :, :].rearrange("p (a b) t -> p a b t", a=2),
                                        PS[0:GT, 0:2, 0:432].rearrange("p a (b t) -> p a b t", b=6),
                                        causal01.unsqueeze(1).unsqueeze(1).to_broadcast([GT, 2, 6, GT]), ALU.mult)\
                    .then_inc(sem("r_p"), 1)

            def out_r(g):
                dve.wait_ge(sem("r_av"), g + 1)
                c = Chain(dve, sem("r_chain2"), g * 2)
                o3 = PS[0:GT, 2, 0:NH * (HD + 1)].rearrange("p (h d) -> p h d", h=NH)
                c(nc.vector.tensor_scalar(r_den[:, :], o3[:, :, HD], 1e-6, None, ALU.add))
                c(nc.vector.reciprocal(r_den[:, :], r_den[:, :]))
                nc.vector.tensor_tensor(r_a[:, :, :], o3[:, :, 0:HD],
                                        r_den[:, :].unsqueeze(2).to_broadcast([GT, NH, HD]), ALU.mult)\
                    .then_inc(sem("r_a"), 1)

            def res_r(g):
                dve.wait_ge(sem("r_proj"), g + 1)
                nc.vector.tensor_tensor(h[:, bass.ds(g, 1), :], h[:, bass.ds(g, 1), :],
                                        PS[0:GT, 4:5, 0:DIM], ALU.add).then_inc(sem("r_h"), 1)
                dve.wait_ge(sem("r_h"), g + 2)
                stat(4, h, g)

            def step_r(g, par, first=False, second=False, last=False):
                if not first:
                    out_r(g - 1)
                if not first and not second:
                    res_r(g - 2)
                if not last:
                    mask_r(g + 1, 1 - par)
            mask_r(0, 0)
            step_r(0, 0, first=True)
            step_r(1, 1, second=True)
            with dve.Fori(1, NG // 2 - 1) as n:
                step_r(n * 2, 0)
                step_r(n * 2 + 1, 1)
            step_r(NG - 2, 0)
            step_r(NG - 1, 1, last=True)
            out_r(NG - 1)
            res_r(NG - 2)
            res_r(NG - 1)
            norm(4, h, y)
            for g in range(NG):
                dve.wait_ge(sem(("ln_even", "ln_odd")[g % 2]), 3 * NG // 2 + g // 2 + 1)
                stat(5, y, g)
            norm(5, y, rn, True)
            evict_xnT(5, w1n)
            nc.vector.memset(vb[:, :, :, QD:QD + 1], 1.0).then_inc(sem("b_v1"), 1)
            nc.vector.memset(b_m[:, :], 0.0).then_inc(sem("b_v1"), 1)
            nc.vector.memset(b_kz[:, :, :, :, :], 0.0).then_inc(sem("b_v1"), 1)
            dve.wait_ge(sem("b_v1"), 3)
            nc.vector.tensor_copy(b_m[:, QH:QH + GT], maskb[:, 1, :]).then_inc(sem("b_hin"), 1)
            cos, sin = (t[:, 0:N].unsqueeze(1).to_broadcast([128, 8, N]) for t in (rcos, rsin))
            for n in range(2 * BT):
                dve.wait_ge(sem("b_x"), n + 1)
                if n >= 2:
                    dve.wait_ge(sem("b_r"), n - 1)
                nc.vector.tensor_tensor(rt[:, n % 2, 0, :].rearrange("p (b n) -> p b n", n=N),
                                        qkx[:, n % 2, :].rearrange("p (b n) -> p b n", n=N), cos, ALU.mult)
                dve.wait_ge(sem("b_swap"), n + 1)
                nc.vector.tensor_tensor(rt[:, n % 2, 1, :].rearrange("p (b n) -> p b n", n=N),
                                        PS[:, 6 + n % 2, 0:288].rearrange("p (b n) -> p b n", n=N), sin, ALU.mult)\
                    .then_inc(sem("b_rope"), 1)
            dve.wait_ge(sem("b_r"), 2 * BT)
            dve.wait_ge(sem("b_hin"), 1)

            def in_b(g, par):
                nc.vector.tensor_copy(b_q[:, par, :, :], rqk[:, 0:QT, bass.ts(g, GT)]).then_inc(sem("b_in"), 1)
                for a in range(2):
                    half = slice(64 * a, 64 * a + 64)
                    nc.vector.tensor_copy(b_kz[half, par, :, a, :], rqk[half, QT:BT, bass.ts(g, GT)])\
                        .then_inc(sem("b_in"), 1)

            def max_b(g):
                dve.wait_ge(sem("att_s1"), g + (NG + 1))
                nc.vector.tensor_reduce(b_m[:, 0:QH].rearrange("p (a b) -> p a b", a=2),
                                        PS[0:GT, 0:2, 0:432].rearrange("p a (b k) -> p a b k", k=GT),
                                        AX.X, ALU.max, negate=True).then_inc(sem("att_max"), 1)

            def out_b(g):
                dve.wait_ge(sem("att_av"), g + (NG + 1))
                o4 = PS[0:GT, 6:8, 0:390].rearrange("p a (h d) -> p a h d", h=6)
                nc.vector.reciprocal(b_rec[:, :].rearrange("p (a h) -> p a h", a=2), o4[:, :, :, QD])\
                    .then_inc(sem("att_rec"), 1)
                dve.wait_ge(sem("att_rec"), g + (NG + 1))
                nc.vector.tensor_tensor(b_o[:, :, :].rearrange("p (a h) d -> p a h d", a=2), o4[:, :, :, 0:QD],
                                        b_rec[:, :].rearrange("p (a h) -> p a h", a=2).unsqueeze(3)
                                        .to_broadcast([GT, 2, 6, QD]), ALU.mult).then_inc(sem("att_o"), 1)

            def res_b(g):
                dve.wait_ge(sem("b_proj"), g + 1)
                nc.vector.tensor_tensor(y[:, bass.ds(g, 1), :], y[:, bass.ds(g, 1), :], PS[0:GT, 5:6, 0:DIM],
                                        ALU.add).then_inc(sem("b_hin"), 1)
                dve.wait_ge(sem("b_hin"), g + 2)
                stat(6, y, g)

            def step_b(g, par, first=False, second=False, last=False):
                if not first:
                    out_b(g - 1)
                if not last:
                    in_b(g + 1, 1 - par)
                if not first and not second:
                    res_b(g - 2)
                if not last:
                    max_b(g + 1)
            in_b(0, 0)
            max_b(0)
            step_b(0, 0, first=True)
            step_b(1, 1, second=True)
            with dve.Fori(1, NG // 2 - 1) as n:
                step_b(n * 2, 0)
                step_b(n * 2 + 1, 1)
            step_b(NG - 2, 0)
            step_b(NG - 1, 1, last=True)
            out_b(NG - 1)
            res_b(NG - 2)
            res_b(NG - 1)
            norm(6, y, rn, True)
            evict_xnT(6, w2n)
            for g in range(NG):
                nc.vector.tensor_tensor(h[:, g, :], h[:, g, :], y[:, g, :], ALU.add).then_inc(sem("b_h"), 1)
            dve.wait_ge(sem("b_h"), NG)
            route(1)
            experts_dve(1)
            nc.vector.tensor_copy(tmpg[:, :], rstd[:, :]).then_inc(sem("h_last"), 1)

        @block.tensor
        def _(pe):
            mm = nc.tensor.matmul
            def stoke(bank, n):
                for _ in range(n):
                    mm(PS[:, bank, 0:7 * GT], identb[:, :], headsel[:, 0:7, :], start=True, stop=True)

            def keep_busy(*reached):
                for name, value in reached:
                    pe.wait_ge(sem(name), value)
                    stoke(7, 6)

            def square_sums(c):
                pe.wait_ge(sem("t_sq"), c + 1)
                for g in range(NG):
                    o = (g % 2) * 194
                    last = mm(PS[0:GT, g // 2, o + DIM + 1:o + DIM + 2], xsq[:, c % 4, bass.ts(g, GT)],
                              wc[:, c, DIM:DIM + 1], start=False, stop=(c == FC - 1), skip_group_check=True)
                last.then_inc(sem("t_used"), 1)

            pe.wait_ge(sem("gb_in"), 32)
            for c in range(FC):
                pe.wait_ge(sem(f"tok_in{c}"), 32)
                pe.wait_ge(sem("t_wc"), 2 * c + 2)
                for g in range(NG):
                    o = (g % 2) * 194
                    mm(PS[0:GT, g // 2, o:o + DIM + 1], xw[:, c, bass.ts(g, GT)], wc[:, c, :],
                       start=(c == 0 and g % 2 == 0), stop=(c == FC - 1), skip_group_check=True)
                if c >= 3:
                    square_sums(c - 3)
            for c in range(FC - 3, FC):
                square_sums(c)
            pe.wait_ge(sem("t_wcs"), FC - 1)
            mm(PS[0:GT, 4, 0:DIM], ones[0:FP, 0:GT], wcs[:, :], start=True, stop=True, skip_group_check=True)
            pe.wait_ge(sem("t_wbd"), (FC - BC) * SH)
            mm(PS[0:GT, 4, DIM:2 * DIM], ones[0:FP, 0:GT], wbd[:, :], start=False, stop=False,
               skip_group_check=True)
            pe.wait_ge(sem("t_wbs"), BC - 1)
            mm(PS[0:GT, 4, DIM:2 * DIM], ones[0:FP, 0:GT], wb[:, 0, :], start=False, stop=False,
               skip_group_check=True)
            mm(PS[0:GT, 4, DIM:2 * DIM], ones[0:1, 0:GT], brow[:, :], start=False, stop=True,
               skip_group_check=True).then_inc(sem("t_gsum"), 1)

            def transpose_xn(k, src=y):
                for b in range(4):
                    hf, q = b // 2, b % 2
                    for i in range(4):
                        g = 4 * q + i
                        pe.wait_ge(sem(("ln_even", "ln_odd")[g % 2]), (k - 1) * NG // 2 + g // 2 + 1)
                        last = nc.tensor.transpose(PS[0:HB, b, i * GT:(i + 1) * GT],
                                                   src[:, g, hf * HB:(hf + 1) * HB], ident[0:GT, 0:GT])
                    last.then_inc(sem("ln_T"), 1)

            pe.wait_ge(sem("bf_in"), 80)
            keep_busy(("t_inv", 1), ("t_h", NG // 2 + 2), ("t_h", NG // 2 + NG), ("ln_stat", NG), ("ln_inv", 1))
            transpose_xn(1)
            pe.wait_ge(sem("pads"), 3)
            pe.wait_ge(sem("wA_in"), 48)
            pe.wait_ge(sem("xnT"), 4)
            for j in range(2 * NJ):
                for q in range(2):
                    n = 2 * j + q
                    if n >= 2:
                        if n - 2 < 2 * NJ:
                            pe.wait_ge(sem("a_qT"), n - 1)
                        else:
                            pe.wait_ge(sem("a_ka"), n - 1 - 2 * NJ)
                    for k in range(2):
                        last = mm(PS[:, 4 + n % 2, 0:288], wA[:, k, j * 128:(j + 1) * 128],
                                  xnT[:, k, q * 288:(q + 1) * 288], start=(k == 0), stop=(k == 1))
                    last.then_inc(sem("a_qk"), 1)
            pe.wait_ge(sem("posk_in"), 16)
            pe.wait_ge(sem("bf_in"), 80)
            pe.wait_ge(sem("a_qT"), 2 * NJ)
            pe.wait_ge(sem("a_ka"), 2 * NJ)
            qn = qT[:, :, :].rearrange("p j (b n) -> p n j b", n=N)
            for n in range(N):
                i = n % 9
                last = mm(PS[:, 2 + n // 9, i * 48:(i + 1) * 48].rearrange("p (j b) -> p j b", j=NJ),
                          posk[:, n, :], qn[:, n, :, :], start=True, stop=True)
                if i == 8:
                    last.then_inc(sem("a_pos"), 1)
            for g in range(NG):
                if g >= 2:
                    pe.wait_ge(sem("a_va"), g - 1)
                for k in range(2):
                    last = mm(PS[0:GT, g % 2, 0:DIM], xnT[:, k, bass.ts(g, GT)], wV0[:, k, :],
                              start=(k == 0), stop=(k == 1))
                last.then_inc(sem("a_v"), 1)
            pe.wait_ge(sem("a_qa"), 4)
            pe.wait_ge(sem("a_va"), NG)

            def s1_a(g, par):
                pe.wait_ge(sem("a_in"), 4 * g + 4)
                for a in range(2):
                    mm(PS[0:GT, a, 0:432], identb[0:GT, 0:GT], maskb[:, 0:1, :].to_broadcast([GT, 6, GT]),
                       start=True, stop=False, skip_group_check=True)
                for j, r, n, a, at in PIECES:
                    last = mm(PS[0:GT, a, at * GT:(at + n) * GT], a_q[:, par, j, :], a_kz[:, par, j, r:r + n, :],
                              start=False, stop=True, skip_group_check=True)
                last.then_inc(sem("att_s1"), 1)

            def maxT(m, bank):
                nc.tensor.transpose(PS[:, bank, 432:468].bitcast(bf16), m[:, :], identb[0:GT, 0:GT])\
                    .then_inc(sem("att_mt_ps"), 1)

            def oT_a(g):
                pe.wait_ge(sem("att_o"), g + 1)
                for j in range(NJ):
                    last = nc.tensor.transpose(PS[:, 2, j * GT:(j + 1) * GT],
                                               a_o[:, 4 * j:4 * j + 4, :], ident[0:GT, 0:GT])
                last.then_inc(sem("a_oT"), 1)

            def step_a(g, par, first=False, last=False):
                pe.wait_ge(sem("att_max"), g + 1)
                maxT(a_m, 4)
                pe.wait_ge(sem("a_qz"), 4 * g + 4)
                for j, r, n, a, at in PIECES:
                    if j == 1 and a == 1:
                        pe.wait_ge(sem("att_mt"), g + 1)
                    mm(PS[0:GT, 3 + a, at * GT:(at + n) * GT], a_k[:, par, j, :], a_qz[:, par, j, r:r + n, :],
                       start=(at == 0), stop=False, skip_group_check=True)
                for hh in range(NH):
                    ins_ = mm(PS[0:GT, 3 + hh // 6, hh % 6 * GT:(hh % 6 + 1) * GT], headsel[:, hh, :], a_mT[:, :],
                              start=False, stop=True, skip_group_check=True)
                ins_.then_inc(sem("att_s2"), 1)
                if not first:
                    oT_a(g - 1)
                if not last:
                    s1_a(g + 1, 1 - par)
                pe.wait_ge(sem("att_exp"), g + 1)
                for hh in range(NH):
                    ins_ = mm(PS[0:GT, 7, hh * 32:(hh + 1) * 32], a_p[:, hh, :],
                              va[:, bass.ds(g, 1), hh, :], start=True, stop=True)
                ins_.then_inc(sem("att_av"), 1)
            s1_a(0, 0)
            pipelined(pe, step_a)
            pe.wait_ge(sem("a_oaT"), NG - 1)
            oT_a(NG - 1)
            stoke(6, 6)
            pe.wait_ge(sem("a_oaT"), NG)
            pe.wait_ge(sem("posv_in"), 16)
            on = oaT[:, :, :].rearrange("p j (b n) -> p n j b", n=N)
            for n in range(N):
                i = n % 9
                last = mm(PS[0:64, n // 9, i * 48:(i + 1) * 48].rearrange("p (j b) -> p j b", j=NJ),
                          posv[:, n, :], on[:, n, :, :], start=True, stop=True)
                if i == 8:
                    last.then_inc(sem("a_pos2"), 1)
            pe.wait_ge(sem("a_of"), 4)
            for g in range(NG):
                if g >= 2:
                    pe.wait_ge(sem("a_res"), g)
                for j in range(NJ):
                    last = mm(PS[0:GT, 4 + g % 2, 0:DIM], of[:, j, bass.ts(g, GT)], wP0[:, j, :],
                              start=(j == 0), stop=(j == NJ - 1))
                last.then_inc(sem("a_proj"), 1)

            def route_pe(L):
                p, E = f"m{L}_", EX[L]
                pe.wait_ge(sem("rw_in"), 32)
                pe.wait_ge(sem("pads"), 12)
                for g in range(NG):
                    for k in range(2):
                        last = mm(PS[0:GT, 6, g * E:(g + 1) * E], xnT[:, k, bass.ts(g, GT)], RW[L][:, k, :],
                                  start=(k == 0), stop=(k == 1))
                last.then_inc(sem("route_logits"), 1)
                pe.wait_ge(sem("route_sel"), L + 1)
                mm(PS[0:GT, 7, 0:NG * E], tri[:, :], selb[:, :, 0:E], start=True, stop=False,
                   skip_group_check=True)
                for g in range(NG - 1):
                    mm(PS[0:GT, 7, (g + 1) * E:NG * E], oneb[:, :],
                       selb[:, g:g + 1, 0:E].to_broadcast([GT, NG - 1 - g, E]), start=False, stop=(g == NG - 2),
                       skip_group_check=True)
                for g in range(NG):
                    last = mm(PS[0:GT, 5, 0:E], oneb[:, :], selb[:, g, 0:E], start=(g == 0), stop=(g == NG - 1))
                last.then_inc(sem("route_pos"), 1)

            def experts_pe(L):
                p, H = f"m{L}_", HC[L]
                pe.wait_ge(sem(p + "first"), 1)

                def block_T():
                    for k in range(2):
                        last = nc.tensor.transpose(PS[0:HB, 4, k * BS:(k + 1) * BS], bx[:, k * HB:(k + 1) * HB],
                                                   ident[0:BS, 0:BS])
                    last.then_inc(sem(p + "xT_ps"), 1)
                pe.wait_ge(sem(p + "slot"), 1)
                with pe.Fori(0, 11) as _:
                    stoke(7, 7)
                pe.wait_ge(sem(p + "x_in"), 16)
                block_T()
                R = RING[L]
                with pe.Fori(0, EX[L] // R) as q:
                    _, ends = nc.values_load_multi_w_load_instructions(firsti[0:1, bass.ds(q * R, R + 1)], engines=[mybir.EngineType.PE], min_val=0,
                                          max_val=MAXB[L])
                    for r in range(R):
                        lo, hi = ends[r], ends[r + 1]
                        with pe.Fori(lo, hi) as b:
                            pe.wait_ge(sem(p + f"w{r}"), q * 32 + 32)
                            pe.wait_ge(sem(p + "xT"), b * 2 + 2)
                            for c in range(H):
                                for u in range(2):
                                    o = (u * H + c) * 128
                                    for k in range(2):
                                        last = mm(PS[:, GUB[c], u * BS:(u + 1) * BS],
                                                  WGU[L][:, r, k, o:o + 128], bxT[:, k, :],
                                                  start=(k == 0), stop=(k == 1))
                                last.then_inc(sem(p + "gu"), 1)
                            pe.wait_ge(sem(p + "x_in"), b * 16 + 32)
                            block_T()
                            for c in range(H):
                                pe.wait_ge(sem(p + "h"), b * H + (c + 1))
                                last = mm(PS[0:BS, 5, 0:DIM], hT[:, c, :], WD[L][:, r, c, :],
                                          start=(c == 0), stop=(c == H - 1))
                            last.then_inc(sem(p + "y_ps"), 1)

            keep_busy(("ln_agg", 2 * NG))
            transpose_xn(2)
            pe.wait_ge(sem("xnT"), 8)
            route_pe(0)
            experts_pe(0)
            pe.wait_ge(sem("l1_in"), 16 * 8)

            keep_busy(*((f"back{g}", 32) for g in range(2, NG)), ("ln_stat", 3 * NG), ("ln_inv", 3))
            transpose_xn(3)
            pe.wait_ge(sem("xnT"), 12)
            for q in range(2):
                for m in range(4):
                    n = 4 * q + m
                    if n >= 2:
                        pe.wait_ge(sem("r_cT"), n - 1)
                    for k in range(2):
                        last = mm(PS[0:HB, 4 + n % 2, 0:288], wC1[:, k, m * HB:(m + 1) * HB],
                                  xnT[:, k, q * 288:(q + 1) * 288], start=(k == 0), stop=(k == 1))
                    last.then_inc(sem("r_c"), 1)
                stoke(7, 6)
                pe.wait_ge(sem("r_cT"), 4 * q + 4)
                for g in range(4 * q, 4 * q + 4):
                    if g >= 2:
                        pe.wait_ge(sem("r_sf"), g - 1)
                    for m in range(4):
                        last = mm(PS[0:GT, g % 2, m * HB:(m + 1) * HB], cT[:, m, bass.ts(g, GT)], wF1[:, :],
                                  start=True, stop=True)
                    last.then_inc(sem("r_s"), 1)

            def features_T(q):
                pe.wait_ge(sem("r_exp"), q + 1)
                for m in range(4):
                    b = 4 * q + m
                    if b >= 2:
                        pe.wait_ge(sem("r_fT"), b - 1)
                    for i in range(4):
                        last = nc.tensor.transpose(PS[0:HB, 4 + b % 2, i * GT:(i + 1) * GT],
                                                   sf[:, 4 * q + i, 6 * m:6 * m + 6, :], ident[0:GT, 0:GT])
                    last.then_inc(sem("r_fT_ps"), 1)
            for g in range(NG):
                if g >= 2:
                    pe.wait_ge(sem("r_vr"), g - 1)
                for k in range(2):
                    last = mm(PS[0:GT, 2 + g % 2, 0:DIM], xnT[:, k, bass.ts(g, GT)], wV1[:, k, :],
                              start=(k == 0), stop=(k == 1))
                last.then_inc(sem("r_v"), 1)

            features_T(0)
            pe.wait_ge(sem("r_v1"), 2)
            pe.wait_ge(sem("pads"), 14)

            def qk_r(g, par):
                pe.wait_ge(sem("r_in"), 3 * g + 3)
                for i in range(2):
                    last = mm(PS[0:GT, i, 0:432], r_k[:, par, i, :], r_qz[:, par, i, :, :], start=True, stop=True)
                last.then_inc(sem("r_qk"), 1)

            def aT_r(g):
                pe.wait_ge(sem("r_a"), g + 1)
                for i in range(2):
                    last = nc.tensor.transpose(PS[0:HB, 3, i * GT:(i + 1) * GT], r_a[:, 6 * i:6 * i + 6, :],
                                               ident[0:GT, 0:GT])
                last.then_inc(sem("r_aT_ps"), 1)

            def proj_r(g):
                pe.wait_ge(sem("r_aT"), g + 1)
                pe.wait_ge(sem("r_h"), g + 1)
                for i in range(2):
                    last = mm(PS[0:GT, 4, 0:DIM], r_aT[:, i, :], wO1[:, i, :], start=(i == 0), stop=(i == 1))
                last.then_inc(sem("r_proj"), 1)

            def step_r(g, par, first=False, last=False):
                pe.wait_ge(sem("r_p"), g + 1)
                if not last:
                    qk_r(g + 1, 1 - par)
                if not first:
                    aT_r(g - 1)
                for hh in range(NH):
                    ins_ = mm(PS[0:GT, 2, hh * (HD + 1):(hh + 1) * (HD + 1)], r_p[:, par, hh, :],
                              vr[:, bass.ds(g, 1), hh, :], start=True, stop=True)
                ins_.then_inc(sem("r_av"), 1)
                if not first:
                    proj_r(g - 1)
            pe.wait_ge(sem("r_vr"), NG)
            qk_r(0, 0)
            features_T(1)
            pe.wait_ge(sem("r_fT"), 8)
            pipelined(pe, step_r)
            aT_r(NG - 1)
            proj_r(NG - 1)

            keep_busy(("ln_stat", 4 * NG), ("ln_inv", 4), ("ln_stat", 5 * NG - 4), ("ln_stat", 5 * NG), ("ln_inv", 5))
            transpose_xn(5, rn)
            pe.wait_ge(sem("xnT"), 16)
            def project(n):
                t, q = n // 2, n % 2
                if n >= 2:
                    pe.wait_ge(sem("b_x"), n - 1)
                for k in range(2):
                    last = mm(PS[:, 4 + n % 2, 0:288], wQ2[:, k, t * 128:(t + 1) * 128],
                              xnT[:, k, q * 288:(q + 1) * 288], start=(k == 0), stop=(k == 1))
                last.then_inc(sem("b_x_ps"), 1)
            project(0)
            for n in range(2 * BT):
                if n + 1 < 2 * BT:
                    project(n + 1)
                pe.wait_ge(sem("b_x"), n + 1)
                if n >= 2:
                    pe.wait_ge(sem("b_rope"), n - 1)
                mm(PS[:, 6 + n % 2, 0:288], swap[:, :], qkx[:, n % 2, :], start=True, stop=True)\
                    .then_inc(sem("b_swap"), 1)
            for g in range(NG):
                if g >= 2:
                    pe.wait_ge(sem("b_vb"), g - 1)
                for k in range(2):
                    last = mm(PS[0:GT, g % 2, 0:KVH * QD], xnT[:, k, bass.ts(g, GT)], wV2[:, k, :],
                              start=(k == 0), stop=(k == 1))
                last.then_inc(sem("b_v"), 1)
            pe.wait_ge(sem("b_vb"), NG)

            def s1_b(g, par):
                pe.wait_ge(sem("b_in"), 3 * g + 3)
                for a in range(2):
                    mm(PS[0:GT, a, 0:432], identb[0:GT, 0:GT], maskb[:, 1:2, :].to_broadcast([GT, 6, GT]),
                       start=True, stop=False, skip_group_check=True)
                for t in range(QT):
                    last = mm(PS[0:GT, t // 3, t % 3 * 2 * GT:(t % 3 + 1) * 2 * GT], b_q[:, par, t, :],
                              b_kz[:, par, t // 2, :, :], start=False, stop=True, skip_group_check=True)
                last.then_inc(sem("att_s1"), 1)

            def oT_b(g):
                pe.wait_ge(sem("att_o"), g + (NG + 1))
                for c in range(6):
                    last = nc.tensor.transpose(PS[:, 2, c * GT:(c + 1) * GT], b_o[:, 2 * c:2 * c + 2, :],
                                               ident[0:GT, 0:GT])
                last.then_inc(sem("b_oT_ps"), 1)

            def proj_b(g):
                pe.wait_ge(sem("b_oT"), g + 1)
                pe.wait_ge(sem("b_hin"), g + 1)
                for c in range(6):
                    last = mm(PS[0:GT, 5, 0:DIM], b_oT[:, c, :], wO2[:, c, :], start=(c == 0), stop=(c == 5))
                last.then_inc(sem("b_proj"), 1)

            def step_b(g, par, first=False, last=False):
                pe.wait_ge(sem("att_max"), g + (NG + 1))
                maxT(b_m, 2)
                for j in range(KVH):
                    for a in range(2):
                        h0 = 4 * j + a
                        if h0 // 6 == (h0 + 2) // 6:
                            both = PS[0:GT, 3 + h0 // 6, 0:432].rearrange("p (b k) -> p b k", k=GT)
                            mm(both[:, h0 % 6:h0 % 6 + 3:2, :], b_kz[:, par, j, a, :], b_q[:, par, 2 * j:2 * j + 2, :],
                               start=(h0 % 6 == 0), stop=False, skip_group_check=True)
                        else:
                            for i in range(2):
                                hh = h0 + 2 * i
                                mm(PS[0:GT, 3 + hh // 6, hh % 6 * GT:(hh % 6 + 1) * GT], b_kz[:, par, j, a, :],
                                   b_q[:, par, 2 * j + i, :], start=(hh % 6 == 0), stop=False,
                                   skip_group_check=True)
                pe.wait_ge(sem("att_mt"), g + (NG + 1))
                for hh in range(QH):
                    ins_ = mm(PS[0:GT, 3 + hh // 6, hh % 6 * GT:(hh % 6 + 1) * GT], headsel[:, hh, :], b_mT[:, :],
                              start=False, stop=True, skip_group_check=True)
                ins_.then_inc(sem("att_s2"), 1)
                if not first:
                    oT_b(g - 1)
                if not last:
                    s1_b(g + 1, 1 - par)
                pe.wait_ge(sem("att_exp"), g + (NG + 1))
                for hh in range(QH):
                    ins_ = mm(PS[0:GT, 6 + hh // 6, hh % 6 * (QD + 1):(hh % 6 + 1) * (QD + 1)], b_p[:, hh, :],
                              vb[:, bass.ds(g, 1), hh // 4, :], start=True, stop=True)
                ins_.then_inc(sem("att_av"), 1)
                if not first:
                    proj_b(g - 1)
            s1_b(0, 0)
            pipelined(pe, step_b)
            oT_b(NG - 1)
            proj_b(NG - 1)
            keep_busy(("ln_agg", 6 * NG))
            transpose_xn(6, rn)
            pe.wait_ge(sem("xnT"), 20)
            route_pe(1)
            experts_pe(1)


def layouts(inputs):
    import numpy as np
    f = np.float32
    a = {k: np.asarray(v) for k, v in inputs.items()}
    d = {}
    feats = [(u, v, c) for u in range(18) for v in range(18) if not (u in (0, 17) and v in (0, 17)) for c in range(CH)]
    pad = np.zeros((B, CH, IMG + 2, IMG + 2), f)
    pad[:, :, 1:-1, 1:-1] = a["x"]
    fu, fv, fc = (np.array(t) for t in zip(*feats))
    at = PATCH * np.arange(GRID)
    win = pad[:, fc[:, None, None], fu[:, None, None] + at[None, :, None], fv[:, None, None] + at[None, None, :]]
    d["xw"] = win.transpose(1, 0, 2, 3).reshape(FC, FP, TOK).transpose(1, 0, 2)
    shifts = [(1, 1), (1, 0), (1, 2), (0, 1), (2, 1)]
    w5 = np.zeros((FC * FP, SH, DIM), f)
    gb = np.zeros((2, FC * FP, SH), f)
    count = np.zeros(FC * FP, f)
    for s, (du, dv) in enumerate(shifts):
        i, j = fu - du, fv - dv
        ok = (i >= 0) & (i < PATCH) & (j >= 0) & (j < PATCH)
        row = ((i * PATCH + j) * SH * CH + s * CH + fc)[ok]
        w5[ok, s] = a["L0_tok_w"][row]
        gb[0, ok, s] = a["L0_tok_ln_gamma"][row]
        gb[1, ok, s] = a["L0_tok_ln_beta"][row]
        count[ok] += 1
    d["w5"] = w5.reshape(FC, FP, SH, DIM).transpose(1, 0, 2, 3)
    d["gb5"] = gb.reshape(2, FC, FP, SH).transpose(2, 0, 1, 3).reshape(FP, 2, FC * SH)
    d["tok_b"] = a["L0_tok_b"][None, :]
    d["ident"] = np.eye(128, dtype=f)
    d["identb"] = np.eye(128).astype(f)
    cst = np.zeros((128, 768), f)
    cst[:, 0:4] = np.arange(128)[:, None] // 32 == np.arange(4)
    cst[:HB, 4:10] = np.arange(HB)[:, None] // 16 == np.arange(6)
    cst[:FP, 16:24] = count.reshape(FC, FP).T
    L = N - 1
    side = int(L ** 0.5)
    r_ = np.arange(L)
    krow = np.zeros((16, N), f)
    krow[0:7, 1:] = r_ // side == np.arange(7)[:, None]
    krow[7:12, 1:] = r_ % side == np.arange(5)[:, None]
    krow[12:14, 0] = 1
    for r in range(4):
        cst[32 * r + 16:32 * r + 32, 32:68] = krow
    vrow = np.concatenate([krow, krow], axis=1).T.copy()
    vrow[:, 14] = 1
    cst[:GT, 68:84] = vrow
    img, pos = np.arange(GT) // N, np.arange(GT) % N
    same = img[:, None] == img[None, :]
    before = same & (pos[None, :] <= pos[:, None])
    cst[:GT, 96:168] = before.T
    freq = (1.0 / f(10000.0) ** (np.arange(0, QD, 2, dtype=f) / f(QD))).astype(f)
    ang = (pos[None, :].astype(f) * np.tile(freq, 4)[:, None]).astype(f)
    cst[:, 168:240] = np.cos(ang)
    cst[:, 240:312] = np.sin(ang) * np.where(np.arange(128) // 32 % 2 == 0, -1, 1)[:, None].astype(f)
    cst[:, 312:320] = np.arange(8)
    cst[:, 320:336] = np.arange(16)
    cst[:, 336:464] = 1
    cst[:, 464] = EPS_LN
    cst[:, 465] = EPS_RMS
    cst[:, 24] = f(1e-6) * f(HD ** -0.5)
    cst[:HB, 466:468] = a["L1_ffn_norm1_w"].reshape(2, HB).T
    cst[:HB, 468:470] = a["L1_ffn_norm2_w"].reshape(2, HB).T
    cst[:HB, 470:474] = a["L1_attn_b_inp"][:2 * DIM].reshape(4, HB).T
    cst[:, 474:474 + NTHR] = BS * np.arange(1, NTHR + 1)
    cst[:, 480:480 + (E1 + 1) * E1] = (np.arange(E1)[None, :] < np.arange(E1 + 1)[:, None]).reshape(-1)
    d["cst"] = cst
    d["tri"] = (np.arange(GT)[:, None] < np.arange(GT)[None, :]).astype(f)
    d["oneb"] = np.ones((GT, GT)).astype(f)
    d["rw0"] = a["L0_ffn_router_w"].T.reshape(2, HB, E0).transpose(1, 0, 2)
    d["rw1"] = a["L1_ffn_w_router"].reshape(2, HB, E1).transpose(1, 0, 2)
    wgu = np.concatenate([a["L0_ffn_Wg"], a["L0_ffn_Wu"]], 1)
    d["wgu0"] = wgu.transpose(0, 2, 1).reshape(E0, 2, HB, 2 * F0).transpose(0, 2, 1, 3)
    d["wd0"] = a["L0_ffn_Wd"].transpose(0, 2, 1).reshape(E0, 6, 128, DIM).transpose(0, 2, 1, 3)
    d["wgu1"] = a["L1_ffn_w_gate_up"].reshape(E1, 2, HB, 2 * F1).transpose(0, 2, 1, 3)
    d["wd1"] = a["L1_ffn_w_down"].reshape(E1, 3, 128, DIM).transpose(0, 2, 1, 3)
    d["maskb"] = np.stack([np.where(same, 0, NEG), np.where(before, 0, NEG)], 1).astype(f)
    hs = np.zeros((128, NH, GT), f)
    hs[np.arange(NH), np.arange(NH)] = 1
    for k in range(GT):
        hs[NH + k, :, k] = 1
    d["headsel"] = hs.astype(f)
    d["bias"] = np.broadcast_to(np.stack([a["L0_attn_b_proj"], a["L1_attn_b_out"],
                                          a["L1_attn_b_inp"][2 * DIM:]])[None], (GT, 3, DIM))
    wq = a["L0_attn_w_qkv"].reshape(2, HB, 3, NH, HD)
    wA = np.zeros((2, HB, 2, NH, 32), f)
    wA[..., :HD] = wq[:, :, 0:2]
    d["wA"] = wA.reshape(2, HB, 2 * NJ * 128).transpose(1, 0, 2)
    d["wV0"] = wq[:, :, 2].reshape(2, HB, DIM).transpose(1, 0, 2)
    d["wP0"] = a["L0_attn_w_proj"].reshape(NJ, 64, DIM).transpose(1, 0, 2)
    MAXREL = 14

    def by_position(tv, th):
        t = np.zeros((N, 16, HD), f)
        t[0, 0:7] = tv[0]
        t[0, 7:12] = th[0]
        for n in range(1, N):
            rq, cq = (n - 1) // side, (n - 1) % side
            t[n, 0:7] = tv[np.clip(np.arange(7) - rq, -MAXREL, MAXREL) + MAXREL + 1]
            t[n, 7:12] = th[np.clip(np.arange(5) - cq, -MAXREL, MAXREL) + MAXREL + 1]
        t[:, 12] = tv[0]
        t[:, 13] = th[0]
        return t
    tk = by_position(a["L0_attn_tab_vk"], a["L0_attn_tab_hk"])
    tv = by_position(a["L0_attn_tab_vv"], a["L0_attn_tab_hv"])
    pk = np.zeros((4, 32, N, 4, 32), f)
    pv = np.zeros((4, 32, N, 4, HD), f)
    for r in range(4):
        pk[r, :HD, :, r, :HD] = np.eye(HD)[:, None, :]
        pk[r, :HD, :, r, HD:] = tk.transpose(2, 0, 1)
        pv[r, :HD, :, r, :] = np.eye(HD)[:, None, :]
        pv[r, HD:, :, r, :] = tv.transpose(1, 0, 2)
    w = a["L1_attn_w_inp"][0].reshape(2, HB, 3 * DIM).transpose(1, 0, 2)
    d["wC1"], d["wV1"] = w[:, :, :2 * DIM], w[:, :, 2 * DIM:]
    wf = np.zeros((6, HD, 6, HD), f)
    for i in range(6):
        wf[i, :, i, :] = a["L1_attn_omega"].T
    d["wF1"] = wf.reshape(HB, HB)
    d["wO1"] = a["L1_attn_w_out"][0].reshape(2, HB, DIM).transpose(1, 0, 2)
    w = a["L1_ffn_w_qkv"].reshape(2, HB, QH + 2 * KVH, QD // 2, 2)
    wq, wk = w[:, :, :QH], np.repeat(w[:, :, QH:QH + KVH], 2, axis=2)
    w2 = np.concatenate([wq, wk], 2).transpose(0, 1, 2, 4, 3)
    d["wQ2"] = w2.reshape(2, HB, BT * 128).transpose(1, 0, 2)
    d["swap"] = np.eye(128, dtype=f)[np.arange(128) ^ 32]
    d["wV2"] = w[:, :, QH + KVH:].reshape(2, HB, KVH * QD).transpose(1, 0, 2)
    d["wO2"] = a["L1_ffn_w_out"].reshape(6, 128, DIM).transpose(1, 0, 2)
    d["posk"] = pk.reshape(128, N, 128)
    d["posv"] = pv.reshape(128, N, 64)
    return {k: np.ascontiguousarray(v) for k, v in d.items()}


def kernel(**inputs):
    import numpy as np
    import concourse.bacc as bacc
    from concourse.bass_utils import run_bass_kernel_spmd as run

    nc = bacc.Bacc("TRN2", target_bir_lowering=False, num_devices=1)
    arrays = layouts(inputs)
    ins = {k: nc.dram_tensor(f"in_{k}", v.shape, mybir.dt.from_np(v.dtype), kind="ExternalInput").ap()
           for k, v in arrays.items()}
    out = nc.dram_tensor("out_0_dram", (B, N, DIM), mybir.dt.float32, kind="ExternalOutput").ap()
    tower(nc, ins, out.rearrange("(g b) n d -> (b n) g d", g=NG))
    r = run(nc, [{f"in_{k}": v for k, v in arrays.items()}], core_ids=[0])
    return r.results[0]["out_0_dram"]
```
